# Optimizing a Trainium2 kernel written in Bass

```python
import numpy as np
import jax
import jax.numpy as jnp

def _softmax(x, axis=-1):
    return jax.nn.softmax(x, axis=axis)

def _gelu(x):
    return jax.nn.gelu(x, approximate=True)

def _silu(x):
    return jax.nn.silu(x)

def _sigmoid(x):
    return jax.nn.sigmoid(x)

def _layernorm(x, axis=-1, eps=1e-05):
    m = jnp.mean(x, axis=axis, keepdims=True)
    v = jnp.var(x, axis=axis, keepdims=True)
    return (x - m) / jnp.sqrt(v + eps)

def _scatter_add(tgt, idx, src, axis=0):
    return tgt.at[idx].add(src)

def _segment_sum(src, seg, n):
    return jax.ops.segment_sum(src, seg, n)
kernel_name = 'mk_gnn_ffn_d1_gnn_r32_fe17ec'

def setup_inputs(seed: int=0):
    np.random.seed(seed)
    _w = jnp.asarray

    def _rec_inputs():
        import jax
        import jax.numpy as jnp
        _gk = jax.random.key(seed)
        x = -0.0002117 + 1 * jax.random.normal(jax.random.fold_in(_gk, 1), (10000, 512), jnp.float32)
        src = jax.random.randint(jax.random.fold_in(_gk, 2), (5000,), 0, 10000, jnp.int32)
        dst = jnp.minimum((10000 * jax.random.uniform(jax.random.fold_in(_gk, 3), (5000,)) ** 2.0).astype(jnp.int32), 9999)
        _o = jnp.argsort(dst, stable=True)
        src = src[_o]
        dst = dst[_o]
        edge_attr_64 = -5.3897e-05 + 0.999841 * jax.random.normal(jax.random.fold_in(_gk, 11), (5000, 64), jnp.float32)
        return (x, src, dst, edge_attr_64)
    x, src, dst, edge_attr_64 = _rec_inputs()

    def _L0_gnn_setup():
        import jax, jax.numpy as jnp
        import numpy as np
        N, E, H, ED = (50000, 12500, 512, 64)
        BN_EPS = 1e-05

        def _bn(h, g, b):
            mu = jnp.mean(h, axis=0)
            var = jnp.mean(jnp.square(h - mu), axis=0)
            return (h - mu) * jax.lax.rsqrt(var + BN_EPS) * g + b
        key = jax.random.key(seed)
        ks = jax.random.split(key, 8)
        s = lambda d: 1.0 / np.sqrt(d)
        return {'x': jax.random.normal(ks[0], (N, H), jnp.float32), 'edge_attr': jax.random.normal(ks[1], (E, ED), jnp.float32), 'edge_index': jax.random.randint(ks[2], (2, E), 0, N, jnp.int32), 'W_e': jax.random.normal(ks[3], (ED, H), jnp.float32) * s(ED), 'b_e': jnp.zeros((H,), jnp.float32), 'W1': jax.random.normal(ks[4], (H, 2 * H), jnp.float32) * s(H), 'b1': jnp.zeros((2 * H,), jnp.float32), 'g1': jnp.ones((2 * H,), jnp.float32), 'beta1': jnp.zeros((2 * H,), jnp.float32), 'W2': jax.random.normal(ks[5], (2 * H, H), jnp.float32) * s(2 * H), 'b2': jnp.zeros((H,), jnp.float32), 'g2': jnp.ones((H,), jnp.float32), 'beta2': jnp.zeros((H,), jnp.float32), 'eps': jnp.zeros((), jnp.float32)}
    _L0_gnn_all = _L0_gnn_setup()
    _L0_gnn_in = {k: v for k, v in _L0_gnn_all.items() if k in ('W_e', 'b_e', 'W1', 'b1', 'g1', 'beta1', 'W2', 'b2', 'g2', 'beta2', 'eps')}
    del _L0_gnn_all

    def _L0_ffn_setup():
        import jax, jax.numpy as jnp
        import numpy as np
        NEXPERTS = 16
        key = jax.random.key(seed)
        k1, k2, k3, k4 = jax.random.split(key, 4)
        B, S, D = (4, 64, 512)
        E, Sets, F = (16, 4, 32)
        scale = 0.02
        return {'x': jax.random.normal(k1, (B, S, D), dtype=jnp.float32), 'controller': jax.random.normal(k2, (D, E, Sets), dtype=jnp.float32) * scale, 'f1': jax.random.normal(k3, (D, E, Sets, F), dtype=jnp.float32) * scale, 'f2': jax.random.normal(k4, (E, Sets, F, D), dtype=jnp.float32) * scale}
    _L0_ffn_all = _L0_ffn_setup()
    _L0_ffn_in = {k: v for k, v in _L0_ffn_all.items() if k in ('controller', 'f1', 'f2')}
    del _L0_ffn_all
    return {'x': x, 'src': src, 'dst': dst, 'edge_attr_64': edge_attr_64, 'L0_gnn_W_e': _L0_gnn_in['W_e'], 'L0_gnn_b_e': _L0_gnn_in['b_e'], 'L0_gnn_W1': _L0_gnn_in['W1'], 'L0_gnn_b1': _L0_gnn_in['b1'], 'L0_gnn_g1': _L0_gnn_in['g1'], 'L0_gnn_beta1': _L0_gnn_in['beta1'], 'L0_gnn_W2': _L0_gnn_in['W2'], 'L0_gnn_b2': _L0_gnn_in['b2'], 'L0_gnn_g2': _L0_gnn_in['g2'], 'L0_gnn_beta2': _L0_gnn_in['beta2'], 'L0_gnn_eps': _L0_gnn_in['eps'], 'L0_ffn_controller': _L0_ffn_in['controller'], 'L0_ffn_f1': _L0_ffn_in['f1'], 'L0_ffn_f2': _L0_ffn_in['f2']}

def reference(x, src, dst, edge_attr_64, L0_gnn_W_e, L0_gnn_b_e, L0_gnn_W1, L0_gnn_b1, L0_gnn_g1, L0_gnn_beta1, L0_gnn_W2, L0_gnn_b2, L0_gnn_g2, L0_gnn_beta2, L0_gnn_eps, L0_ffn_controller, L0_ffn_f1, L0_ffn_f2):
    import jax
    import jax.numpy as jnp

    def _L0_gnn_ref(x, edge_attr, edge_index, W_e, b_e, W1, b1, g1, beta1, W2, b2, g2, beta2, eps):
        import jax, jax.numpy as jnp
        import numpy as np
        N, E, H, ED = (50000, 12500, 512, 64)
        BN_EPS = 1e-05

        def _bn(h, g, b):
            mu = jnp.mean(h, axis=0)
            var = jnp.mean(jnp.square(h - mu), axis=0)
            return (h - mu) * jax.lax.rsqrt(var + BN_EPS) * g + b
        src, dst = (edge_index[0], edge_index[1])
        msg = jax.nn.relu(x[src] + edge_attr @ W_e + b_e)
        aggr = jax.ops.segment_sum(msg, dst, num_segments=x.shape[0])
        h = (1.0 + eps) * x + aggr
        h = jax.nn.silu(_bn(h @ W1 + b1, g1, beta1))
        h = h @ W2 + b2
        return jax.nn.silu(_bn(h, g2, beta2))

    def _L0_ffn_ref(x, controller, f1, f2):
        import jax, jax.numpy as jnp
        import numpy as np
        NEXPERTS = 16
        B, S, D = x.shape
        t = NEXPERTS
        grouped = x.reshape(B, S // t, t, D)
        cont_logits = jnp.einsum('bgtd,des->bgtes', grouped, controller)
        tie = jnp.linspace(0.0, 1e-06, t, dtype=x.dtype).reshape(t, 1, 1)
        cont_logits = cont_logits + tie
        cont_perm = (cont_logits == jnp.max(cont_logits, axis=-3, keepdims=True)).astype(x.dtype)
        intermediate = jnp.einsum('bgtd,desf->bgtesf', grouped, f1)
        inner = jnp.einsum('bgtesf,bgtes->bgesf', intermediate, cont_perm)
        inner = jax.nn.relu(inner)
        inter2 = jnp.einsum('bgesf,esfd->bgesd', inner, f2)
        result = jnp.einsum('bgesd,bgtes->bgtd', inter2, cont_perm)
        return result.reshape(B, S, D)
    edge_index = jnp.stack([src, dst])
    x = x + _L0_gnn_ref(_layernorm(x, axis=-1), edge_attr_64, edge_index, L0_gnn_W_e, L0_gnn_b_e, L0_gnn_W1, L0_gnn_b1, L0_gnn_g1, L0_gnn_beta1, L0_gnn_W2, L0_gnn_b2, L0_gnn_g2, L0_gnn_beta2, L0_gnn_eps)
    x = x + _L0_ffn_ref(_layernorm(x, axis=-1)[None], L0_ffn_controller, L0_ffn_f1, L0_ffn_f2)[0]
    return x

_drawn_inputs = setup_inputs


def setup_inputs(seed=0):
    import zlib

    import numpy as np

    out = dict(_drawn_inputs(seed))
    spreads = {'L0_gnn_b_e': (0.0, 0.1),
     'L0_gnn_b1': (0.0, 0.1),
     'L0_gnn_g1': (1.0, 0.2),
     'L0_gnn_beta1': (0.0, 0.1),
     'L0_gnn_b2': (0.0, 0.1),
     'L0_gnn_g2': (1.0, 0.2),
     'L0_gnn_beta2': (0.0, 0.1)}
    factors = {}
    for name, (base, spread) in spreads.items():
        noise = np.random.default_rng([zlib.crc32(name.encode()), seed]).standard_normal(out[name].shape)
        drawn = base * np.exp(spread * noise) if base else spread * noise
        out[name] = jnp.asarray(drawn.astype(out[name].dtype))
    for name, factor in factors.items():
        out[name] = (out[name] * factor).astype(out[name].dtype)
    return out
```

```python
import numpy as np
import concourse.bass as bass
from concourse import mybir
from contextlib import ExitStack

F32 = mybir.dt.float32
F32R = mybir.dt.float32r
I32 = mybir.dt.int32
ALU = mybir.AluOpType
ACT = mybir.ActivationFunctionType
AX = mybir.AxisListType

N, H = 10000, 512
E, ED = 5000, 64
P = 128
KH = H // P
F = 2 * H
KF = F // P
EPS = 1e-5
ET = E // P
ER = E - ET * P
EU = 3
TRASH = P
CW = 500
NCH = N // CW
SUB = 4
RT = CW // SUB
GT = 16
NE, NS, FF = 16, 4, 32
ES = NE * NS
GB = P // GT
TB = 8
BW = TB * P
NB = -(-N // BW)
QB = ES // GT


def wait_apart(eng, met, *waits):
    found = [(sem, value if isinstance(value, int) else eng.to_reg(value)) for sem, value in waits]
    eng.wait_ge(*met)
    for sem, value in found:
        eng.wait_ge(sem, value)


def edge_aggregate(nc, sems, psum, ident, x, src, dst, edge_attr, W_e, b_e, agg):
    with ExitStack() as ctx:
        def sb(name, shape, dt=F32):
            return ctx.enter_context(nc.sbuf_tensor(name, shape, dt))

        sem = sems
        zeros = sb("zeros", [P, 2048])
        web = sb("web", [ED + 1, H])
        before = sb("before", [P, P])
        trash = sb("trash", [P, 1])
        mhalf = sb("mhalf_e", [P, 1])
        dcol = [sb(f"dcol{i}", [P, 1], I32) for i in range(EU)]
        scol = [sb(f"scol{i}", [P, 1], I32) for i in range(EU)]
        drow = [sb(f"drow{i}", [P, P], I32) for i in range(EU)]
        ea = [sb(f"ea{i}", [P, ED]) for i in range(EU)]
        eaT = [sb(f"eaT{i}", [ED + 1, P]) for i in range(EU)]
        xg = [sb(f"xg{i}", [P, H]) for i in range(EU)]
        dcolf = [sb(f"dcolf{i}", [P, 1]) for i in range(EU)]
        sel = [sb(f"sel{i}", [P, P]) for i in range(EU)]
        scr = [sb(f"scr{i}", [P, P]) for i in range(EU)]
        cnt = [sb(f"cnt{i}", [P, 1]) for i in range(EU)]
        away = [sb(f"away{i}", [P, 1]) for i in range(EU)]
        idx = [sb(f"idx{i}", [P, 1], I32) for i in range(EU)]
        st = [sb(f"est{i}", [P, 6]) for i in range(EU)]
        mv = [sb(f"emv{i}", [P, 2]) for i in range(EU)]
        ve = [sb(f"eve{i}", [P, 1]) for i in range(EU)]
        rs = [sb(f"ers{i}", [P, 1]) for i in range(EU)]
        xn = [sb(f"exn{i}", [P, H]) for i in range(EU)]
        pre = [sb(f"pre{i}", [P, H]) for i in range(EU)]
        msg = [sb(f"msg{i}", [P, H]) for i in range(EU)]
        comb = [sb(f"comb{i}", [P, H]) for i in range(EU)]
        tp = [psum[0], psum[1]]
        emb = [psum[2], psum[3], psum[4]]
        cps = [psum[5], psum[6], psum[7]]

        zeroed, wld, const = sem("zeroed"), sem("edge_w_loaded"), sem("edge_const")
        ld = [sem(f"edge_loaded{i}") for i in range(EU)]
        gat = [sem(f"rows_gathered{i}") for i in range(EU)]
        sca = sem("rows_added")
        dcf, sl, ct, aw, ix = sem("dstf"), sem("sel_ready"), sem("cnt_ready"), sem("away_ready"), sem("idx_ready")
        bst, bag, vpe, rst = sem("estats"), sem("emeanvar"), sem("evar_eps"), sem("erstd")
        xnr, prr, msr = sem("exn_ready"), sem("pre_ready"), sem("msg_ready")
        tpr, etr, emr, cpr, cbr = sem("ea_transposed"), sem("eaT_ready"), sem("emb_ready"), sem("comb_psum"), sem("comb_ready")

        NT = ET + 1
        flat = agg.rearrange("a b -> (a b)").rearrange("(p c) -> p c", p=P)
        cols = flat.shape[1]
        full = cols // 2048

        def turns(eng, body):
            with eng.Fori(0, ET // EU) as it:
                for u in range(EU):
                    body(it * EU + u, u, P, it)
            body(ET, ET % EU, ER, ET // EU)

        with nc.Block() as block:
            @block.sync
            def _(sp):
                sp.wait_ge(const, 1)
                for c in range(full):
                    sp.dma_start(flat[:, c * 2048:(c + 1) * 2048], zeros[:, :]).then_inc(zeroed, 16)
                sp.dma_start(flat[:, full * 2048:cols], zeros[:, 0:cols - full * 2048]).then_inc(zeroed, 16)
                sp.wait_ge(sca, 16 * NT)
                sp.wait_ge(zeroed, 16 * (full + 1))

            @block.scalar
            def _(act):
                act.dma_start(web[0:ED, :], W_e).then_inc(wld, 16)
                act.dma_start(web[ED:ED + 1, :], b_e.rearrange("(a n) -> a n", a=1)).then_inc(wld, 16)

                def load(t, u, p, it):
                    if not (isinstance(it, int) and it == 0):
                        act.wait_ge(ix, t - EU + 1)
                        act.wait_ge(gat[u], it * 16)
                        act.wait_ge(tpr, t - EU + 1)
                    e0 = t * P
                    act.dma_start(dcol[u][0:p, :], dst[bass.ds(e0, p)].rearrange("(p a) -> p a", a=1)).then_inc(ld[u], 16)
                    act.dma_start(scol[u][0:p, :], src[bass.ds(e0, p)].rearrange("(p a) -> p a", a=1)).then_inc(ld[u], 16)
                    act.dma_start(drow[u][0:p, 0:p], dst[bass.ds(e0, p)].rearrange("(a p) -> a p", a=1).to_broadcast([p, p])).then_inc(ld[u], 16)
                    act.dma_start(ea[u][0:p, :], edge_attr[bass.ds(e0, p), :]).then_inc(ld[u], 16)

                def tile(t, u, p, it):
                    act.wait_ge(tpr, t + 1)
                    nc.scalar.activation(eaT[u][0:ED, 0:p], tp[0][0:ED, 128 * u:128 * u + p], ACT.Copy).then_inc(etr, 1)
                    act.wait_ge(prr, t + 1)
                    nc.scalar.activation(msg[u][0:p, :], pre[u][0:p, :], ACT.Relu).then_inc(msr, 1)
                    act.wait_ge(cpr, t + 1)
                    nc.scalar.activation(comb[u][0:p, :], cps[u][0:p, :], ACT.Copy).then_inc(cbr, 1)

                for u in range(EU):
                    load(u, u, P, 0)
                with act.Fori(0, ET // EU - 1) as it:
                    for u in range(EU):
                        tile(it * EU + u, u, P, it)
                        load(it * EU + u + EU, u, P, it + 1)
                for u in range(EU):
                    t = ET - EU + u
                    tile(t, u, P, ET // EU - 1)
                    if u == 0:
                        load(ET, 0, ER, ET // EU)
                tile(ET, 0, ER, ET // EU)

            @block.gpsimd
            def _(pool):
                nc.gpsimd.memset(zeros[:, :], 0.0).then_inc(const, 1)
                nc.gpsimd.memset(before[:, :], 1.0).then_inc(const, 1)
                pool.wait_ge(const, 2)
                nc.gpsimd.affine_select(out=before[:, :], in_=before[:, :], compare_op=ALU.is_gt, fill=0.0,
                                        base=0, pattern=[[-1, P]], channel_multiplier=1).then_inc(const, 1)
                nc.gpsimd.iota(trash[:, :], pattern=[[0, 1]], base=N, channel_multiplier=1,
                               allow_small_or_imprecise_dtypes=True).then_inc(const, 1)
                pool.wait_ge(const, 4)
                nc.gpsimd.memset(mhalf[:, :], -0.5).then_inc(const, 1)
                for i in range(EU):
                    pool.wait_ge(const, 5 + i)
                    nc.gpsimd.memset(eaT[i][ED:ED + 1, :], 1.0).then_inc(const, 1)
                pool.wait_ge(const, 5 + EU)

                def gather(t, u, p, it):
                    free = [] if isinstance(it, int) and it == 0 else [(xnr, t - EU + 1)]
                    wait_apart(pool, (const, 5 + EU), (ld[u], (it + 1) * 64), *free)
                    nc.gpsimd.indirect_dma_start(
                        out=xg[u][0:p, :], out_offset=None, in_=x,
                        in_offset=bass.IndirectOffsetOnAxis(ap=scol[u][0:p, 0:1], axis=0)).then_inc(gat[u], 16)

                def root(t, u, p, it):
                    pool.wait_ge(vpe, t + 1)
                    nc.gpsimd.tensor_tensor(rs[u][0:p, :], ve[u][0:p, :], mhalf[0:p, :], ALU.pow).then_inc(rst, 1)

                def scatter(t, u, p, it):
                    before = [] if isinstance(it, int) and it == 0 and u == 0 else [(sca, t * 16)]
                    wait_apart(pool, (const, 5 + EU), (cbr, t + 1), *before)
                    nc.gpsimd.indirect_dma_start(
                        out=agg, out_offset=bass.IndirectOffsetOnAxis(ap=idx[u][0:p, 0:1], axis=0),
                        in_=comb[u][0:p, :], in_offset=None, compute_op=ALU.add).then_inc(sca, 16)

                for u in range(2):
                    gather(u, u, P, 0)
                root(0, 0, P, 0)
                pool.wait_ge(zeroed, 16 * (full + 1))

                def step(t, u, it, last=False):
                    if not last:
                        u2 = (u + 2) % EU
                        gather(t + 2, u2, P, it + (u + 2) // EU)
                    root(t + 1, (u + 1) % EU, P, it)
                    scatter(t, u, P, it)

                step(0, 0, 0)
                step(1, 1, 0)
                step(2, 2, 0)
                with pool.Fori(1, ET // EU - 1) as it:
                    for u in range(EU):
                        step(it * EU + u, u, it)
                last = ET // EU - 1
                t0 = last * EU
                step(t0, 0, last)
                gather(ET, 0, ER, ET // EU)
                root(t0 + 2, 2, P, last)
                scatter(t0 + 1, 1, P, last)
                root(ET, 0, ER, ET // EU)
                scatter(t0 + 2, 2, P, last)
                scatter(ET, 0, ER, ET // EU)

            @block.vector
            def _(dve):
                dve.wait_ge(const, 5 + EU)

                def tile(t, u, p, it):
                    first = isinstance(it, int) and it == 0
                    dve.wait_ge(ld[u], (it + 1) * 64)
                    if not first:
                        dve.wait_ge(sca, (t - EU + 1) * 16)
                        dve.wait_ge(cpr, t - EU + 1)
                    nc.vector.tensor_copy(dcolf[u][0:p, :], dcol[u][0:p, :]).then_inc(dcf, 1)
                    dve.wait_ge(dcf, t + 1)
                    nc.vector.tensor_scalar(sel[u][0:p, 0:p], drow[u][0:p, 0:p], dcolf[u][0:p, 0:1], None,
                                            ALU.is_equal).then_inc(sl, 1)
                    wait_apart(dve, (const, 5 + EU), (sl, t + 1))
                    nc.vector.tensor_tensor_reduce(out=scr[u][0:p, 0:p], in0=sel[u][0:p, 0:p], in1=before[0:p, 0:p],
                                                   scale=1.0, scalar=0.0, op0=ALU.mult, op1=ALU.max,
                                                   accum_out=cnt[u][0:p, 0:1]).then_inc(ct, 1)
                    nc.vector.tensor_tensor(away[u][0:p, :], trash[0:p, :], dcolf[u][0:p, :], ALU.subtract).then_inc(aw, 1)
                    dve.wait_ge(ct, t + 1)
                    dve.wait_ge(aw, t + 1)
                    nc.vector.scalar_tensor_tensor(out=idx[u][0:p, :], in0=away[u][0:p, :], scalar=cnt[u][0:p, 0:1],
                                                   in1=dcolf[u][0:p, :], op0=ALU.mult, op1=ALU.add).then_inc(ix, 1)
                    dve.wait_ge(gat[u], (it + 1) * 16)
                    nc.vector.bn_stats(st[u][0:p, :], xg[u][0:p, :]).then_inc(bst, 1)
                    wait_apart(dve, (const, 5 + EU), (bst, t + 1))
                    nc.vector.bn_aggr(mv[u][0:p, :], st[u][0:p, :]).then_inc(bag, 1)
                    dve.wait_ge(bag, t + 1)
                    nc.vector.tensor_scalar_add(ve[u][0:p, :], mv[u][0:p, 1:2], EPS).then_inc(vpe, 1)
                    dve.wait_ge(rst, t + 1)
                    nc.vector.tensor_scalar(xn[u][0:p, :], xg[u][0:p, :], mv[u][0:p, 0:1], rs[u][0:p, 0:1],
                                            ALU.subtract, ALU.mult).then_inc(xnr, 1)
                    dve.wait_ge(xnr, t + 1)
                    dve.wait_ge(emr, t + 1)
                    if not first:
                        dve.wait_ge(msr, t - EU + 1)
                    nc.vector.tensor_tensor(pre[u][0:p, :], xn[u][0:p, :], emb[u][0:p, :], ALU.add).then_inc(prr, 1)

                for u in range(EU):
                    tile(u, u, P, 0)
                with dve.Fori(1, ET // EU) as it:
                    for u in range(EU):
                        tile(it * EU + u, u, P, it)
                tile(ET, 0, ER, ET // EU)

            @block.tensor
            def _(pe):
                pe.wait_ge(wld, 32)

                def embed(t, u, p, it):
                    first = isinstance(it, int) and it == 0
                    free = [] if first else [(etr, t - EU + 1)]
                    wait_apart(pe, (const, 5 + EU), (ld[u], (it + 1) * 64), *free)
                    nc.tensor.transpose(tp[0][0:ED, 128 * u:128 * u + p], ea[u][0:p, :], ident[0:p, 0:p]).then_inc(tpr, 1)
                    pe.wait_ge(etr, t + 1)
                    if not first:
                        pe.wait_ge(prr, t - EU + 1)
                    nc.tensor.matmul(emb[u][0:p, :], eaT[u][:, 0:p], web[:, :], start=True, stop=True).then_inc(emr, 1)

                def combine(t, u, p, it):
                    pe.wait_ge(msr, t + 1)
                    if not (isinstance(it, int) and it == 0):
                        pe.wait_ge(cbr, t - EU + 1)
                    nc.tensor.matmul(cps[u][0:p, :], sel[u][0:p, 0:p], msg[u][0:p, :], start=True, stop=True).then_inc(cpr, 1)

                pe.wait_ge(const, 5 + EU)
                for u in range(EU):
                    embed(u, u, P, 0)
                    combine(u, u, P, 0)
                with pe.Fori(1, ET // EU) as it:
                    for u in range(EU):
                        embed(it * EU + u, u, P, it)
                        combine(it * EU + u, u, P, it)
                embed(ET, 0, ER, ET // EU)
                combine(ET, 0, ER, ET // EU)


def split_weight(dve, whole, hi, lo, hi_done, lo_done, k):
    nc_v = dve
    nc_v.tensor_copy(hi[:, k, :], whole[:, k, :]).then_inc(hi_done, 1)
    dve.wait_ge(hi_done, k + 1)
    nc_v.tensor_tensor(lo[:, k, :], whole[:, k, :], hi[:, k, :].bitcast(F32), ALU.subtract).then_inc(lo_done, 1)


def product(nc, out, w_hi, w_lo, a_hi, a_lo, chunks, m):
    cols = slice(m * P, (m + 1) * P)
    for k in range(chunks):
        nc.tensor.matmul(out, w_hi[:, k, cols], a_hi[:, k, :], start=(k == 0), stop=False)
        nc.tensor.matmul(out, w_hi[:, k, cols], a_lo[:, k, :], start=False, stop=False)
        last = nc.tensor.matmul(out, w_lo[:, k, cols], a_hi[:, k, :], start=False, stop=(k == chunks - 1))
    return last


def gnn_up(nc, sem, psum, ident, mhalf, x, agg, W1, b1, eps, h1T, stats1):
    with ExitStack() as ctx:
        def sb(name, shape, dt=F32):
            return ctx.enter_context(nc.sbuf_tensor(name, shape, dt))

        wst = sb("w1_whole", [P, KH, F])
        whi, wlo = sb("w1_hi", [P, KH, F], F32R), sb("w1_lo", [P, KH, F], F32R)
        b1c = sb("b1c", [P, KF])
        epsc, ope = sb("epsc", [P, 1]), sb("one_plus_eps", [P, 1])
        xt = [sb(f"xt{i}", [P, SUB, H]) for i in range(2)]
        at = [sb(f"at{i}", [P, SUB, H]) for i in range(2)]
        ht = sb("ht", [P, SUB, H])
        st = sb("st", [P, SUB, 6])
        mv = sb("mv", [P, SUB, 2])
        ve, rs, rse = sb("ve", [P, SUB]), sb("rs", [P, SUB]), sb("rse", [P, SUB])
        hhi = [sb(f"hhi{i}", [P, KH, CW], F32R) for i in range(2)]
        hlo = [sb(f"hlo{i}", [P, KH, CW], F32R) for i in range(2)]
        h1o = [sb(f"h1o{i}", [P, KF, CW]) for i in range(2)]
        tb, mb = psum[0:KH], psum[4:8]

        wld, whd, wld2 = sem("w1_loaded"), sem("w1_hi_done"), sem("w1_lo_done")
        ldx = [sem(f"x_agg_loaded{i}") for i in range(2)]
        sto = [sem(f"h1_stored{i}") for i in range(2)]
        bst, bag, vpe, rst, rsd = sem("xstats"), sem("xmeanvar"), sem("xvar_eps"), sem("xrstd"), sem("xrstd_eps")
        opr = sem("ope_ready")
        nrm, hrd = sem("x_normalized"), sem("h_ready")
        tpr, hir, lor = sem("h_transposed"), sem("h_hi_ready"), sem("h_lo_ready")
        mmr, evr, str_ = sem("h1_psum"), sem("h1_evicted"), sem("h1_stats")

        def span(c):
            return bass.ds(c * CW, CW)

        def chunks(eng, body):
            body(1, 1)
            body(2, 0)
            with eng.Fori(1, (NCH - 2) // 2) as it:
                body(it * 2 + 1, 1)
                body(it * 2 + 2, 0)
            body(NCH - 1, 1)

        def static(c, least):
            return isinstance(c, int) and c < least

        with nc.Block() as block:
            @block.sync
            def _(sp):
                sp.dma_start(wst[:, :, :], W1.rearrange("(k p) n -> p k n", p=P)).then_inc(wld, 16)
                with nc.allow_non_contiguous_dma(reason="a bias by channel"):
                    sp.dma_start(b1c[:, :], b1.rearrange("(m p) -> p m", p=P)).then_inc(wld, 16)
                sp.dma_start(epsc[:, :], eps.rearrange("(a n) -> a n", a=1).to_broadcast([P, 1])).then_inc(wld, 16)

                def load(c, b):
                    if not static(c, 2):
                        sp.wait_ge(hrd, (c - 1) * SUB)
                    rows = x[span(c), :].rearrange("(j p) h -> p j h", p=RT)
                    sp.dma_start(xt[b][0:RT, :, :], rows).then_inc(ldx[b], 16)
                    rows = agg[span(c), :].rearrange("(j p) h -> p j h", p=RT)
                    sp.dma_start(at[b][0:RT, :, :], rows).then_inc(ldx[b], 16)

                def store(c, b):
                    sp.wait_ge(evr, (c + 1) * KF)
                    sp.dma_start(h1T[:, :, span(c)].rearrange("m p n -> p m n"), h1o[b][:, :, :]).then_inc(sto[b], 16)

                load(0, 0)
                load(1, 1)
                store_first = store
                load(2, 0)
                store_first(0, 0)
                with sp.Fori(0, (NCH - 4) // 2) as it:
                    load(it * 2 + 3, 1)
                    store(it * 2 + 1, 1)
                    load(it * 2 + 4, 0)
                    store(it * 2 + 2, 0)
                load(NCH - 1, 1)
                store(NCH - 3, 1)
                store(NCH - 2, 0)
                store(NCH - 1, 1)
                for b in range(2):
                    sp.wait_ge(sto[b], 16 * (NCH // 2))

            @block.gpsimd
            def _(pool):
                def root(c, b):
                    pool.wait_ge(vpe, c + 1)
                    nc.gpsimd.tensor_tensor(rs[0:RT, :], ve[0:RT, :], mhalf[0:RT, 0:SUB], ALU.pow).then_inc(rst, 1)

                root(0, 0)
                chunks(pool, root)

            @block.vector
            def _(dve):
                dve.wait_ge(wld, 48)
                for k in range(KH):
                    split_weight(nc.vector, wst, whi, wlo, whd, wld2, k)
                nc.vector.tensor_scalar_add(ope[:, :], epsc[:, :], 1.0).then_inc(opr, 1)
                dve.wait_ge(opr, 1)

                def prepare(c, b):
                    if b == 0:
                        dve.wait_ge(ldx[0], (c // 2 + 1) * 32 if isinstance(c, int) else (c + 2) * 16)
                    else:
                        dve.wait_ge(ldx[1], (c + 1) * 16)
                    for j in range(SUB):
                        nc.vector.bn_stats(st[0:RT, j, :], xt[b][0:RT, j, :]).then_inc(bst, 1)
                    for j in range(SUB):
                        wait_apart(dve, (wld, 48), (bst, c * SUB + j + 1))
                        nc.vector.bn_aggr(mv[0:RT, j, :], st[0:RT, j, :]).then_inc(bag, 1)
                    dve.wait_ge(bag, c * SUB + SUB)
                    nc.vector.tensor_scalar_add(ve[0:RT, :], mv[0:RT, :, 1], EPS).then_inc(vpe, 1)
                    dve.wait_ge(rst, c + 1)
                    nc.vector.tensor_scalar(rse[0:RT, :], rs[0:RT, :], ope[0:RT, 0:1], None, ALU.mult).then_inc(rsd, 1)
                    dve.wait_ge(rsd, c + 1)
                    if not static(c, 1):
                        dve.wait_ge(tpr, c * KH)
                    for j in range(SUB):
                        nc.vector.tensor_scalar(ht[0:RT, j, :], xt[b][0:RT, j, :], mv[0:RT, j, 0:1], rse[0:RT, j:j + 1],
                                                ALU.subtract, ALU.mult).then_inc(nrm, 1)
                    for j in range(SUB):
                        dve.wait_ge(nrm, c * SUB + j + 1)
                        nc.vector.tensor_tensor(ht[0:RT, j, :], ht[0:RT, j, :], at[b][0:RT, j, :], ALU.add).then_inc(hrd, 1)

                def low(c, b):
                    if not static(c, 2):
                        dve.wait_ge(mmr, (c - 1) * KF)
                    for k in range(KH):
                        dve.wait_ge(hir, c * KH + k + 1)
                        nc.vector.tensor_tensor(hlo[b][:, k, :], tb[k][:, 0:CW], hhi[b][:, k, :].bitcast(F32),
                                                ALU.subtract).then_inc(lor, 1)

                def stats(c, b, m0, m1):
                    for m in range(m0, m1):
                        dve.wait_ge(evr, c * KF + m + 1)
                        nc.vector.bn_stats(stats1[:, m, bass.ds(c * 6, 6)], h1o[b][:, m, :]).then_inc(str_, 1)

                prepare(0, 0)
                low(0, 0)

                def body(c, b):
                    prepare(c, b)
                    stats(c - 1, 1 - b, 0, 4)
                    low(c, b)
                    stats(c - 1, 1 - b, 4, KF)

                chunks(dve, body)
                stats(NCH - 1, 1, 0, KF)
                dve.wait_ge(str_, NCH * KF)

            @block.scalar
            def _(act):
                act.wait_ge(wld, 48)

                def high(c, b):
                    if not static(c, 2):
                        act.wait_ge(mmr, (c - 1) * KF)
                    for k in range(KH):
                        act.wait_ge(tpr, c * KH + k + 1)
                        nc.scalar.activation(hhi[b][:, k, :], tb[k][:, 0:CW], ACT.Copy).then_inc(hir, 1)

                def evict(c, b, m0, m1):
                    if not static(c, 2) and m0 == 0:
                        if b == 0:
                            act.wait_ge(sto[0], (c // 2) * 16 if isinstance(c, int) else c * 8)
                        else:
                            act.wait_ge(sto[1], (c - 1) * 8)
                        act.wait_ge(str_, (c - 1) * KF)
                    for m in range(m0, m1):
                        act.wait_ge(mmr, c * KF + m + 1)
                        nc.scalar.activation(h1o[b][:, m, :], mb[m % 4][:, 0:CW], ACT.Identity,
                                             bias=b1c[:, m:m + 1]).then_inc(evr, 1)

                high(0, 0)

                def body(c, b):
                    evict(c - 1, 1 - b, 0, 4)
                    high(c, b)
                    evict(c - 1, 1 - b, 4, KF)

                chunks(act, body)
                evict(NCH - 1, 1, 0, KF)

            @block.tensor
            def _(pe):
                pe.wait_ge(wld2, KH)

                def turn(c, b):
                    pe.wait_ge(hrd, (c + 1) * SUB)
                    if not static(c, 1):
                        pe.wait_ge(lor, c * KH)
                    for k in range(KH):
                        for j in range(SUB):
                            last = nc.tensor.transpose(tb[k][:, j * RT:(j + 1) * RT], ht[0:RT, j, k * P:(k + 1) * P],
                                                       ident[0:RT, 0:RT])
                        last.then_inc(tpr, 1)

                def multiply(c, b, m0, m1):
                    if m0 == 0:
                        pe.wait_ge(lor, (c + 1) * KH)
                    for m in range(m0, m1):
                        if not (static(c, 1) and m < 4):
                            pe.wait_ge(evr, c * KF + m - 3)
                        product(nc, mb[m % 4][:, 0:CW], whi, wlo, hhi[b], hlo[b], KH, m).then_inc(mmr, 1)

                turn(0, 0)

                def body(c, b):
                    multiply(c - 1, 1 - b, 0, 4)
                    turn(c, b)
                    multiply(c - 1, 1 - b, 4, KF)

                chunks(pe, body)
                multiply(NCH - 1, 1, 0, KF)


def norm_constants(nc, dve, pool_root, gam, bet, stats, mv, ve, rs, sc, sh, sems, n, rows):
    agr, vpe, rst, scr, tmr, shr = sems
    for m in range(n):
        nc.vector.bn_aggr(mv[:, m, :], stats[:, m, :]).then_inc(agr, 1)
    dve.wait_ge(agr, n)
    nc.vector.tensor_scalar_add(ve[:, :], mv[:, :, 1], EPS).then_inc(vpe, 1)
    dve.wait_ge(rst, 1)
    nc.vector.tensor_tensor(sc[:, :], gam[:, :], rs[:, :], ALU.mult).then_inc(scr, 1)
    dve.wait_ge(scr, 1)
    nc.vector.tensor_tensor(rs[:, :], mv[:, :, 0], sc[:, :], ALU.mult).then_inc(tmr, 1)
    dve.wait_ge(tmr, 1)
    nc.vector.tensor_tensor(sh[:, :], bet[:, :], rs[:, :], ALU.subtract).then_inc(shr, 1)


def gnn_down(nc, sem, psum, mhalf, h1T, g1, beta1, W2, b2, h2T, stats1, stats2):
    with ExitStack() as ctx:
        def sb(name, shape, dt=F32):
            return ctx.enter_context(nc.sbuf_tensor(name, shape, dt))

        wst = sb("w2_whole", [P, KF, H])
        whi, wlo = sb("w2_hi", [P, KF, H], F32R), sb("w2_lo", [P, KF, H], F32R)
        b2c, gc, bc = sb("b2c", [P, KH]), sb("g1c", [P, KF]), sb("beta1c", [P, KF])
        mv, ve, rs = sb("mv1", [P, KF, 2]), sb("ve1", [P, KF]), sb("rs1", [P, KF])
        sc, sh = sb("scale1", [P, KF]), sb("shift1", [P, KF])
        h1 = [sb(f"h1in{i}", [P, KF, CW]) for i in range(2)]
        aw = sb("a_whole", [P, KF, CW])
        ahi = [sb(f"ahi{i}", [P, KF, CW], F32R) for i in range(2)]
        alo = [sb(f"alo{i}", [P, KF, CW], F32R) for i in range(2)]
        h2o = [sb(f"h2o{i}", [P, KH, CW]) for i in range(2)]

        wld, whd, wld2 = sem("w2_loaded"), sem("w2_hi_done"), sem("w2_lo_done")
        nrm = [sem(n) for n in ("h1_agg", "h1_var_eps", "h1_rstd", "scale1_ready", "mean_scaled1", "shift1_ready")]
        ldh = [sem(f"h1_loaded{i}") for i in range(2)]
        sto = [sem(f"h2_stored{i}") for i in range(2)]
        awr, hir, lor = sem("a_ready"), sem("a_hi_ready"), sem("a_lo_ready")
        mmr, evr, str_ = sem("h2_psum"), sem("h2_evicted"), sem("h2_stats")

        def span(c):
            return bass.ds(c * CW, CW)

        def static(c, least):
            return isinstance(c, int) and c < least

        def chunks(eng, body):
            body(0, 0)
            body(1, 1)
            with eng.Fori(1, NCH // 2) as it:
                body(it * 2, 0)
                body(it * 2 + 1, 1)

        def half(c, b, of):
            return (c - b) * (of // 2) + of

        with nc.Block() as block:
            @block.sync
            def _(sp):
                with nc.allow_non_contiguous_dma(reason="vectors by channel"):
                    sp.dma_start(gc[:, :], g1.rearrange("(m p) -> p m", p=P)).then_inc(wld, 16)
                    sp.dma_start(bc[:, :], beta1.rearrange("(m p) -> p m", p=P)).then_inc(wld, 16)
                    sp.dma_start(b2c[:, :], b2.rearrange("(m p) -> p m", p=P)).then_inc(wld, 16)
                sp.dma_start(wst[:, :, :], W2.rearrange("(k p) n -> p k n", p=P)).then_inc(wld, 16)

                def load(c, b):
                    if not static(c, 2):
                        sp.wait_ge(hir, (c - 1) * KF)
                    sp.dma_start(h1[b][:, :, :], h1T[:, :, span(c)].rearrange("m p n -> p m n")).then_inc(ldh[b], 16)

                def store(c, b):
                    sp.wait_ge(evr, (c + 1) * KH)
                    sp.dma_start(h2T[:, :, span(c)].rearrange("m p n -> p m n"), h2o[b][:, :, :]).then_inc(sto[b], 16)

                load(0, 0)
                load(1, 1)
                with sp.Fori(0, NCH // 2 - 1) as it:
                    load(it * 2 + 2, 0)
                    store(it * 2, 0)
                    load(it * 2 + 3, 1)
                    store(it * 2 + 1, 1)
                store(NCH - 2, 0)
                store(NCH - 1, 1)
                for b in range(2):
                    sp.wait_ge(sto[b], 16 * (NCH // 2))

            @block.gpsimd
            def _(pool):
                pool.wait_ge(nrm[1], 1)
                nc.gpsimd.tensor_tensor(rs[:, :], ve[:, :], mhalf[:, 0:KF], ALU.pow).then_inc(nrm[2], 1)

            @block.vector
            def _(dve):
                dve.wait_ge(wld, 64)
                norm_constants(nc, dve, None, gc, bc, stats1, mv, ve, rs, sc, sh, nrm, KF, None)
                for k in range(KF):
                    split_weight(nc.vector, wst, whi, wlo, whd, wld2, k)

                def low(c, b):
                    if not static(c, 2):
                        dve.wait_ge(mmr, (c - 1) * KH)
                    for k in range(KF):
                        dve.wait_ge(hir, c * KF + k + 1)
                        nc.vector.tensor_tensor(alo[b][:, k, :], aw[:, k, :], ahi[b][:, k, :].bitcast(F32),
                                                ALU.subtract).then_inc(lor, 1)

                def stats(c, b):
                    for m in range(KH):
                        dve.wait_ge(evr, c * KH + m + 1)
                        nc.vector.bn_stats(stats2[:, m, bass.ds(c * 6, 6)], h2o[b][:, m, :]).then_inc(str_, 1)

                low(0, 0)
                low(1, 1)
                stats(0, 0)
                with dve.Fori(1, NCH // 2) as it:
                    low(it * 2, 0)
                    stats(it * 2 - 1, 1)
                    low(it * 2 + 1, 1)
                    stats(it * 2, 0)
                stats(NCH - 1, 1)
                dve.wait_ge(str_, NCH * KH)

            @block.scalar
            def _(act):
                act.wait_ge(nrm[5], 1)
                act.wait_ge(wld, 64)

                def nonlinear(c, b):
                    act.wait_ge(ldh[b], half(c, b, 16))
                    if not static(c, 2):
                        act.wait_ge(mmr, (c - 1) * KH)
                    for k in range(KF):
                        if not static(c, 1):
                            act.wait_ge(lor, (c - 1) * KF + k + 1)
                        nc.scalar.activation(aw[:, k, :], h1[b][:, k, :], ACT.Silu, bias=sh[:, k:k + 1],
                                             scale=sc[:, k:k + 1]).then_inc(awr, 1)
                        act.wait_ge(awr, c * KF + k + 1)
                        nc.scalar.activation(ahi[b][:, k, :], aw[:, k, :], ACT.Copy).then_inc(hir, 1)

                def evict(c, b):
                    if not static(c, 2):
                        act.wait_ge(sto[b], half(c, b, 16) - 16)
                        act.wait_ge(str_, (c - 1) * KH)
                    for m in range(KH):
                        act.wait_ge(mmr, c * KH + m + 1)
                        nc.scalar.activation(h2o[b][:, m, :], psum[(4 * b + m)][:, 0:CW], ACT.Identity,
                                             bias=b2c[:, m:m + 1]).then_inc(evr, 1)

                nonlinear(0, 0)
                nonlinear(1, 1)
                evict(0, 0)
                with act.Fori(1, NCH // 2) as it:
                    nonlinear(it * 2, 0)
                    evict(it * 2 - 1, 1)
                    nonlinear(it * 2 + 1, 1)
                    evict(it * 2, 0)
                evict(NCH - 1, 1)

            @block.tensor
            def _(pe):
                pe.wait_ge(wld2, KF)

                def multiply(c, b):
                    pe.wait_ge(lor, (c + 1) * KF)
                    for m in range(KH):
                        if not static(c, 2):
                            pe.wait_ge(evr, (c - 2) * KH + m + 1)
                        product(nc, psum[4 * b + m][:, 0:CW], whi, wlo, ahi[b], alo[b], KF, m).then_inc(mmr, 1)

                chunks(pe, multiply)


def mixture(nc, sem, psum, ident, mhalf, x, h2T, x1d, g2, beta2, controller, f1, f2, out, stats2):
    with ExitStack() as ctx:
        def sb(name, shape, dt=F32):
            return ctx.enter_context(nc.sbuf_tensor(name, shape, dt))

        f1s = sb("f1s", [P, KH, ES * FF])
        f2s = sb("f2s", [P, NE, H])
        cts = sb("controller_s", [P, KH, ES])
        yT = sb("yT", [P, KH, ES, TB * GB])
        ibd = sb("inner_bd", [P, NE, TB, NS, GB])
        pT = sb("perm_T", [ES, TB, P], F32R)
        gc, bc = sb("g2c", [P, KH]), sb("beta2c", [P, KH])
        mv2, ve2, rs2 = sb("mv2", [P, KH, 2]), sb("ve2", [P, KH]), sb("rs2", [P, KH])
        sc, sh = sb("scale2", [P, KH]), sb("shift2", [P, KH])
        h2 = [sb(f"h2in{i}", [P, KH, 2 * P]) for i in range(2)]
        gT = sb("gT", [P, KH, 2 * P])
        xt = [sb(f"xres{i}", [P, H]) for i in range(2)]
        x1 = [sb(f"x1_{i}", [P, H]) for i in range(2)]
        st, mv = sb("st2", [P, 6]), sb("mvx", [P, 2])
        ve, rs = sb("vex", [P, 1]), sb("rsx", [P, 1])
        xn = sb("xn2", [P, H])
        xhi = [sb(f"xn2_hi{i}", [P, H], F32R) for i in range(2)]
        xlo = [sb(f"xn2_lo{i}", [P, H], F32R) for i in range(2)]
        xT = sb("xn2_T", [P, KH, P])
        lg, mx = sb("logits", [ES, P]), sb("logits_max", [ES, GB])
        tie = sb("tie", [ES, GT])
        pbd = sb("perm_bd", [P, ES, GB], F32R)
        rbd = sb("back_bd", [P, QB, P], F32R)
        ihi = [sb(f"inter_hi{i}", [P, H], F32R) for i in range(2)]
        ilo = [sb(f"inter_lo{i}", [P, H], F32R) for i in range(2)]
        x1b = [sb(f"x1_back{i}", [P, H]) for i in range(2)]
        ob = [sb(f"out_s{i}", [P, H]) for i in range(2)]
        rep = sb("rep", [ES, QB * P], F32R)
        repf = ob[0][0:ES, :]
        pidx, pq = sb("pidx", [P, 1], I32), sb("pq", [P, 2], I32)
        pqf = sb("pqf", [P, 2])
        gid, tgid = sb("gid", [P, GB]), ob[1][:, 0:P]
        mtg, mrt = sb("mask_token_group", [P, GB]), sb("mask_row_token", [P, P])

        bA, bB, bC, bD, bI, bF = psum[0], psum[1], psum[2], psum[3:5], psum[5:7], psum[7]
        bL, bP = bB[0:ES, 0:P], bC[:, 0:ES]

        wld, wld2 = sem("norm2_loaded"), sem("ffn_loaded")
        nrm = [sem(n) for n in ("h2_agg", "h2_var_eps", "h2_rstd", "scale2_ready", "mean_scaled2", "shift2_ready")]
        cst, cstv = sem("ffn_const"), sem("ffn_const_v")
        ldh = [sem(f"h2_loaded{i}") for i in range(2)]
        ldx = [sem(f"x_loaded{i}") for i in range(2)]
        x1s = [sem(f"x1_stored{i}") for i in range(2)]
        ldb = [sem(f"x1_back_loaded{i}") for i in range(2)]
        ots = [sem(f"out_stored{i}") for i in range(2)]
        gr, t1, x1r = sem("g_ready"), sem("g_transposed"), sem("x1_ready")
        bst, bag, vpe, rst = sem("x1_stats"), sem("x1_meanvar"), sem("x1_var_eps"), sem("x1_rstd")
        xnr, xhr, xlr, t2, xTr = sem("xn2_ready"), sem("xn2_hi_r"), sem("xn2_lo_r"), sem("xn2_transposed"), sem("xn2T_ready")
        lgp, lgr, mxr, pTr = sem("logits_psum"), sem("logits_ready"), sem("max_ready"), sem("permT_ready")
        ptp, pbr, yp, yr = sem("perm_transposed"), sem("perm_bd_ready"), sem("y_psum"), sem("y_ready")
        inp, inr = sem("inner_psum"), sem("inner_ready")
        rp, rr, ip, ihr, ilr = sem("r_psum"), sem("r_ready"), sem("inter_psum"), sem("inter_hi_r"), sem("inter_lo_r")
        fp, otr = sem("final_psum"), sem("out_ready")

        def static(c, least):
            return isinstance(c, int) and c < least

        def row(k, j):
            return (N - BW if isinstance(k, int) and k == NB - 1 else k * BW) + j * P

        def by2(t, par, of):
            return (t - par) * (of // 2) + of

        def blocks(eng, body):
            body(0, None)
            body(1, 0)
            with eng.Fori(2, NB - 1) as k:
                body(k, k - 1)
            body(NB - 1, NB - 2)
            body(None, NB - 1)

        STEPS = TB + 2

        def steps(front, back):
            for m in range(STEPS):
                yield (m,
                       m if front and m < TB else None,
                       m - 1 if front and 1 <= m <= TB else None,
                       m - 2 if front and m >= 2 else None,
                       m if back and m < TB else None)

        with nc.Block() as block:
            @block.sync
            def _(sp):
                with nc.allow_non_contiguous_dma(reason="vectors by channel"):
                    sp.dma_start(gc[:, :], g2.rearrange("(m p) -> p m", p=P)).then_inc(wld, 16)
                    sp.dma_start(bc[:, :], beta2.rearrange("(m p) -> p m", p=P)).then_inc(wld, 16)
                sp.dma_start(cts[:, :, :], controller.rearrange("(k p) e s -> p k (e s)", p=P)).then_inc(wld2, 16)
                sp.dma_start(f1s[:, :, :], f1.rearrange("(k p) e s f -> p k (e s f)", p=P)).then_inc(wld2, 16)
                sp.dma_start(f2s[:, :, :], f2.rearrange("e s f d -> (s f) e d")).then_inc(wld2, 16)

                def load_h(k, p):
                    pair = k * (TB // 2) + p
                    if not static(pair, 2):
                        sp.wait_ge(gr, (pair - 1) * KH)
                    sp.dma_start(h2[p % 2][:, :, :], h2T[:, :, bass.ds(row(k, 2 * p), 2 * P)].rearrange("m p n -> p m n"))\
                        .then_inc(ldh[p % 2], 16)

                def load_x(k, j):
                    t = k * TB + j
                    if not static(t, 2):
                        sp.wait_ge(x1r, t - 1)
                    sp.dma_start(xt[j % 2][:, :], x[bass.ds(row(k, j), P), :]).then_inc(ldx[j % 2], 16)

                def store_x1(k, j):
                    t = k * TB + j
                    sp.wait_ge(x1r, t + 1)
                    sp.dma_start(x1d[bass.ds(t * P, P), :], x1[j % 2][:, :]).then_inc(x1s[j % 2], 16)

                def body(k, _):
                    if k is None:
                        return
                    load_h(k, 0)
                    load_x(k, 0)
                    load_x(k, 1)
                    load_h(k, 1)
                    for j in range(TB):
                        store_x1(k, j)
                        if j + 2 < TB:
                            load_x(k, j + 2)
                        if j % 2 and j // 2 + 2 < TB // 2:
                            load_h(k, j // 2 + 2)

                blocks(sp, body)

            @block.gpsimd
            def _(pool):
                nc.gpsimd.iota(pidx[:, :], pattern=[[0, 1]], base=0, channel_multiplier=1).then_inc(cst, 1)
                nc.gpsimd.iota(gid[:, :], pattern=[[1, GB]], base=0, channel_multiplier=0,
                               allow_small_or_imprecise_dtypes=True).then_inc(cst, 1)
                nc.gpsimd.iota(tgid[:, :], pattern=[[1, GB], [0, GT]], base=0, channel_multiplier=0,
                               allow_small_or_imprecise_dtypes=True).then_inc(cst, 1)
                pool.wait_ge(cst, 3)
                pool.wait_ge(cstv, 1)
                nc.gpsimd.affine_select(out=repf[:, :], in_=repf[:, :], compare_op=ALU.is_ge, fill=0.0, base=0,
                                        pattern=[[1, QB * P]], channel_multiplier=-GB).then_inc(cst, 1)
                pool.wait_ge(cst, 4)
                nc.gpsimd.affine_select(out=repf[:, :], in_=repf[:, :], compare_op=ALU.is_ge, fill=0.0, base=GB - 1,
                                        pattern=[[-1, QB * P]], channel_multiplier=GB).then_inc(cst, 1)
                pool.wait_ge(nrm[1], 1)
                nc.gpsimd.tensor_tensor(rs2[:, :], ve2[:, :], mhalf[:, 0:KH], ALU.pow).then_inc(nrm[2], 1)

                def load_back(kb, j):
                    t = kb * TB + j
                    pool.wait_ge(x1s[j % 2], by2(t, j % 2, 16))
                    if not static(t, 2):
                        pool.wait_ge(otr, t - 1)
                    pool.dma_start(x1b[j % 2][:, :], x1d[bass.ds(t * P, P), :]).then_inc(ldb[j % 2], 16)

                def store_out(kb, j):
                    t = kb * TB + j
                    pool.wait_ge(otr, t + 1)
                    pool.dma_start(out[bass.ds(row(kb, j), P), :], ob[j % 2][:, :]).then_inc(ots[j % 2], 16)

                def body(k, kb):
                    if k is None:
                        for b in range(2):
                            pool.wait_ge(ots[b], 16 * (TB // 2) * (NB - 1))
                    if kb is not None:
                        load_back(kb, 0)
                        load_back(kb, 1)
                    for m, new, _, _, back in steps(k is not None, kb is not None):
                        if new is not None:
                            t = k * TB + new
                            pool.wait_ge(vpe, t + 1)
                            nc.gpsimd.tensor_tensor(rs[:, :], ve[:, :], mhalf[:, 0:1], ALU.pow).then_inc(rst, 1)
                            free = [] if static(t, 2) else [(yp, (t - 1) * KH)]
                            wait_apart(pool, (cst, 5), (xnr, t + 1), *free)
                            nc.gpsimd.tensor_copy(xhi[new % 2][:, :], xn[:, :]).then_inc(xhr, 1)
                        if kb is not None and 1 <= m < TB - 1:
                            load_back(kb, m + 1)
                        if kb is not None and 1 <= m <= TB:
                            store_out(kb, m - 1)

                blocks(pool, body)
                for b in range(2):
                    pool.wait_ge(ots[b], 16 * (TB // 2) * NB)

            @block.vector
            def _(dve):
                nc.vector.memset(repf[:, :], 1.0).then_inc(cstv, 1)
                nc.vector.memset(ibd[:, :, :, :, :], 0.0).then_inc(cstv, 1)
                for t in range(GT):
                    nc.vector.memset(tie[:, t:t + 1], float(np.linspace(0.0, 1e-6, GT, dtype=np.float32)[t])).then_inc(cstv, 1)
                dve.wait_ge(wld, 32)
                norm_constants(nc, dve, None, gc, bc, stats2, mv2, ve2, rs2, sc, sh, nrm, KH, None)
                dve.wait_ge(cst, 5)
                nc.vector.tensor_copy(rep[:, :], repf[:, :]).then_inc(cstv, 1)
                nc.vector.tensor_scalar(pq[:, 0:1], pidx[:, :], 4, None, ALU.logical_shift_right).then_inc(cstv, 1)
                nc.vector.tensor_scalar(pq[:, 1:2], pidx[:, :], GB - 1, None, ALU.bitwise_and).then_inc(cstv, 1)
                dve.wait_ge(cstv, GT + 5)
                nc.vector.tensor_copy(pqf[:, :], pq[:, :]).then_inc(cstv, 1)
                dve.wait_ge(cstv, GT + 6)
                nc.vector.tensor_scalar(mtg[:, :], gid[:, :], pqf[:, 0:1], None, ALU.is_equal).then_inc(cstv, 1)
                nc.vector.tensor_scalar(mrt[:, :], tgid[:, :], pqf[:, 1:2], None, ALU.is_equal).then_inc(cstv, 1)
                dve.wait_ge(cstv, GT + 8)

                def new_tile(k, j):
                    t = k * TB + j
                    dve.wait_ge(t1, t + 1)
                    dve.wait_ge(ldx[j % 2], by2(t, j % 2, 16))
                    if not static(t, 2):
                        dve.wait_ge(x1s[j % 2], by2(t, j % 2, 16) - 16)
                    nc.vector.tensor_tensor(x1[j % 2][:, :], xt[j % 2][:, :], bA[:, :], ALU.add).then_inc(x1r, 1)
                    dve.wait_ge(x1r, t + 1)
                    nc.vector.bn_stats(st[:, :], x1[j % 2][:, :]).then_inc(bst, 1)
                    wait_apart(dve, (cstv, GT + 8), (bst, t + 1))
                    nc.vector.bn_aggr(mv[:, :], st[:, :]).then_inc(bag, 1)
                    dve.wait_ge(bag, t + 1)
                    nc.vector.tensor_scalar_add(ve[:, :], mv[:, 1:2], EPS).then_inc(vpe, 1)

                def normalize(k, j):
                    t = k * TB + j
                    dve.wait_ge(rst, t + 1)
                    if not static(t, 1):
                        dve.wait_ge(t2, t)
                        dve.wait_ge(xhr, t)
                    nc.vector.tensor_scalar(xn[:, :], x1[j % 2][:, :], mv[:, 0:1], rs[:, 0:1],
                                            ALU.subtract, ALU.mult).then_inc(xnr, 1)

                def low(k, j):
                    t = k * TB + j
                    dve.wait_ge(xhr, t + 1)
                    if not static(t, 2):
                        dve.wait_ge(yp, (t - 1) * KH)
                    nc.vector.tensor_tensor(xlo[j % 2][:, :], xn[:, :], xhi[j % 2][:, :].bitcast(F32),
                                            ALU.subtract).then_inc(xlr, 1)

                def select(k, j):
                    t = k * TB + j
                    dve.wait_ge(lgp, t + 1)
                    lg3 = lg[:, :].rearrange("p (g t) -> p g t", t=GT)
                    nc.vector.tensor_tensor(lg3, bL.rearrange("p (g t) -> p g t", t=GT),
                                            tie[:, :].unsqueeze(1).to_broadcast([ES, GB, GT]), ALU.add).then_inc(lgr, 1)
                    dve.wait_ge(lgr, t + 1)
                    nc.vector.tensor_reduce(mx[:, :], lg3, AX.X, ALU.max).then_inc(mxr, 1)
                    dve.wait_ge(mxr, t + 1)
                    if not static(k, 1):
                        dve.wait_ge(rp, t - TB + 1)
                    nc.vector.tensor_tensor(pT[:, j, :].rearrange("p (g t) -> p g t", t=GT), lg3,
                                            mx[:, :].unsqueeze(2).to_broadcast([ES, GB, GT]), ALU.is_equal).then_inc(pTr, 1)

                def spread(k, j):
                    t = k * TB + j
                    dve.wait_ge(ptp, t + 1)
                    if not static(t, 1):
                        dve.wait_ge(yp, t * KH)
                    nc.vector.tensor_tensor(pbd[:, :, :], bP.unsqueeze(2).to_broadcast([P, ES, GB]),
                                            mtg[:, :].unsqueeze(1).to_broadcast([P, ES, GB]), ALU.mult).then_inc(pbr, 1)

                def back_rows(kb, j):
                    t = kb * TB + j
                    dve.wait_ge(rp, t + 1)
                    if not static(t, 1):
                        dve.wait_ge(fp, t * QB)
                    nc.vector.tensor_tensor(rbd[:, :, :], bA[:, :].rearrange("p (b t) -> p b t", t=P),
                                            mrt[:, :].unsqueeze(1).to_broadcast([P, QB, P]), ALU.mult).then_inc(rr, 1)

                def inter_low(kb, j, b):
                    q = (kb * TB + j) * QB + b
                    dve.wait_ge(ihr, q + 1)
                    if not static(q, 2):
                        dve.wait_ge(fp, q - 1)
                    nc.vector.tensor_tensor(ilo[b % 2][:, :], bI[b % 2][:, :], ihi[b % 2][:, :].bitcast(F32),
                                            ALU.subtract).then_inc(ilr, 1)

                def result(kb, j):
                    t = kb * TB + j
                    dve.wait_ge(fp, (t + 1) * QB)
                    dve.wait_ge(ldb[j % 2], by2(t, j % 2, 16))
                    if not static(t, 2):
                        dve.wait_ge(ots[j % 2], by2(t, j % 2, 16) - 16)
                    nc.vector.tensor_tensor(ob[j % 2][:, :], bF[:, :], x1b[j % 2][:, :], ALU.add).then_inc(otr, 1)

                def body(k, kb):
                    for m, new, sel, _, back in steps(k is not None, kb is not None):
                        if new is not None:
                            new_tile(k, new)
                        if sel is not None:
                            select(k, sel)
                        if new is not None:
                            normalize(k, new)
                        if back is not None:
                            back_rows(kb, back)
                        if new is not None:
                            low(k, new)
                        if back is not None:
                            inter_low(kb, back, 0)
                            inter_low(kb, back, 1)
                            inter_low(kb, back, 2)
                            inter_low(kb, back, 3)
                        if sel is not None:
                            spread(k, sel)
                        if back is not None:
                            result(kb, back)
                    if k is not None:
                        for h in range(2):
                            dve.wait_ge(inp, k * 2 + h + 1)
                            for s in range(0, NS):
                                nc.vector.tensor_scalar_max(
                                    ibd[32 * s:32 * s + 32, 8 * h:8 * h + 8, :, s, :],
                                    bD[h][32 * s:32 * s + 32, :].rearrange("p (e j g) -> p e j g", e=8, g=GB),
                                    0.0).then_inc(inr, 1)

                blocks(dve, body)

            @block.scalar
            def _(act):
                act.wait_ge(nrm[5], 1)

                def nonlinear(k, p):
                    pair = k * (TB // 2) + p
                    act.wait_ge(ldh[p % 2], by2(pair, p % 2, 16))
                    if not static(pair, 1):
                        act.wait_ge(t1, pair * 2)
                    for c in range(KH):
                        nc.scalar.activation(gT[:, c, :], h2[p % 2][:, c, :], ACT.Silu, bias=sh[:, c:c + 1],
                                             scale=sc[:, c:c + 1]).then_inc(gr, 1)

                def body(k, kb):
                    if k is not None:
                        nonlinear(k, 0)
                    for m, new, sel, summed, back in steps(k is not None, kb is not None):
                        if summed is not None:
                            t = k * TB + summed
                            if summed == 0 and not static(k, 1):
                                act.wait_ge(inp, k * 2)
                            for c in range(KH):
                                act.wait_ge(yp, t * KH + c + 1)
                                nc.scalar.activation(
                                    yT[:, c, :, summed * GB:(summed + 1) * GB],
                                    bD[c % 2][:, :].rearrange("p (e g) -> p e g", g=GB), ACT.Copy).then_inc(yr, 1)
                        if back is not None:
                            for b in range(2):
                                inter_high(kb, back, b)
                        if new is not None:
                            t = k * TB + new
                            act.wait_ge(t2, t + 1)
                            if not static(t, 1):
                                act.wait_ge(lgp, t)
                            nc.scalar.activation(xT[:, :, :], bB[:, :].rearrange("p (k n) -> p k n", n=P),
                                                 ACT.Copy).then_inc(xTr, 1)
                        if back is not None:
                            for b in range(2, QB):
                                inter_high(kb, back, b)
                        if new is not None and new % 2 and new + 1 < TB:
                            nonlinear(k, new // 2 + 1)

                def inter_high(kb, j, b):
                    q = (kb * TB + j) * QB + b
                    act.wait_ge(ip, q + 1)
                    if not static(q, 2):
                        act.wait_ge(fp, q - 1)
                    nc.scalar.activation(ihi[b % 2][:, :], bI[b % 2][:, :], ACT.Copy).then_inc(ihr, 1)

                blocks(act, body)

            @block.tensor
            def _(pe):
                pe.wait_ge(wld2, 48)
                pe.wait_ge(cstv, GT + 8)

                def turn_g(k, j):
                    t = k * TB + j
                    pe.wait_ge(gr, (k * (TB // 2) + j // 2 + 1) * KH)
                    if not static(k, 1):
                        pe.wait_ge(rr, t - TB)
                    elif j > 0:
                        pe.wait_ge(x1r, t)
                    for c in range(KH):
                        last = nc.tensor.transpose(bA[:, c * P:(c + 1) * P],
                                                   gT[:, c, (j % 2) * P:(j % 2 + 1) * P], ident[:, :])
                    last.then_inc(t1, 1)

                def turn_x(k, j):
                    t = k * TB + j
                    pe.wait_ge(xnr, t + 1)
                    if not static(t, 1):
                        pe.wait_ge(lgr, t)
                    for c in range(KH):
                        last = nc.tensor.transpose(bB[:, c * P:(c + 1) * P], xn[:, c * P:(c + 1) * P], ident[:, :])
                    last.then_inc(t2, 1)

                def logits(k, j):
                    t = k * TB + j
                    pe.wait_ge(xTr, t + 1)
                    for c in range(KH):
                        last = nc.tensor.matmul(bL, cts[:, c, :], xT[:, c, :], start=(c == 0), stop=(c == KH - 1))
                    last.then_inc(lgp, 1)

                def turn_p(k, j):
                    t = k * TB + j
                    free = [] if static(t, 1) else [(pbr, t)]
                    wait_apart(pe, (cstv, GT + 8), (pTr, t + 1), *free)
                    nc.tensor.transpose(bP, pT[:, j, :].bitcast(F32), ident[0:ES, 0:ES]).then_inc(ptp, 1)

                def sums(k, j):
                    t = k * TB + j
                    pe.wait_ge(pbr, t + 1)
                    pe.wait_ge(xlr, t + 1)
                    if j == 0 and not static(k, 1):
                        pe.wait_ge(inr, k * 8)
                    for c in range(KH):
                        q = t * KH + c
                        if not static(q, 2):
                            pe.wait_ge(yr, q - 1)
                        o = bD[c % 2][:, :]
                        r = pbd[:, :, :].rearrange("p e g -> p (e g)")
                        nc.tensor.matmul(o, xhi[j % 2][:, c * P:(c + 1) * P], r, start=True, stop=False)
                        nc.tensor.matmul(o, xlo[j % 2][:, c * P:(c + 1) * P], r, start=False, stop=True).then_inc(yp, 1)

                def rows(k, kb, j):
                    if k is not None:
                        pe.wait_ge(x1r, k * TB + j + 1)
                    else:
                        pe.wait_ge(rr, kb * TB + j)
                    for b in range(QB):
                        last = nc.tensor.matmul(bA[:, b * P:(b + 1) * P], rep[:, b * P:(b + 1) * P], pT[:, j, :],
                                                start=True, stop=True)
                    last.then_inc(rp, 1)

                def inter(kb, j, b):
                    q = (kb * TB + j) * QB + b
                    if b == 0 and j == 0:
                        pe.wait_ge(inr, (kb + 1) * 8)
                    if not static(q, 2):
                        pe.wait_ge(ilr, q - 1)
                    for i in range(NS):
                        e = 4 * b + i
                        last = nc.tensor.matmul(bI[b % 2][32 * i:32 * i + 32, :],
                                                ibd[:, e, j, :, :].rearrange("p s g -> p (s g)"), f2s[:, e, :],
                                                start=True, stop=True)
                    last.then_inc(ip, 1)

                def final(kb, j, b):
                    q = (kb * TB + j) * QB + b
                    if b == 0:
                        pe.wait_ge(rr, kb * TB + j + 1)
                    pe.wait_ge(ilr, q + 1)
                    if b == 0 and not static(kb * TB + j, 1):
                        pe.wait_ge(otr, kb * TB + j)
                    nc.tensor.matmul(bF[:, :], rbd[:, b, :], ihi[b % 2][:, :], start=(b == 0), stop=False)
                    nc.tensor.matmul(bF[:, :], rbd[:, b, :], ilo[b % 2][:, :], start=False, stop=(b == QB - 1))\
                        .then_inc(fp, 1)

                def body(k, kb):
                    for m, new, sel, summed, back in steps(k is not None, kb is not None):
                        if new is not None:
                            turn_g(k, new)
                        if sel is not None:
                            logits(k, sel)
                        if summed is not None:
                            sums(k, summed)
                        if back is not None:
                            rows(k, kb, back)
                            inter(kb, back, 0)
                            inter(kb, back, 1)
                        if new is not None:
                            turn_x(k, new)
                        if back is not None:
                            final(kb, back, 0)
                            inter(kb, back, 2)
                            final(kb, back, 1)
                            inter(kb, back, 3)
                        if sel is not None:
                            turn_p(k, sel)
                        if back is not None:
                            final(kb, back, 2)
                            final(kb, back, 3)
                    if k is not None:
                        pe.wait_ge(yr, (k + 1) * TB * KH)
                        for h in range(2):
                            for e in range(8 * h, 8 * h + 8):
                                for c in range(KH):
                                    for s in range(NS):
                                        es = e * NS + s
                                        last = nc.tensor.matmul(
                                            bD[h][32 * s:32 * s + 32, (e % 8) * 64:(e % 8) * 64 + 64],
                                            f1s[:, c, es * FF:(es + 1) * FF], yT[:, c, es, :],
                                            start=(c == 0), stop=(c == KH - 1))
                            last.then_inc(inp, 1)

                blocks(pe, body)


def gnn_mixture(nc, x, src, dst, edge_attr, W_e, b_e, W1, b1, g1, beta1, W2, b2, g2, beta2, eps,
                controller, f1, f2, out):
    agg = nc.dram_tensor("aggregate", [N + TRASH, H], F32, kind="Internal").ap()
    h1T = nc.dram_tensor("h1T", [KF, P, N], F32, kind="Internal").ap()
    h2T = nc.dram_tensor("h2T", [KH, P, N], F32, kind="Internal").ap()
    x1d = nc.dram_tensor("x1", [NB * BW, H], F32, kind="Internal").ap()
    with ExitStack() as ctx:
        psum = [ctx.enter_context(nc.psum_tensor(f"bank{i}", [P, 512], F32)) for i in range(8)]
        ident = ctx.enter_context(nc.sbuf_tensor("ident", [P, P], F32))
        mhalf = ctx.enter_context(nc.sbuf_tensor("mhalf", [P, KF], F32))
        stats2 = ctx.enter_context(nc.sbuf_tensor("stats2", [P, KH, NCH * 6], F32))

        def sem(name):
            return ctx.enter_context(nc.semaphore(name))

        identity = sem("identity_ready")
        with nc.Block() as block:
            @block.gpsimd
            def _(pool):
                nc.gpsimd.memset(ident[:, :], 0.0).then_inc(identity, 1)
                pool.wait_ge(identity, 1)
                nc.gpsimd.affine_select(out=ident[:, :], in_=ident[:, :], compare_op=ALU.not_equal, fill=1.0,
                                        base=0, pattern=[[-1, P]], channel_multiplier=1).then_inc(identity, 1)
                pool.wait_ge(identity, 2)
                nc.gpsimd.memset(mhalf[:, :], -0.5).then_inc(identity, 1)
                pool.wait_ge(identity, 3)

            @block.tensor
            def _(pe):
                pe.wait_ge(identity, 3)

        edge_aggregate(nc, sem, psum, ident, x, src, dst, edge_attr, W_e, b_e, agg)
        with nc.sbuf_tensor("stats1", [P, KF, NCH * 6], F32) as stats1:
            gnn_up(nc, sem, psum, ident, mhalf, x, agg, W1, b1, eps, h1T, stats1)
            gnn_down(nc, sem, psum, mhalf, h1T, g1, beta1, W2, b2, h2T, stats1, stats2)
        mixture(nc, sem, psum, ident, mhalf, x, h2T, x1d, g2, beta2, controller, f1, f2, out, stats2)


_INS = ["x", "src", "dst", "edge_attr_64", "L0_gnn_W_e", "L0_gnn_b_e", "L0_gnn_W1", "L0_gnn_b1", "L0_gnn_g1",
        "L0_gnn_beta1", "L0_gnn_W2", "L0_gnn_b2", "L0_gnn_g2", "L0_gnn_beta2", "L0_gnn_eps", "L0_ffn_controller",
        "L0_ffn_f1", "L0_ffn_f2"]


def kernel(**inputs):
    import concourse.bacc as _bacc
    from concourse.bass_utils import run_bass_kernel_spmd as _run

    nc = _bacc.Bacc("TRN2", target_bir_lowering=False, num_devices=1)
    arrays, args = {}, []
    for name in _INS:
        a = np.ascontiguousarray(inputs[name])
        if a.ndim == 0:
            a = a.reshape(1)
        arrays[f"in_{name}"] = a
        args.append(nc.dram_tensor(f"in_{name}", a.shape, mybir.dt.from_np(a.dtype), kind="ExternalInput").ap())
    args.append(nc.dram_tensor("out_0", (N, H), F32, kind="ExternalOutput").ap())
    gnn_mixture(nc, *args)
    r = _run(nc, [arrays], core_ids=[0])
    return r.results[0]["out_0"]
```

```python
import numpy as np
import concourse.bass as bass
from concourse import mybir
from contextlib import ExitStack

F32 = mybir.dt.float32
F32R = mybir.dt.float32r
I32 = mybir.dt.int32
ALU = mybir.AluOpType
ACT = mybir.ActivationFunctionType
AX = mybir.AxisListType

N, H = 10000, 512
E, ED = 5000, 64
P = 128
KH = H // P
F = 2 * H
KF = F // P
EPS = 1e-5
ET = E // P
ER = E - ET * P
EU = 8
ZQ = 3
TRASH = P
CW = 500
NCH = N // CW
SUB = 4
RT = CW // SUB
GT = 16
NE, NS, FF = 16, 4, 32
ES = NE * NS
GB = P // GT
TB = 8
BW = TB * P
NB = -(-N // BW)
QB = ES // GT
UB = 3


def wait_apart(eng, met, *waits):
    found = [(sem, value if isinstance(value, int) else eng.to_reg(value)) for sem, value in waits]
    eng.wait_ge(*met)
    for sem, value in found:
        eng.wait_ge(sem, value)


def edge_aggregate(nc, sem, psum, ident, x, src, dst, edge_attr, W_e, b_e, agg, W1, w1):
    with ExitStack() as ctx:
        def sb(name, shape, dt=F32):
            return ctx.enter_context(nc.sbuf_tensor(name, shape, dt))

        zeros = sb("zeros", [P, 2048])
        web = sb("web", [ED + 1, H])
        before = sb("before", [P, P])
        trash = sb("trash", [P, 1])
        mhalf = sb("mhalf_e", [P, 1])
        eaT = sb("eaT", [ED + 1, EU, P])
        dcol = [sb(f"dcol{i}", [P, 1], I32) for i in range(EU)]
        scol = [sb(f"scol{i}", [P, 1], I32) for i in range(EU)]
        drow = [sb(f"drow{i}", [P, P], I32) for i in range(EU)]
        ea = [sb(f"ea{i}", [P, ED]) for i in range(EU)]
        xg = [sb(f"xg{i}", [P, H]) for i in range(EU)]
        dcolf = [sb(f"dcolf{i}", [P, 1]) for i in range(EU)]
        sel = [sb(f"sel{i}", [P, P]) for i in range(EU)]
        scr = sb("scr", [P, P])
        cnt = [sb(f"cnt{i}", [P, 1]) for i in range(EU)]
        away = [sb(f"away{i}", [P, 1]) for i in range(EU)]
        idx = [sb(f"idx{i}", [P, 1], I32) for i in range(EU)]
        st = [sb(f"est{i}", [P, 6]) for i in range(EU)]
        mv = [sb(f"emv{i}", [P, 2]) for i in range(EU)]
        ve = [sb(f"eve{i}", [P, 1]) for i in range(EU)]
        rs = [sb(f"ers{i}", [P, 1]) for i in range(EU)]
        xn = [sb(f"exn{i}", [P, H]) for i in range(EU)]
        pre = [sb(f"pre{i}", [P, H]) for i in range(EU)]
        msg = [sb(f"msg{i}", [P, H]) for i in range(EU)]
        comb = [sb(f"comb{i}", [P, H]) for i in range(EU)]
        tp, emb, cps = psum[0:2], psum[2:5], psum[5:8]

        wld, const = sem("edge_w_loaded"), sem("edge_const")
        zeroed = [sem(f"zeroed{i}") for i in range(ZQ)]
        w1ld, w1h, w1l = sem("w1_loaded"), sem("w1_hi_done"), sem("w1_lo_done")
        ld = [sem(f"edge_loaded{i}") for i in range(EU)]
        gat = [sem(f"rows_gathered{i}") for i in range(EU)]
        sca = sem("rows_added")
        dcf, sl, ct, aw, ix = sem("dstf"), sem("sel_ready"), sem("cnt_ready"), sem("away_ready"), sem("idx_ready")
        bst, bag, vpe, rst = sem("estats"), sem("emeanvar"), sem("evar_eps"), sem("erstd")
        xnr, prr, msr = sem("exn_ready"), sem("pre_ready"), sem("msg_ready")
        tpr, etr, emr, cpr, cbr = sem("ea_transposed"), sem("eaT_ready"), sem("emb_ready"), sem("comb_psum"), sem("comb_ready")
        CONST = 6

        TURNS = ET // EU + 1
        flat = agg.rearrange("a b -> (a b)").rearrange("(p c) -> p c", p=P)
        cols = flat.shape[1]
        pieces = [(c, min(c + 2048, cols)) for c in range(0, cols, 2048)]
        ROOTS = EU - 2

        def tile_of(it, u):
            it, u = it + u // EU, u % EU
            rows = ER if isinstance(it, int) and it * EU + u == ET else P
            return it * EU + u, u, rows, it

        def turns(eng, turn):
            turn(0, False)
            with eng.Fori(1, TURNS - 2) as it:
                turn(it, False)
            turn(TURNS - 2, False)
            turn(TURNS - 1, True)

        def exists(it, u):
            return not isinstance(it, int) or it * EU + u <= ET

        def used(t, u, n):
            earlier = [v for v in range(EU) if v % n == u % n]
            back = n if u >= n else EU - max(earlier) + u
            return 0 if isinstance(t, int) and t < back else t - back + 1

        def all_zero(eng):
            for i in range(ZQ):
                eng.wait_ge(zeroed[i], 16 * len(pieces[i::ZQ]))

        def static0(value):
            return isinstance(value, int) and value == 0

        def load(eng, it, u):
            t, u, p, it = tile_of(it, u)
            if not (isinstance(it, int) and it == 0):
                wait_apart(eng, (const, CONST), (ix, t - EU + 1), (gat[u], it * 16), (tpr, t - EU + 1))
            e0 = t * P
            eng.dma_start(scol[u][0:p, :], src[bass.ds(e0, p)].rearrange("(p a) -> p a", a=1)).then_inc(ld[u], 16)
            eng.dma_start(dcol[u][0:p, :], dst[bass.ds(e0, p)].rearrange("(p a) -> p a", a=1)).then_inc(ld[u], 16)
            eng.dma_start(drow[u][0:p, 0:p], dst[bass.ds(e0, p)].rearrange("(a p) -> a p", a=1).to_broadcast([p, p])).then_inc(ld[u], 16)
            eng.dma_start(ea[u][0:p, :], edge_attr[bass.ds(e0, p), :]).then_inc(ld[u], 16)

        with nc.Block() as block:
            @block.sync
            def _(sp):
                sp.dma_start(web[0:ED, :], W_e).then_inc(wld, 16)
                sp.dma_start(web[ED:ED + 1, :], b_e.rearrange("(a n) -> a n", a=1)).then_inc(wld, 16)
                sp.wait_ge(const, 1)
                for i, (c0, c1) in enumerate(pieces):
                    if i >= ZQ:
                        sp.wait_ge(zeroed[i % ZQ], 16 * (i // ZQ))
                    sp.dma_start(flat[:, c0:c1], zeros[:, 0:c1 - c0]).then_inc(zeroed[i % ZQ], 16)

                def turn(it, last):
                    for u in range(EU):
                        if exists(it, u + EU):
                            load(sp, it, u + EU)
                    if isinstance(it, int) and it == 0:
                        sp.dma_start(w1["whole"][:, :, :], W1.rearrange("(k p) n -> p k n", p=P)).then_inc(w1ld, 16)

                turns(sp, turn)
                sp.wait_ge(sca, 16 * (ET + 1))
                all_zero(sp)

            @block.scalar
            def _(act):
                def attributes(it, u):
                    t, u, p, it = tile_of(it, u)
                    act.wait_ge(tpr, t + 1)
                    if not (isinstance(it, int) and it == 0):
                        act.wait_ge(emr, t - EU + 1)
                    nc.scalar.activation(eaT[0:ED, u, 0:p], tp[u % 2][0:ED, 0:p], ACT.Copy).then_inc(etr, 1)

                def turn(it, last):
                    for u in range(EU):
                        t, _, p, _ = tile_of(it, u)
                        if exists(it, u + 1):
                            attributes(it, u + 1)
                        act.wait_ge(prr, t + 1)
                        if not (isinstance(it, int) and it == 0):
                            act.wait_ge(cpr, t - EU + 1)
                        nc.scalar.activation(msg[u][0:p, :], pre[u][0:p, :], ACT.Relu).then_inc(msr, 1)
                        act.wait_ge(cpr, t + 1)
                        if not (isinstance(it, int) and it == 0):
                            act.wait_ge(sca, (t - EU + 1) * 16)
                        nc.scalar.activation(comb[u][0:p, :], cps[u % 3][0:p, :], ACT.Copy).then_inc(cbr, 1)

                for u in range(EU):
                    load(act, 0, u)
                act.wait_ge(const, CONST)
                attributes(0, 0)
                turns(act, turn)

            @block.gpsimd
            def _(pool):
                nc.gpsimd.memset(zeros[:, :], 0.0).then_inc(const, 1)
                nc.gpsimd.memset(before[:, :], 1.0).then_inc(const, 1)
                pool.wait_ge(const, 2)
                nc.gpsimd.affine_select(out=before[:, :], in_=before[:, :], compare_op=ALU.is_gt, fill=0.0,
                                        base=0, pattern=[[-1, P]], channel_multiplier=1).then_inc(const, 1)
                nc.gpsimd.iota(trash[:, :], pattern=[[0, 1]], base=N, channel_multiplier=1,
                               allow_small_or_imprecise_dtypes=True).then_inc(const, 1)
                pool.wait_ge(const, 4)
                nc.gpsimd.memset(mhalf[:, :], -0.5).then_inc(const, 1)
                pool.wait_ge(const, 5)
                nc.gpsimd.memset(eaT[ED:ED + 1, :, :], 1.0).then_inc(const, 1)
                pool.wait_ge(const, CONST)

                def gather(it, u):
                    t, u, p, it = tile_of(it, u)
                    free = [] if isinstance(it, int) and it == 0 else [(xnr, t - EU + 1)]
                    wait_apart(pool, (const, CONST), (ld[u], (it + 1) * 64), *free)
                    nc.gpsimd.indirect_dma_start(
                        out=xg[u][0:p, :], out_offset=None, in_=x,
                        in_offset=bass.IndirectOffsetOnAxis(ap=scol[u][0:p, 0:1], axis=0)).then_inc(gat[u], 16)

                def root(it, u):
                    t, u, p, it = tile_of(it, u)
                    pool.wait_ge(vpe, t + 1)
                    nc.gpsimd.tensor_tensor(rs[u][0:p, :], ve[u][0:p, :], mhalf[0:p, :], ALU.pow).then_inc(rst, 1)

                def scatter(it, u):
                    t, u, p, it = tile_of(it, u)
                    earlier = [] if isinstance(t, int) and t == 0 else [(sca, t * 16)]
                    wait_apart(pool, (const, CONST), (cbr, t + 1), *earlier)
                    nc.gpsimd.indirect_dma_start(
                        out=agg, out_offset=bass.IndirectOffsetOnAxis(ap=idx[u][0:p, 0:1], axis=0),
                        in_=comb[u][0:p, :], in_offset=None, compute_op=ALU.add).then_inc(sca, 16)

                for u in range(EU):
                    gather(0, u)
                    if u >= 2:
                        root(0, u - 2)
                all_zero(pool)

                def turn(it, last):
                    for u in range(EU):
                        scatter(it, u)
                        if exists(it, u + EU):
                            gather(it, u + EU)
                        if exists(it, u + ROOTS):
                            root(it, u + ROOTS)

                turns(pool, turn)

            @block.vector
            def _(dve):
                dve.wait_ge(const, CONST)

                def tile(it, u):
                    t, u, p, it = tile_of(it, u)
                    first = isinstance(it, int) and it == 0
                    dve.wait_ge(ld[u], (it + 1) * 64)
                    if not first:
                        dve.wait_ge(sca, (t - EU + 1) * 16)
                        dve.wait_ge(cpr, t - EU + 1)
                    nc.vector.tensor_copy(dcolf[u][0:p, :], dcol[u][0:p, :]).then_inc(dcf, 1)
                    dve.wait_ge(dcf, t + 1)
                    nc.vector.tensor_scalar(sel[u][0:p, 0:p], drow[u][0:p, 0:p], dcolf[u][0:p, 0:1], None,
                                            ALU.is_equal).then_inc(sl, 1)
                    wait_apart(dve, (const, CONST), (sl, t + 1))
                    nc.vector.tensor_tensor_reduce(out=scr[0:p, 0:p], in0=sel[u][0:p, 0:p], in1=before[0:p, 0:p],
                                                   scale=1.0, scalar=0.0, op0=ALU.mult, op1=ALU.max,
                                                   accum_out=cnt[u][0:p, 0:1]).then_inc(ct, 1)
                    nc.vector.tensor_tensor(away[u][0:p, :], trash[0:p, :], dcolf[u][0:p, :], ALU.subtract).then_inc(aw, 1)
                    dve.wait_ge(ct, t + 1)
                    dve.wait_ge(aw, t + 1)
                    nc.vector.scalar_tensor_tensor(out=idx[u][0:p, :], in0=away[u][0:p, :], scalar=cnt[u][0:p, 0:1],
                                                   in1=dcolf[u][0:p, :], op0=ALU.mult, op1=ALU.add).then_inc(ix, 1)
                    dve.wait_ge(gat[u], (it + 1) * 16)
                    nc.vector.bn_stats(st[u][0:p, :], xg[u][0:p, :]).then_inc(bst, 1)
                    wait_apart(dve, (const, CONST), (bst, t + 1))
                    nc.vector.bn_aggr(mv[u][0:p, :], st[u][0:p, :]).then_inc(bag, 1)
                    dve.wait_ge(bag, t + 1)
                    nc.vector.tensor_scalar_add(ve[u][0:p, :], mv[u][0:p, 1:2], EPS).then_inc(vpe, 1)
                    dve.wait_ge(rst, t + 1)
                    nc.vector.tensor_scalar(xn[u][0:p, :], xg[u][0:p, :], mv[u][0:p, 0:1], rs[u][0:p, 0:1],
                                            ALU.subtract, ALU.mult).then_inc(xnr, 1)
                    dve.wait_ge(xnr, t + 1)
                    dve.wait_ge(emr, t + 1)
                    if not first:
                        dve.wait_ge(msr, t - EU + 1)
                    nc.vector.tensor_tensor(pre[u][0:p, :], xn[u][0:p, :], emb[u % 3][0:p, :], ALU.add).then_inc(prr, 1)

                def turn(it, last):
                    for u in range(EU):
                        tile(it, u)
                    if isinstance(it, int) and it == TURNS - 2:
                        dve.wait_ge(w1ld, 16)
                        for k in range(KH):
                            split_weight(nc.vector, w1["whole"], w1["hi"], w1["lo"], w1h, w1l, k)

                turns(dve, turn)
                dve.wait_ge(w1l, KH)

            @block.tensor
            def _(pe):
                def embed(it, u):
                    t, u, p, it = tile_of(it, u)
                    waits = [(etr, used(t, u, 2))]
                    wait_apart(pe, (const, CONST), (ld[u], (it + 1) * 64), *(w for w in waits if not static0(w[1])))
                    nc.tensor.transpose(tp[u % 2][0:ED, 0:p], ea[u][0:p, :], ident[0:p, 0:p]).then_inc(tpr, 1)
                    pe.wait_ge(etr, t + 1)
                    if not static0(used(t, u, 3)):
                        pe.wait_ge(prr, used(t, u, 3))
                    nc.tensor.matmul(emb[u % 3][0:p, :], eaT[:, u, 0:p], web[:, :], start=True, stop=True).then_inc(emr, 1)

                def combine(it, u):
                    t, u, p, it = tile_of(it, u)
                    pe.wait_ge(msr, t + 1)
                    if not static0(used(t, u, 3)):
                        pe.wait_ge(cbr, used(t, u, 3))
                    nc.tensor.matmul(cps[u % 3][0:p, :], sel[u][0:p, 0:p], msg[u][0:p, :], start=True, stop=True).then_inc(cpr, 1)

                def turn(it, last):
                    for u in range(EU):
                        if exists(it, u + 1):
                            embed(it, u + 1)
                        combine(it, u)

                pe.wait_ge(wld, 32)
                pe.wait_ge(const, CONST)
                embed(0, 0)
                turns(pe, turn)


def split_weight(dve, whole, hi, lo, hi_done, lo_done, k):
    nc_v = dve
    nc_v.tensor_copy(hi[:, k, :], whole[:, k, :]).then_inc(hi_done, 1)
    dve.wait_ge(hi_done, k + 1)
    nc_v.tensor_tensor(lo[:, k, :], whole[:, k, :], hi[:, k, :].bitcast(F32), ALU.subtract).then_inc(lo_done, 1)


def product(nc, out, w_hi, w_lo, a_hi, a_lo, chunks, m):
    cols = slice(m * P, (m + 1) * P)
    for k in range(chunks):
        nc.tensor.matmul(out, w_hi[:, k, cols], a_hi[:, k, :], start=(k == 0), stop=False)
        nc.tensor.matmul(out, w_hi[:, k, cols], a_lo[:, k, :], start=False, stop=False)
        last = nc.tensor.matmul(out, w_lo[:, k, cols], a_hi[:, k, :], start=False, stop=(k == chunks - 1))
    return last


def gnn_up(nc, sem, psum, ident, mhalf, x, agg, w1, b1, eps, h1T, stats1, W2, w2):
    with ExitStack() as ctx:
        def sb(name, shape, dt=F32):
            return ctx.enter_context(nc.sbuf_tensor(name, shape, dt))

        whi, wlo = w1["hi"], w1["lo"]
        b1c = sb("b1c", [P, KF])
        epsc, ope = sb("epsc", [P, 1]), sb("one_plus_eps", [P, 1])
        xt = [sb(f"xt{i}", [P, SUB, H]) for i in range(2)]
        at = [sb(f"at{i}", [P, SUB, H]) for i in range(2)]
        ht = sb("ht", [P, SUB, H])
        st = sb("st", [P, SUB, 6])
        mv = sb("mv", [P, SUB, 2])
        ve, rs, rse = sb("ve", [P, SUB]), sb("rs", [P, SUB]), sb("rse", [P, SUB])
        hhi = [sb(f"hhi{i}", [P, KH, CW], F32R) for i in range(2)]
        hlo = [sb(f"hlo{i}", [P, KH, CW], F32R) for i in range(2)]
        h1o = [sb(f"h1o{i}", [P, KF, CW]) for i in range(2)]
        tb, mb = psum[0:KH], psum[4:8]

        wld = sem("eps_b1_loaded")
        w2ld, w2h, w2l = sem("w2_loaded"), sem("w2_hi_done"), sem("w2_lo_done")
        ldx = [sem(f"x_agg_loaded{i}") for i in range(2)]
        sto = [sem(f"h1_stored{i}") for i in range(2)]
        bst, bag, vpe, rst, rsd = sem("xstats"), sem("xmeanvar"), sem("xvar_eps"), sem("xrstd"), sem("xrstd_eps")
        opr = sem("ope_ready")
        nrm, hrd = sem("x_normalized"), sem("h_ready")
        tpr, hir, lor = sem("h_transposed"), sem("h_hi_ready"), sem("h_lo_ready")
        mmr, evr, str_ = sem("h1_psum"), sem("h1_evicted"), sem("h1_stats")

        def span(c):
            return bass.ds(c * CW, CW)

        def chunks(eng, body):
            body(1, 1)
            body(2, 0)
            with eng.Fori(1, (NCH - 2) // 2) as it:
                body(it * 2 + 1, 1)
                body(it * 2 + 2, 0)
            body(NCH - 1, 1)

        def static(c, least):
            return isinstance(c, int) and c < least

        with nc.Block() as block:
            @block.sync
            def _(sp):
                sp.dma_start(epsc[:, :], eps.rearrange("(a n) -> a n", a=1).to_broadcast([P, 1])).then_inc(wld, 16)

                def load(c, b):
                    if not static(c, 2):
                        sp.wait_ge(hrd, (c - 1) * SUB)
                    rows = x[span(c), :].rearrange("(j p) h -> p j h", p=RT)
                    sp.dma_start(xt[b][0:RT, :, :], rows).then_inc(ldx[b], 16)
                    rows = agg[span(c), :].rearrange("(j p) h -> p j h", p=RT)
                    sp.dma_start(at[b][0:RT, :, :], rows).then_inc(ldx[b], 16)

                def store(c, b):
                    sp.wait_ge(evr, (c + 1) * KF)
                    sp.dma_start(h1T[:, :, span(c)].rearrange("m p n -> p m n"), h1o[b][:, :, :]).then_inc(sto[b], 16)

                load(0, 0)
                with nc.allow_non_contiguous_dma(reason="a bias by channel"):
                    sp.dma_start(b1c[:, :], b1.rearrange("(m p) -> p m", p=P)).then_inc(wld, 16)
                load(1, 1)
                sp.dma_start(w2["whole"][:, :, :], W2.rearrange("(k p) n -> p k n", p=P)).then_inc(w2ld, 16)
                load(2, 0)
                store(0, 0)
                with sp.Fori(0, (NCH - 4) // 2) as it:
                    load(it * 2 + 3, 1)
                    store(it * 2 + 1, 1)
                    load(it * 2 + 4, 0)
                    store(it * 2 + 2, 0)
                load(NCH - 1, 1)
                store(NCH - 3, 1)
                store(NCH - 2, 0)
                store(NCH - 1, 1)
                for b in range(2):
                    sp.wait_ge(sto[b], 16 * (NCH // 2))

            @block.gpsimd
            def _(pool):
                def root(c, b):
                    pool.wait_ge(vpe, c + 1)
                    nc.gpsimd.tensor_tensor(rs[0:RT, :], ve[0:RT, :], mhalf[0:RT, 0:SUB], ALU.pow).then_inc(rst, 1)

                root(0, 0)

                def body(c, b):
                    root(c, b)
                    if isinstance(c, int) and c <= 2:
                        half = range((c - 1) * KF // 2, c * KF // 2)
                        pool.wait_ge(w2ld, 16)
                        for k in half:
                            nc.gpsimd.tensor_copy(w2["hi"][:, k, :], w2["whole"][:, k, :]).then_inc(w2h, 1)
                        for k in half:
                            pool.wait_ge(w2h, k + 1)
                            nc.gpsimd.tensor_tensor(w2["lo"][:, k, :], w2["whole"][:, k, :],
                                                    w2["hi"][:, k, :].bitcast(F32), ALU.subtract).then_inc(w2l, 1)

                chunks(pool, body)
                pool.wait_ge(w2l, KF)

            @block.vector
            def _(dve):
                dve.wait_ge(wld, 32)
                nc.vector.tensor_scalar_add(ope[:, :], epsc[:, :], 1.0).then_inc(opr, 1)
                dve.wait_ge(opr, 1)

                def prepare(c, b):
                    if b == 0:
                        dve.wait_ge(ldx[0], (c // 2 + 1) * 32 if isinstance(c, int) else (c + 2) * 16)
                    else:
                        dve.wait_ge(ldx[1], (c + 1) * 16)
                    for j in range(SUB):
                        nc.vector.bn_stats(st[0:RT, j, :], xt[b][0:RT, j, :]).then_inc(bst, 1)
                    for j in range(SUB):
                        wait_apart(dve, (wld, 32), (bst, c * SUB + j + 1))
                        nc.vector.bn_aggr(mv[0:RT, j, :], st[0:RT, j, :]).then_inc(bag, 1)
                    dve.wait_ge(bag, c * SUB + SUB)
                    nc.vector.tensor_scalar_add(ve[0:RT, :], mv[0:RT, :, 1], EPS).then_inc(vpe, 1)
                    dve.wait_ge(rst, c + 1)
                    nc.vector.tensor_scalar(rse[0:RT, :], rs[0:RT, :], ope[0:RT, 0:1], None, ALU.mult).then_inc(rsd, 1)
                    dve.wait_ge(rsd, c + 1)
                    if not static(c, 1):
                        dve.wait_ge(tpr, c * KH)
                    for j in range(SUB):
                        nc.vector.tensor_scalar(ht[0:RT, j, :], xt[b][0:RT, j, :], mv[0:RT, j, 0:1], rse[0:RT, j:j + 1],
                                                ALU.subtract, ALU.mult).then_inc(nrm, 1)
                    for j in range(SUB):
                        dve.wait_ge(nrm, c * SUB + j + 1)
                        nc.vector.tensor_tensor(ht[0:RT, j, :], ht[0:RT, j, :], at[b][0:RT, j, :], ALU.add).then_inc(hrd, 1)

                def low(c, b):
                    if not static(c, 2):
                        dve.wait_ge(mmr, (c - 1) * KF)
                    for k in range(KH):
                        dve.wait_ge(hir, c * KH + k + 1)
                        nc.vector.tensor_tensor(hlo[b][:, k, :], tb[k][:, 0:CW], hhi[b][:, k, :].bitcast(F32),
                                                ALU.subtract).then_inc(lor, 1)

                def stats(c, b, m0, m1):
                    for m in range(m0, m1):
                        dve.wait_ge(evr, c * KF + m + 1)
                        nc.vector.bn_stats(stats1[:, m, bass.ds(c * 6, 6)], h1o[b][:, m, :]).then_inc(str_, 1)

                prepare(0, 0)
                low(0, 0)

                def body(c, b):
                    prepare(c, b)
                    stats(c - 1, 1 - b, 0, 4)
                    low(c, b)
                    stats(c - 1, 1 - b, 4, KF)

                chunks(dve, body)
                stats(NCH - 1, 1, 0, KF)
                dve.wait_ge(str_, NCH * KF)

            @block.scalar
            def _(act):
                act.wait_ge(wld, 32)

                def high(c, b):
                    if not static(c, 2):
                        act.wait_ge(mmr, (c - 1) * KF)
                    for k in range(KH):
                        act.wait_ge(tpr, c * KH + k + 1)
                        nc.scalar.activation(hhi[b][:, k, :], tb[k][:, 0:CW], ACT.Copy).then_inc(hir, 1)

                def evict(c, b, m0, m1):
                    if not static(c, 2) and m0 == 0:
                        if b == 0:
                            act.wait_ge(sto[0], (c // 2) * 16 if isinstance(c, int) else c * 8)
                        else:
                            act.wait_ge(sto[1], (c - 1) * 8)
                        act.wait_ge(str_, (c - 1) * KF)
                    for m in range(m0, m1):
                        act.wait_ge(mmr, c * KF + m + 1)
                        nc.scalar.activation(h1o[b][:, m, :], mb[m % 4][:, 0:CW], ACT.Identity,
                                             bias=b1c[:, m:m + 1]).then_inc(evr, 1)

                high(0, 0)

                def body(c, b):
                    evict(c - 1, 1 - b, 0, 4)
                    high(c, b)
                    evict(c - 1, 1 - b, 4, KF)

                chunks(act, body)
                evict(NCH - 1, 1, 0, KF)

            @block.tensor
            def _(pe):
                def turn(c, b):
                    pe.wait_ge(hrd, (c + 1) * SUB)
                    if not static(c, 1):
                        pe.wait_ge(lor, c * KH)
                    for k in range(KH):
                        for j in range(SUB):
                            last = nc.tensor.transpose(tb[k][:, j * RT:(j + 1) * RT], ht[0:RT, j, k * P:(k + 1) * P],
                                                       ident[0:RT, 0:RT])
                        last.then_inc(tpr, 1)

                def multiply(c, b, m0, m1):
                    if m0 == 0:
                        pe.wait_ge(lor, (c + 1) * KH)
                    for m in range(m0, m1):
                        if not (static(c, 1) and m < 4):
                            pe.wait_ge(evr, c * KF + m - 3)
                        product(nc, mb[m % 4][:, 0:CW], whi, wlo, hhi[b], hlo[b], KH, m).then_inc(mmr, 1)

                turn(0, 0)

                def body(c, b):
                    multiply(c - 1, 1 - b, 0, 4)
                    turn(c, b)
                    multiply(c - 1, 1 - b, 4, KF)

                chunks(pe, body)
                multiply(NCH - 1, 1, 0, KF)


def norm_constants(nc, dve, pool_root, gam, bet, stats, mv, ve, rs, sc, sh, sems, n, rows):
    agr, vpe, rst, scr, tmr, shr = sems
    for m in range(n):
        nc.vector.bn_aggr(mv[:, m, :], stats[:, m, :]).then_inc(agr, 1)
    dve.wait_ge(agr, n)
    nc.vector.tensor_scalar_add(ve[:, :], mv[:, :, 1], EPS).then_inc(vpe, 1)
    dve.wait_ge(rst, 1)
    nc.vector.tensor_tensor(sc[:, :], gam[:, :], rs[:, :], ALU.mult).then_inc(scr, 1)
    dve.wait_ge(scr, 1)
    nc.vector.tensor_tensor(rs[:, :], mv[:, :, 0], sc[:, :], ALU.mult).then_inc(tmr, 1)
    dve.wait_ge(tmr, 1)
    nc.vector.tensor_tensor(sh[:, :], bet[:, :], rs[:, :], ALU.subtract).then_inc(shr, 1)


def gnn_down(nc, sem, psum, mhalf, h1T, g1, beta1, w2, b2, h2T, stats1, stats2):
    with ExitStack() as ctx:
        def sb(name, shape, dt=F32):
            return ctx.enter_context(nc.sbuf_tensor(name, shape, dt))

        whi, wlo = w2["hi"], w2["lo"]
        b2c, gc, bc = sb("b2c", [P, KH]), sb("g1c", [P, KF]), sb("beta1c", [P, KF])
        mv, ve, rs = sb("mv1", [P, KF, 2]), sb("ve1", [P, KF]), sb("rs1", [P, KF])
        sc, sh = sb("scale1", [P, KF]), sb("shift1", [P, KF])
        h1 = [sb(f"h1in{i}", [P, KF, CW]) for i in range(2)]
        aw = sb("a_whole", [P, KF, CW])
        ahi = [sb(f"ahi{i}", [P, KF, CW], F32R) for i in range(2)]
        alo = [sb(f"alo{i}", [P, KF, CW], F32R) for i in range(2)]
        h2o = [sb(f"h2o{i}", [P, KH, CW]) for i in range(2)]

        wld = sem("norm1_loaded")
        nrm = [sem(n) for n in ("h1_agg", "h1_var_eps", "h1_rstd", "scale1_ready", "mean_scaled1", "shift1_ready")]
        ldh = [sem(f"h1_loaded{i}") for i in range(2)]
        sto = [sem(f"h2_stored{i}") for i in range(2)]
        awr, hir, lor = sem("a_ready"), sem("a_hi_ready"), sem("a_lo_ready")
        mmr, evr, str_ = sem("h2_psum"), sem("h2_evicted"), sem("h2_stats")

        def span(c):
            return bass.ds(c * CW, CW)

        def static(c, least):
            return isinstance(c, int) and c < least

        def chunks(eng, body):
            body(0, 0)
            body(1, 1)
            with eng.Fori(1, NCH // 2) as it:
                body(it * 2, 0)
                body(it * 2 + 1, 1)

        def half(c, b, of):
            return (c - b) * (of // 2) + of

        with nc.Block() as block:
            @block.sync
            def _(sp):
                with nc.allow_non_contiguous_dma(reason="vectors by channel"):
                    sp.dma_start(gc[:, :], g1.rearrange("(m p) -> p m", p=P)).then_inc(wld, 16)
                    sp.dma_start(bc[:, :], beta1.rearrange("(m p) -> p m", p=P)).then_inc(wld, 16)
                    sp.dma_start(b2c[:, :], b2.rearrange("(m p) -> p m", p=P)).then_inc(wld, 16)

                def load(c, b):
                    if not static(c, 2):
                        sp.wait_ge(hir, (c - 1) * KF)
                    sp.dma_start(h1[b][:, :, :], h1T[:, :, span(c)].rearrange("m p n -> p m n")).then_inc(ldh[b], 16)

                def store(c, b):
                    sp.wait_ge(evr, (c + 1) * KH)
                    sp.dma_start(h2T[:, :, span(c)].rearrange("m p n -> p m n"), h2o[b][:, :, :]).then_inc(sto[b], 16)

                load(0, 0)
                load(1, 1)
                with sp.Fori(0, NCH // 2 - 1) as it:
                    load(it * 2 + 2, 0)
                    store(it * 2, 0)
                    load(it * 2 + 3, 1)
                    store(it * 2 + 1, 1)
                store(NCH - 2, 0)
                store(NCH - 1, 1)
                for b in range(2):
                    sp.wait_ge(sto[b], 16 * (NCH // 2))

            @block.gpsimd
            def _(pool):
                pool.wait_ge(nrm[1], 1)
                nc.gpsimd.tensor_tensor(rs[:, :], ve[:, :], mhalf[:, 0:KF], ALU.pow).then_inc(nrm[2], 1)

            @block.vector
            def _(dve):
                dve.wait_ge(wld, 48)
                norm_constants(nc, dve, None, gc, bc, stats1, mv, ve, rs, sc, sh, nrm, KF, None)

                def low(c, b):
                    if not static(c, 2):
                        dve.wait_ge(mmr, (c - 1) * KH)
                    for k in range(KF):
                        dve.wait_ge(hir, c * KF + k + 1)
                        nc.vector.tensor_tensor(alo[b][:, k, :], aw[:, k, :], ahi[b][:, k, :].bitcast(F32),
                                                ALU.subtract).then_inc(lor, 1)

                def stats(c, b):
                    for m in range(KH):
                        dve.wait_ge(evr, c * KH + m + 1)
                        nc.vector.bn_stats(stats2[:, m, bass.ds(c * 6, 6)], h2o[b][:, m, :]).then_inc(str_, 1)

                low(0, 0)
                low(1, 1)
                stats(0, 0)
                with dve.Fori(1, NCH // 2) as it:
                    low(it * 2, 0)
                    stats(it * 2 - 1, 1)
                    low(it * 2 + 1, 1)
                    stats(it * 2, 0)
                stats(NCH - 1, 1)
                dve.wait_ge(str_, NCH * KH)

            @block.scalar
            def _(act):
                act.wait_ge(nrm[5], 1)
                act.wait_ge(wld, 48)

                def nonlinear(c, b):
                    act.wait_ge(ldh[b], half(c, b, 16))
                    if not static(c, 2):
                        act.wait_ge(mmr, (c - 1) * KH)
                    for k in range(KF):
                        if not static(c, 1):
                            act.wait_ge(lor, (c - 1) * KF + k + 1)
                        nc.scalar.activation(aw[:, k, :], h1[b][:, k, :], ACT.Silu, bias=sh[:, k:k + 1],
                                             scale=sc[:, k:k + 1]).then_inc(awr, 1)
                        act.wait_ge(awr, c * KF + k + 1)
                        nc.scalar.activation(ahi[b][:, k, :], aw[:, k, :], ACT.Copy).then_inc(hir, 1)

                def evict(c, b):
                    if not static(c, 2):
                        act.wait_ge(sto[b], half(c, b, 16) - 16)
                        act.wait_ge(str_, (c - 1) * KH)
                    for m in range(KH):
                        act.wait_ge(mmr, c * KH + m + 1)
                        nc.scalar.activation(h2o[b][:, m, :], psum[(4 * b + m)][:, 0:CW], ACT.Identity,
                                             bias=b2c[:, m:m + 1]).then_inc(evr, 1)

                nonlinear(0, 0)
                nonlinear(1, 1)
                evict(0, 0)
                with act.Fori(1, NCH // 2) as it:
                    nonlinear(it * 2, 0)
                    evict(it * 2 - 1, 1)
                    nonlinear(it * 2 + 1, 1)
                    evict(it * 2, 0)
                evict(NCH - 1, 1)

            @block.tensor
            def _(pe):
                def multiply(c, b):
                    pe.wait_ge(lor, (c + 1) * KF)
                    for m in range(KH):
                        if not static(c, 2):
                            pe.wait_ge(evr, (c - 2) * KH + m + 1)
                        product(nc, psum[4 * b + m][:, 0:CW], whi, wlo, ahi[b], alo[b], KF, m).then_inc(mmr, 1)

                chunks(pe, multiply)


def mixture(nc, sem, psum, ident, mhalf, x, h2T, x1d, g2, beta2, controller, f1, f2, out, stats2):
    with ExitStack() as ctx:
        def sb(name, shape, dt=F32):
            return ctx.enter_context(nc.sbuf_tensor(name, shape, dt))

        f1s = sb("f1s", [P, KH, ES * FF])
        f2s = sb("f2s", [P, NE, H])
        cts = sb("controller_s", [P, KH, ES])
        yT = sb("yT", [P, KH, ES, TB * GB])
        ibd = sb("inner_bd", [P, NE, TB, NS, GB])
        pT = sb("perm_T", [ES, TB, P], F32R)
        pn = [sb(f"perm_new{i}", [ES, P], F32R) for i in range(2)]
        gc, bc = sb("g2c", [P, KH]), sb("beta2c", [P, KH])
        mv2, ve2, rs2 = sb("mv2", [P, KH, 2]), sb("ve2", [P, KH]), sb("rs2", [P, KH])
        sc, sh = sb("scale2", [P, KH]), sb("shift2", [P, KH])
        h2 = [sb(f"h2in{i}", [P, KH, 2 * P]) for i in range(2)]
        gT = sb("gT", [P, KH, 2 * P])
        x1 = [sb(f"x1_{i}", [P, H]) for i in range(2)]
        st, mv = sb("st2", [P, 6]), sb("mvx", [P, 2])
        ve, rs = sb("vex", [P, 1]), sb("rsx", [P, 1])
        xn = sb("xn2", [P, H])
        xhi = [sb(f"xn2_hi{i}", [P, H], F32R) for i in range(2)]
        xlo = [sb(f"xn2_lo{i}", [P, H], F32R) for i in range(2)]
        xT = sb("xn2_T", [P, KH, P])
        lg, mx = sb("logits", [ES, P]), sb("logits_max", [ES, GB])
        tie = sb("tie", [ES, GT])
        pbd = sb("perm_bd", [P, ES, GB], F32R)
        rbd = [sb(f"back_bd{i}", [P, QB, P], F32R) for i in range(2)]
        ihi = [sb(f"inter_hi{i}", [P, H], F32R) for i in range(UB)]
        ilo = [sb(f"inter_lo{i}", [P, H], F32R) for i in range(UB)]
        x1b = [sb(f"x1_back{i}", [P, H]) for i in range(2)]
        rep = sb("rep", [ES, QB * P], F32R)
        repf = x1b[0][0:ES, :]
        pidx, pq = sb("pidx", [P, 1], I32), sb("pq", [P, 2], I32)
        pqf = sb("pqf", [P, 2])
        gid, tgid = sb("gid", [P, GB]), x1b[1][:, 0:P]
        mtg, mrt = sb("mask_token_group", [P, GB]), sb("mask_row_token", [P, P])

        bA, bB, bD, bF = psum[0], psum[1], psum[3:5], psum[7]
        bI = [psum[2], psum[5], psum[6]]
        bL, bP = bB[0:ES, 0:P], bB[:, 0:ES]

        wld, wctl, wf1, wf2 = sem("norm2_loaded"), sem("controller_loaded"), sem("f1_loaded"), sem("f2_loaded")
        nrm = [sem(n) for n in ("h2_agg", "h2_var_eps", "h2_rstd", "scale2_ready", "mean_scaled2", "shift2_ready")]
        cst, cstv = sem("ffn_const"), sem("ffn_const_v")
        ldh = [sem(f"h2_loaded{i}") for i in range(2)]
        ldx = [sem(f"x_loaded{i}") for i in range(2)]
        x1s = [sem(f"x1_stored{i}") for i in range(2)]
        ldb = [sem(f"x1_back_loaded{i}") for i in range(2)]
        ots = [sem(f"out_stored{i}") for i in range(2)]
        gr, t1, x1r = sem("g_ready"), sem("g_transposed"), sem("x1_ready")
        bst, bag, vpe, rst = sem("x1_stats"), sem("x1_meanvar"), sem("x1_var_eps"), sem("x1_rstd")
        xnr, xhr, xlr, t2, xTr = sem("xn2_ready"), sem("xn2_hi_r"), sem("xn2_lo_r"), sem("xn2_transposed"), sem("xn2T_ready")
        pnr = sem("perm_new_ready")
        lgp, lgr, mxr, pTr = sem("logits_psum"), sem("logits_ready"), sem("max_ready"), sem("permT_ready")
        ptp, pbr, yp, yr = sem("perm_transposed"), sem("perm_bd_ready"), sem("y_psum"), sem("y_ready")
        inp, inv, ina = sem("inner_psum"), sem("inner_ready_v"), sem("inner_ready_a")
        rp, rr, ip, ihr, ilr = sem("r_psum"), sem("r_ready"), sem("inter_psum"), sem("inter_hi_r"), sem("inter_lo_r")
        fp, otr = sem("final_psum"), sem("out_ready")

        def static(c, least):
            return isinstance(c, int) and c < least

        def row(k, j):
            if isinstance(k, int) and k * TB + j >= (NB - 1) * TB:
                return N - BW + (k - (NB - 1)) * BW + j * P
            return k * BW + j * P

        def by2(t, par, of):
            return (t - par) * (of // 2) + of

        def blocks(eng, body):
            body(0, None)
            body(1, 0)
            with eng.Fori(2, NB - 2) as k:
                body(k, k - 1)
            body(NB - 2, NB - 3)
            body(NB - 1, NB - 2)
            body(None, NB - 1)

        STEPS = TB + 1
        UNITS = TB * QB

        def exists(k, j):
            return k is not None and not (isinstance(k, int) and k == NB - 1 and j >= TB)

        def schedule(front, back):
            if front is not None and static(front, 1):
                yield "turn_g", 0
                yield "turn_x", 0
            given = 0
            for m in range(STEPS):
                goal = min(QB * (m + 1) - 2, UNITS)
                units = list(range(given, goal)) if back is not None else []
                given = goal
                if m == 0:
                    units = [None, *units]
                slots = [[u] if u is not None else [] for u in units] + [[]] * (QB - len(units))
                new = m < TB and exists(front, m + 1)
                if new:
                    yield "turn_g", m + 1
                if back is not None and m >= 2:
                    yield "result", m - 2
                if front is not None and m < TB:
                    yield "select", m
                if front is not None and m >= 1:
                    yield "sum_a", m - 1
                for u in slots[0] + slots[1]:
                    yield "unit", u
                if new:
                    yield "turn_x", m + 1
                if back is not None and m < TB:
                    yield "rows", m
                if front is not None and m >= 1:
                    yield "sum_b", m - 1
                for u in slots[2]:
                    yield "unit", u
                if front is not None and m < TB:
                    yield "spread", m
                for u in slots[3]:
                    yield "unit", u
            if front is not None:
                yield "inner", 0
            if back is not None:
                yield "ends", UNITS
            if front is not None:
                yield "inner", 1

        def relu(op, h, s, *more):
            return op(ibd[32 * s:32 * s + 32, 8 * h:8 * h + 8, :, s, :],
                      bD[h][32 * s:32 * s + 32, :].rearrange("p (e j g) -> p e j g", e=8, g=GB), *more)

        def unit_of(kb, u):
            return kb * UNITS + u

        def freed(kb, u):
            if u >= UB:
                return unit_of(kb, u - UB) + 1
            if static(kb, 1):
                return 0
            return (kb - 1) * UNITS + max(v for v in range(UNITS) if v % UB == u % UB) + 1

        with nc.Block() as block:
            @block.sync
            def _(sp):
                with nc.allow_non_contiguous_dma(reason="vectors by channel"):
                    sp.dma_start(gc[:, :], g2.rearrange("(m p) -> p m", p=P)).then_inc(wld, 16)
                    sp.dma_start(bc[:, :], beta2.rearrange("(m p) -> p m", p=P)).then_inc(wld, 16)
                    sp.dma_start(cts[:, :, :], controller.rearrange("(k p) e s -> p k (e s)", p=P)).then_inc(wctl, 16)

                def load_h(k, p):
                    pair = k * (TB // 2) + p
                    if not static(pair, 2):
                        sp.wait_ge(gr, (pair - 1) * KH)
                    sp.dma_start(h2[p % 2][:, :, :], h2T[:, :, bass.ds(row(k, 2 * p), 2 * P)].rearrange("m p n -> p m n"))\
                        .then_inc(ldh[p % 2], 16)

                def load_x(k, j):
                    t = k * TB + j
                    if not static(t, 2):
                        wait_apart(sp, (wld, 32), (xnr, t - 1), (x1s[j % 2], by2(t, j % 2, 16) - 16))
                    sp.dma_start(x1[j % 2][:, :], x[bass.ds(row(k, j), P), :]).then_inc(ldx[j % 2], 16)

                def store_x1(k, j):
                    t = k * TB + j
                    sp.wait_ge(x1r, t + 1)
                    sp.dma_start(x1d[bass.ds(t * P, P), :], x1[j % 2][:, :]).then_inc(x1s[j % 2], 16)

                def load_back(kb, j):
                    t = kb * TB + j
                    sp.wait_ge(x1s[j % 2], by2(t, j % 2, 16))
                    if not static(t, 2):
                        sp.wait_ge(ots[j % 2], by2(t, j % 2, 16) - 16)
                    sp.dma_start(x1b[j % 2][:, :], x1d[bass.ds(t * P, P), :]).then_inc(ldb[j % 2], 16)

                def store_out(kb, j):
                    t = kb * TB + j
                    sp.wait_ge(otr, t + 1)
                    sp.dma_start(out[bass.ds(row(kb, j), P), :], x1b[j % 2][:, :]).then_inc(ots[j % 2], 16)

                def body(k, kb):
                    if static(k, 1):
                        load_h(k, 0)
                        load_x(k, 0)
                        load_x(k, 1)
                        load_h(k, 1)
                        sp.dma_start(f1s[:, :, :], f1.rearrange("(k p) e s f -> p k (e s f)", p=P)).then_inc(wf1, 16)
                        sp.dma_start(f2s[:, :, :], f2.rearrange("e s f d -> (s f) e d")).then_inc(wf2, 16)
                    if kb is not None and not static(kb, 1):
                        store_out(kb - 1, TB - 1)
                    if k is None:
                        for b in range(2):
                            sp.wait_ge(ots[b], 16 * (TB // 2) * (NB - 1))
                    for what, n in schedule(k, kb):
                        if what == "turn_g":
                            store_x1(k, n)
                            if n >= 1 and exists(k, n + 1):
                                load_x(k, n + 1)
                            if n % 2 and exists(k, n + 3):
                                load_h(k, n // 2 + 2)
                        if what == "result":
                            store_out(kb, n)
                        if what == "rows":
                            load_back(kb, n)
                    if k is None:
                        store_out(kb, TB - 1)

                blocks(sp, body)
                for b in range(2):
                    sp.wait_ge(ots[b], 16 * (TB // 2) * NB)

            @block.gpsimd
            def _(pool):
                nc.gpsimd.iota(pidx[:, :], pattern=[[0, 1]], base=0, channel_multiplier=1).then_inc(cst, 1)
                nc.gpsimd.iota(gid[:, :], pattern=[[1, GB]], base=0, channel_multiplier=0,
                               allow_small_or_imprecise_dtypes=True).then_inc(cst, 1)
                nc.gpsimd.iota(tgid[:, :], pattern=[[1, GB], [0, GT]], base=0, channel_multiplier=0,
                               allow_small_or_imprecise_dtypes=True).then_inc(cst, 1)
                pool.wait_ge(cst, 3)
                pool.wait_ge(cstv, 1)
                nc.gpsimd.affine_select(out=repf[:, :], in_=repf[:, :], compare_op=ALU.is_ge, fill=0.0, base=0,
                                        pattern=[[1, QB * P]], channel_multiplier=-GB).then_inc(cst, 1)
                pool.wait_ge(cst, 4)
                nc.gpsimd.affine_select(out=repf[:, :], in_=repf[:, :], compare_op=ALU.is_ge, fill=0.0, base=GB - 1,
                                        pattern=[[-1, QB * P]], channel_multiplier=GB).then_inc(cst, 1)
                pool.wait_ge(nrm[1], 1)
                nc.gpsimd.tensor_tensor(rs2[:, :], ve2[:, :], mhalf[:, 0:KH], ALU.pow).then_inc(nrm[2], 1)

                def keep(k, j):
                    t = k * TB + j
                    free = [] if static(k, 1) else [(rp, t - TB + 1)]
                    wait_apart(pool, (cst, 5), (pnr, t + 1), *free)
                    nc.gpsimd.tensor_copy(pT[:, j, :], pn[j % 2][:, :].bitcast(F32)).then_inc(pTr, 1)

                def body(k, kb):
                    for what, n in schedule(k, kb):
                        if what == "turn_g":
                            t = k * TB + n
                            pool.wait_ge(vpe, t + 1)
                            nc.gpsimd.tensor_tensor(rs[:, :], ve[:, :], mhalf[:, 0:1], ALU.pow).then_inc(rst, 1)
                            free = [] if static(t, 2) else [(yp, (t - 1) * KH)]
                            wait_apart(pool, (cst, 5), (xnr, t + 1), *free)
                            nc.gpsimd.tensor_copy(xhi[n % 2][:, :], xn[:, :]).then_inc(xhr, 1)
                            pool.wait_ge(xhr, t + 1)
                            nc.gpsimd.tensor_tensor(xlo[n % 2][:, :], xn[:, :], xhi[n % 2][:, :].bitcast(F32),
                                                    ALU.subtract).then_inc(xlr, 1)

                        if what == "spread":
                            keep(k, n)

                blocks(pool, body)

            @block.vector
            def _(dve):
                nc.vector.memset(repf[:, :], 1.0).then_inc(cstv, 1)
                nc.vector.memset(ibd[:, :, :, :, :], 0.0).then_inc(cstv, 1)
                for t in range(GT):
                    nc.vector.memset(tie[:, t:t + 1], float(np.linspace(0.0, 1e-6, GT, dtype=np.float32)[t])).then_inc(cstv, 1)
                dve.wait_ge(wld, 32)
                norm_constants(nc, dve, None, gc, bc, stats2, mv2, ve2, rs2, sc, sh, nrm, KH, None)
                dve.wait_ge(cst, 5)
                nc.vector.tensor_copy(rep[:, :], repf[:, :]).then_inc(cstv, 1)
                nc.vector.tensor_scalar(pq[:, 0:1], pidx[:, :], 4, None, ALU.logical_shift_right).then_inc(cstv, 1)
                nc.vector.tensor_scalar(pq[:, 1:2], pidx[:, :], GB - 1, None, ALU.bitwise_and).then_inc(cstv, 1)
                dve.wait_ge(cstv, GT + 5)
                nc.vector.tensor_copy(pqf[:, :], pq[:, :]).then_inc(cstv, 1)
                dve.wait_ge(cstv, GT + 6)
                nc.vector.tensor_scalar(mtg[:, :], gid[:, :], pqf[:, 0:1], None, ALU.is_equal).then_inc(cstv, 1)
                nc.vector.tensor_scalar(mrt[:, :], tgid[:, :], pqf[:, 1:2], None, ALU.is_equal).then_inc(cstv, 1)
                dve.wait_ge(cstv, GT + 8)

                def new_tile(k, j):
                    t = k * TB + j
                    dve.wait_ge(t1, t + 1)
                    dve.wait_ge(ldx[j % 2], by2(t, j % 2, 16))
                    nc.vector.tensor_tensor(x1[j % 2][:, :], x1[j % 2][:, :], bA[:, :], ALU.add).then_inc(x1r, 1)
                    dve.wait_ge(x1r, t + 1)
                    nc.vector.bn_stats(st[:, :], x1[j % 2][:, :]).then_inc(bst, 1)
                    wait_apart(dve, (cstv, GT + 8), (bst, t + 1))
                    nc.vector.bn_aggr(mv[:, :], st[:, :]).then_inc(bag, 1)
                    dve.wait_ge(bag, t + 1)
                    nc.vector.tensor_scalar_add(ve[:, :], mv[:, 1:2], EPS).then_inc(vpe, 1)

                def normalize(k, j):
                    t = k * TB + j
                    dve.wait_ge(rst, t + 1)
                    if not static(t, 1):
                        dve.wait_ge(t2, t)
                        dve.wait_ge(xlr, t)
                    nc.vector.tensor_scalar(xn[:, :], x1[j % 2][:, :], mv[:, 0:1], rs[:, 0:1],
                                            ALU.subtract, ALU.mult).then_inc(xnr, 1)

                def select(k, j):
                    t = k * TB + j
                    dve.wait_ge(lgp, t + 1)
                    lg3 = lg[:, :].rearrange("p (g t) -> p g t", t=GT)
                    nc.vector.tensor_tensor(lg3, bL.rearrange("p (g t) -> p g t", t=GT),
                                            tie[:, :].unsqueeze(1).to_broadcast([ES, GB, GT]), ALU.add).then_inc(lgr, 1)
                    dve.wait_ge(lgr, t + 1)
                    nc.vector.tensor_reduce(mx[:, :], lg3, AX.X, ALU.max).then_inc(mxr, 1)
                    dve.wait_ge(mxr, t + 1)
                    if not static(t, 2):
                        dve.wait_ge(pTr, t - 1)
                        dve.wait_ge(ptp, t - 1)
                    nc.vector.tensor_tensor(pn[j % 2][:, :].rearrange("p (g t) -> p g t", t=GT), lg3,
                                            mx[:, :].unsqueeze(2).to_broadcast([ES, GB, GT]), ALU.is_equal).then_inc(pnr, 1)

                def spread(k, j):
                    t = k * TB + j
                    dve.wait_ge(ptp, t + 1)
                    if not static(t, 1):
                        dve.wait_ge(yp, t * KH)
                    nc.vector.tensor_tensor(pbd[:, :, :], bP.unsqueeze(2).to_broadcast([P, ES, GB]),
                                            mtg[:, :].unsqueeze(1).to_broadcast([P, ES, GB]), ALU.mult).then_inc(pbr, 1)

                def back_rows(kb, j):
                    t = kb * TB + j
                    dve.wait_ge(rp, t + 1)
                    if not static(t, 2):
                        dve.wait_ge(fp, (t - 1) * QB)
                    nc.vector.tensor_tensor(rbd[j % 2][:, :, :], bA[:, :].rearrange("p (b t) -> p b t", t=P),
                                            mrt[:, :].unsqueeze(1).to_broadcast([P, QB, P]), ALU.mult).then_inc(rr, 1)

                def inter_low(kb, u):
                    q = unit_of(kb, u)
                    dve.wait_ge(ihr, q + 1)
                    if not static(freed(kb, u), 1):
                        dve.wait_ge(fp, freed(kb, u))
                    nc.vector.tensor_tensor(ilo[u % UB][:, :], bI[u % UB][:, :], ihi[u % UB][:, :].bitcast(F32),
                                            ALU.subtract).then_inc(ilr, 1)

                def result(kb, j):
                    t = kb * TB + j
                    dve.wait_ge(fp, (t + 1) * QB)
                    dve.wait_ge(ldb[j % 2], by2(t, j % 2, 16))
                    nc.vector.tensor_tensor(x1b[j % 2][:, :], bF[:, :], x1b[j % 2][:, :], ALU.add).then_inc(otr, 1)

                def body(k, kb):
                    for what, n in schedule(k, kb):
                        if what == "turn_g":
                            new_tile(k, n)
                            if n == 0:
                                normalize(k, n)
                        if what == "select":
                            select(k, n)
                            if exists(k, n + 1):
                                normalize(k, n + 1)
                        if what == "spread":
                            spread(k, n)
                        if what == "unit":
                            inter_low(kb, n)
                        if what == "result":
                            result(kb, n)
                        if what == "rows":
                            back_rows(kb, n)
                        if what == "inner":
                            dve.wait_ge(inp, k * 2 + n + 1)
                            for s in range(0, NS, 2):
                                relu(nc.vector.tensor_scalar_max, n, s, 0.0).then_inc(inv, 1)
                        if what == "ends":
                            result(kb, TB - 1)

                blocks(dve, body)

            @block.scalar
            def _(act):
                act.wait_ge(nrm[5], 1)

                def nonlinear(k, p, chunks):
                    pair = k * (TB // 2) + p
                    if chunks[0] == 0:
                        act.wait_ge(ldh[p % 2], by2(pair, p % 2, 16))
                        if not static(pair, 1):
                            act.wait_ge(t1, pair * 2)
                    for c in chunks:
                        nc.scalar.activation(gT[:, c, :], h2[p % 2][:, c, :], ACT.Silu, bias=sh[:, c:c + 1],
                                             scale=sc[:, c:c + 1]).then_inc(gr, 1)

                def to_yT(k, j, c):
                    t = k * TB + j
                    act.wait_ge(yp, t * KH + c + 1)
                    nc.scalar.activation(yT[:, c, :, j * GB:(j + 1) * GB],
                                         bD[c % 2][:, :].rearrange("p (e g) -> p e g", g=GB), ACT.Copy).then_inc(yr, 1)

                def body(k, kb):
                    if static(k, 1):
                        nonlinear(k, 0, range(KH))
                    chunk = KH
                    for what, n in schedule(k, kb):
                        if what == "turn_g" and n % 2 and exists(k, n + 1):
                            pair, chunk = n // 2 + 1, 0
                        elif chunk < KH and what in ("select", "sum_b", "unit"):
                            nonlinear(k, pair, [chunk])
                            chunk += 1
                        elif chunk < KH and what == "spread":
                            nonlinear(k, pair, range(chunk, KH))
                            chunk = KH
                        if what == "sum_a":
                            if n == 0 and not static(k, 1):
                                act.wait_ge(inp, k * 2)
                            to_yT(k, n, 0)
                            to_yT(k, n, 1)
                        if what == "sum_b":
                            to_yT(k, n, 2)
                            to_yT(k, n, 3)
                        if what == "unit":
                            q = unit_of(kb, n)
                            act.wait_ge(ip, q + 1)
                            if not static(freed(kb, n), 1):
                                act.wait_ge(fp, freed(kb, n))
                            nc.scalar.activation(ihi[n % UB][:, :], bI[n % UB][:, :], ACT.Copy).then_inc(ihr, 1)
                        if what == "turn_x":
                            t = k * TB + n
                            act.wait_ge(t2, t + 1)
                            if not static(t, 1):
                                act.wait_ge(lgp, t)
                            nc.scalar.activation(xT[:, :, :], bB[:, :].rearrange("p (k n) -> p k n", n=P),
                                                 ACT.Copy).then_inc(xTr, 1)
                        if what == "inner":
                            act.wait_ge(inp, k * 2 + n + 1)
                            for s in range(1, NS, 2):
                                relu(nc.scalar.activation, n, s, ACT.Relu).then_inc(ina, 1)

                blocks(act, body)

            @block.tensor
            def _(pe):
                pe.wait_ge(cstv, GT + 8)

                def turn_g(k, kb, j, rowed):
                    t = k * TB + j
                    pe.wait_ge(gr, (k * (TB // 2) + j // 2 + 1) * KH)
                    if not static(t, 1):
                        pe.wait_ge(x1r, t)
                    if kb is not None and not (static(kb, 1) and rowed == 0):
                        pe.wait_ge(rr, kb * TB + rowed)
                    for c in range(KH):
                        last = nc.tensor.transpose(bA[:, c * P:(c + 1) * P],
                                                   gT[:, c, (j % 2) * P:(j % 2 + 1) * P], ident[:, :])
                    last.then_inc(t1, 1)

                def turn_x(k, j):
                    t = k * TB + j
                    pe.wait_ge(xnr, t + 1)
                    if not static(t, 1):
                        pe.wait_ge(lgr, t)
                    for c in range(KH):
                        last = nc.tensor.transpose(bB[:, c * P:(c + 1) * P], xn[:, c * P:(c + 1) * P], ident[:, :])
                    last.then_inc(t2, 1)

                def logits(k, j):
                    t = k * TB + j
                    pe.wait_ge(xTr, t + 1)
                    if static(t, 1):
                        pe.wait_ge(wctl, 16)
                    else:
                        pe.wait_ge(pbr, t)
                    for c in range(KH):
                        last = nc.tensor.matmul(bL, cts[:, c, :], xT[:, c, :], start=(c == 0), stop=(c == KH - 1))
                    last.then_inc(lgp, 1)

                def turn_p(k, j):
                    t = k * TB + j
                    turned = t + 2 if exists(k, j + 1) else t + 1
                    wait_apart(pe, (cstv, GT + 8), (pnr, t + 1), (xTr, turned))
                    nc.tensor.transpose(bP, pn[j % 2][:, :].bitcast(F32), ident[0:ES, 0:ES]).then_inc(ptp, 1)

                def sums(k, j, chunks):
                    t = k * TB + j
                    if chunks[0] == 0:
                        pe.wait_ge(pbr, t + 1)
                        pe.wait_ge(xlr, t + 1)
                        if j == 0 and not static(k, 1):
                            pe.wait_ge(inv, k * NS)
                            pe.wait_ge(ina, k * NS)
                    for c in chunks:
                        q = t * KH + c
                        if not static(q, 2):
                            pe.wait_ge(yr, q - 1)
                        o = bD[c % 2][:, :]
                        r = pbd[:, :, :].rearrange("p e g -> p (e g)")
                        nc.tensor.matmul(o, xhi[j % 2][:, c * P:(c + 1) * P], r, start=True, stop=False)
                        nc.tensor.matmul(o, xlo[j % 2][:, c * P:(c + 1) * P], r, start=False, stop=True).then_inc(yp, 1)

                def rows(k, kb, j, turned):
                    if k is not None:
                        pe.wait_ge(x1r, k * TB + turned)
                    if not static(kb * TB + j, 1):
                        pe.wait_ge(rr, kb * TB + j)
                    pe.wait_ge(pTr, kb * TB + j + 1)
                    for b in range(QB):
                        last = nc.tensor.matmul(bA[:, b * P:(b + 1) * P], rep[:, b * P:(b + 1) * P], pT[:, j, :],
                                                start=True, stop=True)
                    last.then_inc(rp, 1)

                def inter(kb, u):
                    j, b, q = u // QB, u % QB, unit_of(kb, u)
                    if static(kb, 1) and u == 0:
                        pe.wait_ge(wf2, 16)
                    if j == 0 and b % 2 == 0:
                        pe.wait_ge(inv, kb * NS + b + 2)
                        pe.wait_ge(ina, kb * NS + b + 2)
                    if not static(freed(kb, u), 1):
                        pe.wait_ge(ilr, freed(kb, u))
                    for i in range(NS):
                        e = 4 * b + i
                        last = nc.tensor.matmul(bI[u % UB][32 * i:32 * i + 32, :],
                                                ibd[:, e, j, :, :].rearrange("p s g -> p (s g)"), f2s[:, e, :],
                                                start=True, stop=True)
                    last.then_inc(ip, 1)

                def final(kb, u):
                    j, b, q = u // QB, u % QB, unit_of(kb, u)
                    if b == 0:
                        pe.wait_ge(rr, kb * TB + j + 1)
                        if not static(kb * TB + j, 1):
                            pe.wait_ge(otr, kb * TB + j)
                    pe.wait_ge(ilr, q + 1)
                    nc.tensor.matmul(bF[:, :], rbd[j % 2][:, b, :], ihi[u % UB][:, :], start=(b == 0), stop=False)
                    nc.tensor.matmul(bF[:, :], rbd[j % 2][:, b, :], ilo[u % UB][:, :], start=False, stop=(b == QB - 1))\
                        .then_inc(fp, 1)

                def inner(k, h):
                    if static(k, 1):
                        pe.wait_ge(wf1, 16)
                    if h == 0:
                        pe.wait_ge(yr, (k + 1) * TB * KH)
                    for e in range(8 * h, 8 * h + 8):
                        for c in range(KH):
                            for s in range(NS):
                                es = e * NS + s
                                last = nc.tensor.matmul(
                                    bD[h][32 * s:32 * s + 32, (e % 8) * 64:(e % 8) * 64 + 64],
                                    f1s[:, c, es * FF:(es + 1) * FF], yT[:, c, es, :],
                                    start=(c == 0), stop=(c == KH - 1))
                    last.then_inc(inp, 1)

                def body(k, kb):
                    turned, rowed = (0 if static(k, 1) else 1), 0
                    for what, n in schedule(k, kb):
                        if what == "turn_g":
                            turn_g(k, kb, n, rowed)
                            turned += 1
                        if what == "select":
                            logits(k, n)
                        if what == "sum_a":
                            sums(k, n, (0, 1))
                        if what == "sum_b":
                            sums(k, n, (2, 3))
                        if what == "turn_x":
                            turn_x(k, n)
                        if what == "spread":
                            turn_p(k, n)
                        if what == "rows":
                            rows(k, kb, n, turned)
                            rowed += 1
                        if what == "unit":
                            inter(kb, n)
                            if n >= 2:
                                final(kb, n - 2)
                        if what == "ends":
                            final(kb, n - 2)
                            final(kb, n - 1)
                        if what == "inner":
                            inner(k, n)

                blocks(pe, body)


def gnn_mixture(nc, x, src, dst, edge_attr, W_e, b_e, W1, b1, g1, beta1, W2, b2, g2, beta2, eps,
                controller, f1, f2, out):
    agg = nc.dram_tensor("aggregate", [N + TRASH, H], F32, kind="Internal").ap()
    h1T = nc.dram_tensor("h1T", [KF, P, N], F32, kind="Internal").ap()
    h2T = nc.dram_tensor("h2T", [KH, P, N], F32, kind="Internal").ap()
    x1d = nc.dram_tensor("x1", [NB * BW, H], F32, kind="Internal").ap()
    with ExitStack() as ctx:
        psum = [ctx.enter_context(nc.psum_tensor(f"bank{i}", [P, 512], F32)) for i in range(8)]
        ident = ctx.enter_context(nc.sbuf_tensor("ident", [P, P], F32))
        mhalf = ctx.enter_context(nc.sbuf_tensor("mhalf", [P, KF], F32))
        stats2 = ctx.enter_context(nc.sbuf_tensor("stats2", [P, KH, NCH * 6], F32))

        def sem(name):
            return ctx.enter_context(nc.semaphore(name))

        identity = sem("identity_ready")
        with nc.Block() as block:
            @block.gpsimd
            def _(pool):
                nc.gpsimd.memset(ident[:, :], 0.0).then_inc(identity, 1)
                pool.wait_ge(identity, 1)
                nc.gpsimd.affine_select(out=ident[:, :], in_=ident[:, :], compare_op=ALU.not_equal, fill=1.0,
                                        base=0, pattern=[[-1, P]], channel_multiplier=1).then_inc(identity, 1)
                pool.wait_ge(identity, 2)
                nc.gpsimd.memset(mhalf[:, :], -0.5).then_inc(identity, 1)
                pool.wait_ge(identity, 3)

            @block.tensor
            def _(pe):
                pe.wait_ge(identity, 3)

        with nc.sbuf_tensor("stats1", [P, KF, NCH * 6], F32) as stats1, ExitStack() as second:
            def split_buffers(ctx, name, chunks, width):
                return {part: ctx.enter_context(nc.sbuf_tensor(f"{name}_{part}", [P, chunks, width], F32R))
                        for part in ("hi", "lo")}

            w2 = split_buffers(second, "w2", KF, H)
            with ExitStack() as first:
                w1 = split_buffers(first, "w1", KH, F)
                whole = first.enter_context(nc.sbuf_tensor("weight_whole", [P, KH * F], F32))
                w1["whole"] = whole[:, :].rearrange("p (k n) -> p k n", k=KH)
                w2["whole"] = whole[:, :].rearrange("p (k n) -> p k n", k=KF)
                edge_aggregate(nc, sem, psum, ident, x, src, dst, edge_attr, W_e, b_e, agg, W1, w1)
                gnn_up(nc, sem, psum, ident, mhalf, x, agg, w1, b1, eps, h1T, stats1, W2, w2)
            gnn_down(nc, sem, psum, mhalf, h1T, g1, beta1, w2, b2, h2T, stats1, stats2)
        mixture(nc, sem, psum, ident, mhalf, x, h2T, x1d, g2, beta2, controller, f1, f2, out, stats2)


_INS = ["x", "src", "dst", "edge_attr_64", "L0_gnn_W_e", "L0_gnn_b_e", "L0_gnn_W1", "L0_gnn_b1", "L0_gnn_g1",
        "L0_gnn_beta1", "L0_gnn_W2", "L0_gnn_b2", "L0_gnn_g2", "L0_gnn_beta2", "L0_gnn_eps", "L0_ffn_controller",
        "L0_ffn_f1", "L0_ffn_f2"]


def kernel(**inputs):
    import concourse.bacc as _bacc
    from concourse.bass_utils import run_bass_kernel_spmd as _run

    nc = _bacc.Bacc("TRN2", target_bir_lowering=False, num_devices=1)
    arrays, args = {}, []
    for name in _INS:
        a = np.ascontiguousarray(inputs[name])
        if a.ndim == 0:
            a = a.reshape(1)
        arrays[f"in_{name}"] = a
        args.append(nc.dram_tensor(f"in_{name}", a.shape, mybir.dt.from_np(a.dtype), kind="ExternalInput").ap())
    args.append(nc.dram_tensor("out_0", (N, H), F32, kind="ExternalOutput").ap())
    gnn_mixture(nc, *args)
    r = _run(nc, [arrays], core_ids=[0])
    return r.results[0]["out_0"]
```

```python
import numpy as np
import concourse.bass as bass
from concourse import mybir
from contextlib import ExitStack

F32 = mybir.dt.float32
F32R = mybir.dt.float32r
I32 = mybir.dt.int32
ALU = mybir.AluOpType
ACT = mybir.ActivationFunctionType
AX = mybir.AxisListType

N, H = 10000, 512
E, ED = 5000, 64
P = 128
KH = H // P
F = 2 * H
KF = F // P
EPS = 1e-5
PAIRS = -(-E // (2 * P))
ER = E - (PAIRS * 2 - 1) * P
PU = 4
ROOTS = 3
ZQ = 3
TRASH = 2 * P
CW = 500
NCH = N // CW
SUB = 4
RT = CW // SUB
GT = 16
NE, NS, FF = 16, 4, 32
ES = NE * NS
GB = P // GT
TB = 8
BW = TB * P
NB = -(-N // BW)
F2P = 4
QB = ES // GT
UB = 3


def wait_apart(eng, met, *waits):
    found = [(sem, value if isinstance(value, int) else eng.to_reg(value)) for sem, value in waits]
    eng.wait_ge(*met)
    for sem, value in found:
        eng.wait_ge(sem, value)


def edge_aggregate(nc, sem, psum, ident, x, src, dst, edge_attr, W_e, b_e, agg, W1, w1, vectors, vec):
    with ExitStack() as ctx:
        def sb(name, shape, dt=F32):
            return ctx.enter_context(nc.sbuf_tensor(name, shape, dt))

        def buffers(name, shape, dt=F32, n=PU):
            return [sb(f"{name}{i}", shape, dt) for i in range(n)]

        zeros = sb("zeros", [P, 2048])
        web = sb("web", [ED + 1, H])
        before = sb("before", [P, 2, 2 * P])
        trash = sb("trash", [P, 2])
        mhalf = sb("mhalf_e", [P, 2])
        eaT = sb("eaT", [ED + 1, PU, 2 * P])
        dcol, scol = buffers("dcol", [P, 2], I32, PU + 1), buffers("scol", [P, 2], I32, PU + 1)
        drow, ea = buffers("drow", [P, 2 * P], I32, PU + 1), buffers("ea", [P, 2, ED], F32, PU + 1)
        xg = buffers("xg", [P, 2, H])
        dcolf, cnt, away = buffers("dcolf", [P, 2]), buffers("cnt", [P, 2]), buffers("away", [P, 2])
        sel, scr = buffers("sel", [P, 2, 2 * P]), sb("scr", [P, 2, 2 * P])
        idx = buffers("idx", [P, 2], I32)
        st, mv = buffers("est", [P, 2, 6]), buffers("emv", [P, 2, 2])
        ve, rs, nb = buffers("eve", [P, 2]), buffers("ers", [P, 2]), buffers("enb", [P, 2])
        xn, pre = buffers("exn", [P, 2, H]), buffers("pre", [P, 2, H])
        msg, comb = buffers("msg", [P, 2, H]), buffers("comb", [P, 2, H])
        tp, emb, cps = psum[0:2], psum[2:6], psum[6:8]

        wld, const = sem("edge_w_loaded"), sem("edge_const")
        zeroed = [sem(f"zeroed{i}") for i in range(ZQ)]
        vld = sem("vectors_loaded")
        w1ld, w1h, w1l = sem("w1_loaded"), sem("w1_hi_done"), sem("w1_lo_done")
        ld = [sem(f"edge_loaded{i}") for i in range(PU + 1)]
        gat = [sem(f"rows_gathered{i}") for i in range(PU)]
        sca = sem("rows_added")
        dcf, sl, ct, aw, ix = sem("dstf"), sem("sel_ready"), sem("cnt_ready"), sem("away_ready"), sem("idx_ready")
        bst, bag, vpe, rst, nbr = sem("estats"), sem("emeanvar"), sem("evar_eps"), sem("erstd"), sem("emean_rstd")
        xnr, prr, msr = sem("exn_ready"), sem("pre_ready"), sem("msg_ready")
        tpr, etr, emr, cpr, cbr = sem("ea_transposed"), sem("eaT_ready"), sem("emb_ready"), sem("comb_psum"), sem("comb_ready")
        CONST = 10
        LOADS = 7 * 16

        flat = agg.rearrange("a b -> (a b)").rearrange("(p c) -> p c", p=P)
        cols = flat.shape[1]
        pieces = [(c, min(c + 2048, cols)) for c in range(0, cols, 2048)]
        TURNS = PAIRS // PU

        def pair_of(it, u):
            it, u = it + u // PU, u % PU
            return it * PU + u, u, it

        def inputs(g, u):
            return PU if isinstance(g, int) and g == PAIRS - 1 else u

        def loaded(g, u, it):
            return (ld[PU], LOADS) if inputs(g, u) == PU else (ld[u], (it + 1) * LOADS)

        def turns(eng, turn):
            turn(0)
            with eng.Fori(1, TURNS - 2) as it:
                turn(it)
            turn(TURNS - 2)
            turn(TURNS - 1)

        def exists(it, u):
            return not isinstance(it, int) or it * PU + u < PAIRS

        def from_(g, least):
            return not isinstance(g, int) or g >= least

        def all_zero(eng):
            for i in range(ZQ):
                eng.wait_ge(zeroed[i], 16 * len(pieces[i::ZQ]))

        def load(eng, it, u):
            g, u, it = pair_of(it, u)
            i, e0 = inputs(g, u), g * 2 * P
            if i == u and from_(g, PU):
                wait_apart(eng, (const, CONST), (ix, 2 * (g - PU + 1)), (gat[u], it * 32), (tpr, g - PU + 1))
            rows = (P, P) if i == u else (P, ER)
            for j, p in enumerate(rows):
                span = bass.ds(e0 + j * P, p)
                eng.dma_start(scol[i][0:p, j:j + 1], src[span].rearrange("(p a) -> p a", a=1)).then_inc(ld[i], 16)
                eng.dma_start(dcol[i][0:p, j:j + 1], dst[span].rearrange("(p a) -> p a", a=1)).then_inc(ld[i], 16)
                eng.dma_start(ea[i][0:p, j, :], edge_attr[span, :]).then_inc(ld[i], 16)
            eng.dma_start(drow[i][:, 0:sum(rows)], dst[bass.ds(e0, sum(rows))].rearrange("(a p) -> a p", a=1)
                          .to_broadcast([P, sum(rows)])).then_inc(ld[i], 16)

        with nc.Block() as block:
            @block.sync
            def _(sp):
                sp.dma_start(web[0:ED, :], W_e).then_inc(wld, 16)
                sp.dma_start(web[ED:ED + 1, :], b_e.rearrange("(a n) -> a n", a=1)).then_inc(wld, 16)
                sp.wait_ge(const, 1)
                for i, (c0, c1) in enumerate(pieces):
                    if i >= ZQ:
                        sp.wait_ge(zeroed[i % ZQ], 16 * (i // ZQ))
                    sp.dma_start(flat[:, c0:c1], zeros[:, 0:c1 - c0]).then_inc(zeroed[i % ZQ], 16)
                sp.wait_ge(const, CONST)
                load(sp, TURNS - 1, PU - 1)

                def turn(it):
                    for u in range(PU):
                        if exists(it, u + PU + 1):
                            load(sp, it, u + PU)
                    if isinstance(it, int) and it == 0:
                        sp.dma_start(w1["whole"][:, :, :], W1.rearrange("(k p) n -> p k n", p=P)).then_inc(w1ld, 16)
                        with nc.allow_non_contiguous_dma(reason="vectors by channel"):
                            for name in ("b1", "g1", "beta1", "b2", "g2", "beta2"):
                                sp.dma_start(vec[name][:, :], vectors[name].rearrange("(m p) -> p m", p=P)).then_inc(vld, 16)
                        sp.dma_start(vec["eps"][:, :], vectors["eps"].rearrange("(a n) -> a n", a=1).to_broadcast([P, 1]))\
                            .then_inc(vld, 16)

                turns(sp, turn)
                sp.wait_ge(vld, 16 * len(vec))
                sp.wait_ge(sca, 32 * PAIRS)
                all_zero(sp)

            @block.scalar
            def _(act):
                def attributes(it, u):
                    g, u, it = pair_of(it, u)
                    act.wait_ge(tpr, g + 1)
                    if from_(g, PU):
                        act.wait_ge(emr, 2 * (g - PU + 1))
                    nc.scalar.activation(eaT[0:ED, u, :], tp[u % 2][0:ED, 0:2 * P], ACT.Copy).then_inc(etr, 1)

                def normalize(it, u):
                    g, u, it = pair_of(it, u)
                    act.wait_ge(nbr, g + 1)
                    if from_(g, PU):
                        act.wait_ge(prr, 2 * (g - PU + 1))
                    for j in range(2):
                        nc.scalar.activation(xn[u][:, j, :], xg[u][:, j, :], ACT.Identity, bias=nb[u][:, j:j + 1],
                                             scale=rs[u][:, j:j + 1]).then_inc(xnr, 1)

                def turn(it):
                    for u in range(PU):
                        g, _, _ = pair_of(it, u)
                        if exists(it, u + 1):
                            attributes(it, u + 1)
                        for j in range(2):
                            act.wait_ge(prr, 2 * g + j + 1)
                            if from_(g, PU) and j == 0:
                                act.wait_ge(cpr, 2 * (g - PU + 1))
                            nc.scalar.activation(msg[u][:, j, :], pre[u][:, j, :], ACT.Relu).then_inc(msr, 1)
                        if exists(it, u + 1):
                            normalize(it, u + 1)
                        for j in range(2):
                            act.wait_ge(cpr, 2 * g + j + 1)
                            if from_(g, PU) and j == 0:
                                act.wait_ge(sca, (g - PU + 1) * 32)
                            nc.scalar.activation(comb[u][:, j, :], cps[j][:, :], ACT.Copy).then_inc(cbr, 1)

                for u in range(PU):
                    load(act, 0, u)
                act.wait_ge(const, CONST)
                attributes(0, 0)
                normalize(0, 0)
                turns(act, turn)

            @block.gpsimd
            def _(pool):
                nc.gpsimd.memset(zeros[:, :], 0.0).then_inc(const, 1)
                nc.gpsimd.memset(before[:, :, :], 1.0).then_inc(const, 1)
                pool.wait_ge(const, 2)
                nc.gpsimd.affine_select(out=before[:, :, :], in_=before[:, :, :], compare_op=ALU.is_gt, fill=0.0,
                                        base=0, pattern=[[P, 2], [-1, 2 * P]], channel_multiplier=1).then_inc(const, 1)
                nc.gpsimd.iota(trash[:, :], pattern=[[P, 2]], base=N, channel_multiplier=1,
                               allow_small_or_imprecise_dtypes=True).then_inc(const, 1)
                nc.gpsimd.iota(dcol[PU][:, :], pattern=[[P, 2]], base=N, channel_multiplier=1).then_inc(const, 1)
                nc.gpsimd.iota(drow[PU][:, :], pattern=[[1, 2 * P]], base=N, channel_multiplier=0).then_inc(const, 1)
                nc.gpsimd.memset(scol[PU][:, :], 0).then_inc(const, 1)
                nc.gpsimd.memset(ea[PU][:, :, :], 0.0).then_inc(const, 1)
                pool.wait_ge(const, 8)
                nc.gpsimd.memset(mhalf[:, :], -0.5).then_inc(const, 1)
                pool.wait_ge(const, 9)
                nc.gpsimd.memset(eaT[ED:ED + 1, :, :], 1.0).then_inc(const, 1)
                pool.wait_ge(const, CONST)

                def gather(it, u):
                    g, u, it = pair_of(it, u)
                    free = [(xnr, 2 * (g - PU + 1))] if from_(g, PU) else []
                    wait_apart(pool, (const, CONST), loaded(g, u, it), *free)
                    for j in range(2):
                        nc.gpsimd.indirect_dma_start(
                            out=xg[u][:, j, :], out_offset=None, in_=x, in_offset=bass.IndirectOffsetOnAxis(
                                ap=scol[inputs(g, u)][:, j:j + 1], axis=0)).then_inc(gat[u], 16)

                def root(it, u):
                    g, u, it = pair_of(it, u)
                    pool.wait_ge(vpe, g + 1)
                    nc.gpsimd.tensor_tensor(rs[u][:, :], ve[u][:, :], mhalf[:, :], ALU.pow).then_inc(rst, 1)

                def scatter(it, u):
                    g, u, it = pair_of(it, u)
                    earlier = [(sca, g * 32)] if from_(g, 1) else []
                    wait_apart(pool, (const, CONST), (cbr, 2 * (g + 1)), *earlier)
                    for j in range(2):
                        nc.gpsimd.indirect_dma_start(
                            out=agg, out_offset=bass.IndirectOffsetOnAxis(ap=idx[u][:, j:j + 1], axis=0),
                            in_=comb[u][:, j, :], in_offset=None, compute_op=ALU.add).then_inc(sca, 16)

                for u in range(PU):
                    gather(0, u)
                    if 1 <= u <= ROOTS:
                        root(0, u - 1)
                all_zero(pool)

                def turn(it):
                    for u in range(PU):
                        scatter(it, u)
                        if exists(it, u + PU):
                            gather(it, u + PU)
                        if exists(it, u + ROOTS):
                            root(it, u + ROOTS)

                turns(pool, turn)

            @block.vector
            def _(dve):
                dve.wait_ge(const, CONST)

                def front(it, u):
                    g, u, it = pair_of(it, u)
                    i = inputs(g, u)
                    dve.wait_ge(*loaded(g, u, it))
                    if from_(g, PU):
                        dve.wait_ge(sca, (g - PU + 1) * 32)
                        dve.wait_ge(cpr, 2 * (g - PU + 1))
                    nc.vector.tensor_copy(dcolf[u][:, :], dcol[i][:, :]).then_inc(dcf, 1)
                    dve.wait_ge(dcf, g + 1)
                    for j in range(2):
                        nc.vector.tensor_scalar(sel[u][:, j, :], drow[i][:, :], dcolf[u][:, j:j + 1], None,
                                                ALU.is_equal).then_inc(sl, 1)
                    nc.vector.tensor_tensor(away[u][:, :], trash[:, :], dcolf[u][:, :], ALU.subtract).then_inc(aw, 1)
                    for j in range(2):
                        wait_apart(dve, (const, CONST), (sl, 2 * g + j + 1))
                        nc.vector.tensor_tensor_reduce(out=scr[:, j, :], in0=sel[u][:, j, :], in1=before[:, j, :],
                                                       scale=1.0, scalar=0.0, op0=ALU.mult, op1=ALU.max,
                                                       accum_out=cnt[u][:, j:j + 1]).then_inc(ct, 1)
                    dve.wait_ge(gat[u], (it + 1) * 32)
                    for j in range(2):
                        nc.vector.bn_stats(st[u][:, j, :], xg[u][:, j, :]).then_inc(bst, 1)
                    dve.wait_ge(aw, g + 1)
                    for j in range(2):
                        dve.wait_ge(ct, 2 * g + j + 1)
                        nc.vector.scalar_tensor_tensor(out=idx[u][:, j:j + 1], in0=away[u][:, j:j + 1],
                                                       scalar=cnt[u][:, j:j + 1], in1=dcolf[u][:, j:j + 1],
                                                       op0=ALU.mult, op1=ALU.add).then_inc(ix, 1)
                    for j in range(2):
                        wait_apart(dve, (const, CONST), (bst, 2 * g + j + 1))
                        nc.vector.bn_aggr(mv[u][:, j, :], st[u][:, j, :]).then_inc(bag, 1)
                    dve.wait_ge(bag, 2 * (g + 1))
                    nc.vector.tensor_scalar_add(ve[u][:, :], mv[u][:, :, 1], EPS).then_inc(vpe, 1)

                def shift(it, u):
                    g, u, it = pair_of(it, u)
                    dve.wait_ge(rst, g + 1)
                    nc.vector.scalar_tensor_tensor(out=nb[u][:, :], in0=mv[u][:, :, 0], scalar=-1.0, in1=rs[u][:, :],
                                                   op0=ALU.mult, op1=ALU.mult).then_inc(nbr, 1)

                def add(it, u):
                    g, u, it = pair_of(it, u)
                    for j in range(2):
                        dve.wait_ge(xnr, 2 * g + j + 1)
                        dve.wait_ge(emr, 2 * g + j + 1)
                        if from_(g, PU) and j == 0:
                            dve.wait_ge(msr, 2 * (g - PU + 1))
                        nc.vector.tensor_tensor(pre[u][:, j, :], xn[u][:, j, :], emb[2 * (u % 2) + j][:, :],
                                                ALU.add).then_inc(prr, 1)

                def turn(it):
                    for u in range(PU):
                        if exists(it, u + 1):
                            shift(it, u + 1)
                        add(it, u)
                        if exists(it, u + 2):
                            front(it, u + 2)
                    if isinstance(it, int) and it == TURNS - 2:
                        dve.wait_ge(w1ld, 16)
                        for k in range(KH):
                            split_weight(nc.vector, w1["whole"], w1["hi"], w1["lo"], w1h, w1l, k)

                front(0, 0)
                front(0, 1)
                shift(0, 0)
                turns(dve, turn)
                dve.wait_ge(w1l, KH)

            @block.tensor
            def _(pe):
                def embed(it, u):
                    g, u, it = pair_of(it, u)
                    free = [(etr, g - 1)] if from_(g, 2) else []
                    wait_apart(pe, (const, CONST), loaded(g, u, it), *free)
                    for j in range(2):
                        last = nc.tensor.transpose(tp[u % 2][0:ED, j * P:(j + 1) * P], ea[inputs(g, u)][:, j, :],
                                                   ident[:, :])
                    last.then_inc(tpr, 1)
                    pe.wait_ge(etr, g + 1)
                    if from_(g, 2):
                        pe.wait_ge(prr, 2 * (g - 1))
                    for j in range(2):
                        nc.tensor.matmul(emb[2 * (u % 2) + j][:, :], eaT[:, u, j * P:(j + 1) * P], web[:, :],
                                         start=True, stop=True).then_inc(emr, 1)

                def combine(it, u):
                    g, u, it = pair_of(it, u)
                    pe.wait_ge(msr, 2 * (g + 1))
                    for j in range(2):
                        if from_(g, 1):
                            pe.wait_ge(cbr, 2 * (g - 1) + j + 1)
                        for i in range(2):
                            last = nc.tensor.matmul(cps[j][:, :], sel[u][:, i, j * P:(j + 1) * P], msg[u][:, i, :],
                                                    start=(i == 0), stop=(i == 1))
                        last.then_inc(cpr, 1)

                def turn(it):
                    for u in range(PU):
                        if exists(it, u + 1):
                            embed(it, u + 1)
                        combine(it, u)

                pe.wait_ge(wld, 32)
                pe.wait_ge(const, CONST)
                embed(0, 0)
                turns(pe, turn)


def split_weight(dve, whole, hi, lo, hi_done, lo_done, k):
    nc_v = dve
    nc_v.tensor_copy(hi[:, k, :], whole[:, k, :]).then_inc(hi_done, 1)
    dve.wait_ge(hi_done, k + 1)
    nc_v.tensor_tensor(lo[:, k, :], whole[:, k, :], hi[:, k, :].bitcast(F32), ALU.subtract).then_inc(lo_done, 1)


def product(nc, out, w_hi, w_lo, a_hi, a_lo, chunks, m, ready=None):
    cols = slice(m * P, (m + 1) * P)
    for k in range(chunks):
        if ready:
            ready(k)
        nc.tensor.matmul(out, w_hi[:, k, cols], a_hi[:, k, :], start=(k == 0), stop=False)
        nc.tensor.matmul(out, w_hi[:, k, cols], a_lo[:, k, :], start=False, stop=False)
        last = nc.tensor.matmul(out, w_lo[:, k, cols], a_hi[:, k, :], start=False, stop=(k == chunks - 1))
    return last


def gnn_up(nc, sem, psum, ident, mhalf, x, agg, w1, vec, h1T, stats1, W2, w2):
    with ExitStack() as ctx:
        def sb(name, shape, dt=F32):
            return ctx.enter_context(nc.sbuf_tensor(name, shape, dt))

        whi, wlo = w1["hi"], w1["lo"]
        b1c, epsc, ope = vec["b1"], vec["eps"], sb("one_plus_eps", [P, 1])
        xt = [sb(f"xt{i}", [P, SUB, H]) for i in range(2)]
        at = [sb(f"at{i}", [P, SUB, H]) for i in range(2)]
        ht = sb("ht", [P, SUB, H])
        st = sb("st", [P, SUB, 6])
        mv = sb("mv", [P, SUB, 2])
        ve, rs, rse = sb("ve", [P, SUB]), sb("rs", [P, SUB]), sb("rse", [P, SUB])
        hhi = [sb(f"hhi{i}", [P, KH, CW], F32R) for i in range(2)]
        hlo = [sb(f"hlo{i}", [P, KH, CW], F32R) for i in range(2)]
        h1o = [sb(f"h1o{i}", [P, KF, CW]) for i in range(2)]
        tb, mb = psum[0:KH], psum[4:8]

        w2ld, w2h, w2l = sem("w2_loaded"), sem("w2_hi_done"), sem("w2_lo_done")
        ldx = [sem(f"x_chunk_loaded{i}") for i in range(2)]
        lda = [sem(f"agg_chunk_loaded{i}") for i in range(2)]
        stl = sem("h1_last_stored")
        sto = [sem(f"h1_stored{i}") for i in range(2)]
        bst, bag, vpe, rst, rsd = sem("xstats"), sem("xmeanvar"), sem("xvar_eps"), sem("xrstd"), sem("xrstd_eps")
        opr = sem("ope_ready")
        nrm, hrd = sem("x_normalized"), sem("h_ready")
        tpr, hir, lor = sem("h_transposed"), sem("h_hi_ready"), sem("h_lo_ready")
        mmr, evr, str_ = sem("h1_psum"), sem("h1_evicted"), sem("h1_stats")

        def span(c):
            return bass.ds(c * CW, CW)

        def chunks(eng, body):
            body(1, 1)
            body(2, 0)
            with eng.Fori(1, (NCH - 2) // 2) as it:
                body(it * 2 + 1, 1)
                body(it * 2 + 2, 0)
            body(NCH - 1, 1)

        def static(c, least):
            return isinstance(c, int) and c < least

        with nc.Block() as block:
            @block.sync
            def _(sp):

                def load(c, b):
                    if not static(c, 2):
                        sp.wait_ge(hrd, (c - 1) * SUB)
                    for table, to, done in ((x, xt, ldx), (agg, at, lda)):
                        rows = table[span(c), :].rearrange("(j p) h -> p j h", p=RT)
                        for p0, p1 in ((0, RT // 16 * 16), (RT // 16 * 16, RT)):
                            sp.dma_start(to[b][p0:p1, :, :], rows[p0:p1]).then_inc(done[b], 16)

                def store(c, b):
                    sp.wait_ge(evr, (c + 1) * KF)
                    sp.dma_start(h1T[:, :, span(c)].rearrange("m p n -> p m n"), h1o[b][:, :, :]).then_inc(sto[b], 16)

                load(0, 0)
                load(1, 1)
                sp.dma_start(w2["whole"][:, :, :], W2.rearrange("(k p) n -> p k n", p=P)).then_inc(w2ld, 16)
                load(2, 0)
                store(0, 0)
                with sp.Fori(0, (NCH - 4) // 2) as it:
                    load(it * 2 + 3, 1)
                    store(it * 2 + 1, 1)
                    load(it * 2 + 4, 0)
                    store(it * 2 + 2, 0)
                load(NCH - 1, 1)
                store(NCH - 3, 1)
                store(NCH - 2, 0)
                for m in range(0, KF, 2):
                    sp.wait_ge(evr, (NCH - 1) * KF + m + 2)
                    sp.dma_start(h1T[m:m + 2, :, span(NCH - 1)].rearrange("m p n -> p m n"), h1o[1][:, m:m + 2, :])\
                        .then_inc(stl, 16)
                sp.wait_ge(sto[0], 16 * (NCH // 2))
                sp.wait_ge(sto[1], 16 * (NCH // 2 - 1))
                sp.wait_ge(stl, 16 * (KF // 2))

            @block.gpsimd
            def _(pool):
                def root(c, b):
                    pool.wait_ge(vpe, c + 1)
                    nc.gpsimd.tensor_tensor(rs[0:RT, :], ve[0:RT, :], mhalf[0:RT, 0:SUB], ALU.pow).then_inc(rst, 1)

                root(0, 0)

                def body(c, b):
                    root(c, b)
                    if isinstance(c, int) and c <= 2:
                        half = range((c - 1) * KF // 2, c * KF // 2)
                        pool.wait_ge(w2ld, 16)
                        for k in half:
                            nc.gpsimd.tensor_copy(w2["hi"][:, k, :], w2["whole"][:, k, :]).then_inc(w2h, 1)
                        for k in half:
                            pool.wait_ge(w2h, k + 1)
                            nc.gpsimd.tensor_tensor(w2["lo"][:, k, :], w2["whole"][:, k, :],
                                                    w2["hi"][:, k, :].bitcast(F32), ALU.subtract).then_inc(w2l, 1)

                chunks(pool, body)
                pool.wait_ge(w2l, KF)

            @block.vector
            def _(dve):
                nc.vector.tensor_scalar_add(ope[:, :], epsc[:, :], 1.0).then_inc(opr, 1)
                dve.wait_ge(opr, 1)

                def prepare(c, b):
                    dve.wait_ge(ldx[b], (c - b) * 16 + 32)
                    for j in range(SUB):
                        nc.vector.bn_stats(st[0:RT, j, :], xt[b][0:RT, j, :]).then_inc(bst, 1)
                    for j in range(SUB):
                        wait_apart(dve, (opr, 1), (bst, c * SUB + j + 1))
                        nc.vector.bn_aggr(mv[0:RT, j, :], st[0:RT, j, :]).then_inc(bag, 1)
                    dve.wait_ge(bag, c * SUB + SUB)
                    nc.vector.tensor_scalar_add(ve[0:RT, :], mv[0:RT, :, 1], EPS).then_inc(vpe, 1)
                    dve.wait_ge(rst, c + 1)
                    nc.vector.tensor_scalar(rse[0:RT, :], rs[0:RT, :], ope[0:RT, 0:1], None, ALU.mult).then_inc(rsd, 1)
                    dve.wait_ge(rsd, c + 1)
                    if not static(c, 1):
                        dve.wait_ge(tpr, c * KH)
                    for j in range(SUB):
                        nc.vector.tensor_scalar(ht[0:RT, j, :], xt[b][0:RT, j, :], mv[0:RT, j, 0:1], rse[0:RT, j:j + 1],
                                                ALU.subtract, ALU.mult).then_inc(nrm, 1)
                    dve.wait_ge(lda[b], (c - b) * 16 + 32)
                    for j in range(SUB):
                        dve.wait_ge(nrm, c * SUB + j + 1)
                        nc.vector.tensor_tensor(ht[0:RT, j, :], ht[0:RT, j, :], at[b][0:RT, j, :], ALU.add).then_inc(hrd, 1)

                def low(c, b):
                    if not static(c, 2):
                        dve.wait_ge(mmr, (c - 1) * KF)
                    for k in range(KH):
                        dve.wait_ge(hir, c * KH + k + 1)
                        nc.vector.tensor_tensor(hlo[b][:, k, :], tb[k][:, 0:CW], hhi[b][:, k, :].bitcast(F32),
                                                ALU.subtract).then_inc(lor, 1)

                def stats(c, b, m0, m1):
                    for m in range(m0, m1):
                        dve.wait_ge(evr, c * KF + m + 1)
                        nc.vector.bn_stats(stats1[:, m, bass.ds(c * 6, 6)], h1o[b][:, m, :]).then_inc(str_, 1)

                prepare(0, 0)
                low(0, 0)

                def body(c, b):
                    prepare(c, b)
                    stats(c - 1, 1 - b, 0, 4)
                    low(c, b)
                    stats(c - 1, 1 - b, 4, KF)

                chunks(dve, body)
                stats(NCH - 1, 1, 0, KF)
                dve.wait_ge(str_, NCH * KF)

            @block.scalar
            def _(act):
                def high(c, b):
                    if not static(c, 2):
                        act.wait_ge(mmr, (c - 1) * KF)
                    for k in range(KH):
                        act.wait_ge(tpr, c * KH + k + 1)
                        nc.scalar.activation(hhi[b][:, k, :], tb[k][:, 0:CW], ACT.Copy).then_inc(hir, 1)

                def evict(c, b, m0, m1):
                    if not static(c, 2) and m0 == 0:
                        if b == 0:
                            act.wait_ge(sto[0], (c // 2) * 16 if isinstance(c, int) else c * 8)
                        else:
                            act.wait_ge(sto[1], (c - 1) * 8)
                        act.wait_ge(str_, (c - 1) * KF)
                    for m in range(m0, m1):
                        act.wait_ge(mmr, c * KF + m + 1)
                        nc.scalar.activation(h1o[b][:, m, :], mb[m % 4][:, 0:CW], ACT.Identity,
                                             bias=b1c[:, m:m + 1]).then_inc(evr, 1)

                high(0, 0)

                def body(c, b):
                    evict(c - 1, 1 - b, 0, 4)
                    high(c, b)
                    evict(c - 1, 1 - b, 4, KF)

                chunks(act, body)
                evict(NCH - 1, 1, 0, KF)

            @block.tensor
            def _(pe):
                def turn(c, b):
                    if static(c, 1):
                        for j in range(SUB):
                            pe.wait_ge(hrd, j + 1)
                            for k in range(KH):
                                last = nc.tensor.transpose(tb[k][:, j * RT:(j + 1) * RT],
                                                           ht[0:RT, j, k * P:(k + 1) * P], ident[0:RT, 0:RT])
                                if j == SUB - 1:
                                    last.then_inc(tpr, 1)
                        return
                    pe.wait_ge(hrd, (c + 1) * SUB)
                    pe.wait_ge(lor, c * KH)
                    for k in range(KH):
                        for j in range(SUB):
                            last = nc.tensor.transpose(tb[k][:, j * RT:(j + 1) * RT], ht[0:RT, j, k * P:(k + 1) * P],
                                                       ident[0:RT, 0:RT])
                        last.then_inc(tpr, 1)

                def multiply(c, b, m0, m1):
                    if m0 == 0:
                        pe.wait_ge(lor, (c + 1) * KH)
                    for m in range(m0, m1):
                        if not (static(c, 1) and m < 4):
                            pe.wait_ge(evr, c * KF + m - 3)
                        product(nc, mb[m % 4][:, 0:CW], whi, wlo, hhi[b], hlo[b], KH, m).then_inc(mmr, 1)

                turn(0, 0)

                def body(c, b):
                    multiply(c - 1, 1 - b, 0, 4)
                    turn(c, b)
                    multiply(c - 1, 1 - b, 4, KF)

                chunks(pe, body)
                multiply(NCH - 1, 1, 0, KF)


def norm_constants(nc, dve, pool_root, gam, bet, stats, mv, ve, rs, sc, sh, sems, n, rows):
    agr, vpe, rst, scr, tmr, shr = sems
    for m in range(n):
        nc.vector.bn_aggr(mv[:, m, :], stats[:, m, :]).then_inc(agr, 1)
    dve.wait_ge(agr, n)
    nc.vector.tensor_scalar_add(ve[:, :], mv[:, :, 1], EPS).then_inc(vpe, 1)
    dve.wait_ge(rst, 1)
    nc.vector.tensor_tensor(sc[:, :], gam[:, :], rs[:, :], ALU.mult).then_inc(scr, 1)
    dve.wait_ge(scr, 1)
    nc.vector.tensor_tensor(rs[:, :], mv[:, :, 0], sc[:, :], ALU.mult).then_inc(tmr, 1)
    dve.wait_ge(tmr, 1)
    nc.vector.tensor_tensor(sh[:, :], bet[:, :], rs[:, :], ALU.subtract).then_inc(shr, 1)


def gnn_down(nc, sem, psum, mhalf, h1T, vec, w2, h2T, stats1, stats2):
    with ExitStack() as ctx:
        def sb(name, shape, dt=F32):
            return ctx.enter_context(nc.sbuf_tensor(name, shape, dt))

        whi, wlo = w2["hi"], w2["lo"]
        b2c, gc, bc = vec["b2"], vec["g1"], vec["beta1"]
        mv, ve, rs = sb("mv1", [P, KF, 2]), sb("ve1", [P, KF]), sb("rs1", [P, KF])
        sc, sh = sb("scale1", [P, KF]), sb("shift1", [P, KF])
        h1 = [sb(f"h1in{i}", [P, KF, CW]) for i in range(2)]
        aw = sb("a_whole", [P, KF, CW])
        ahi = [sb(f"ahi{i}", [P, KF, CW], F32R) for i in range(2)]
        alo = [sb(f"alo{i}", [P, KF, CW], F32R) for i in range(2)]
        h2o = [sb(f"h2o{i}", [P, KH, CW]) for i in range(2)]

        PIECES = 4
        ldp = [sem(f"h1_first_loaded{i}") for i in range(PIECES)]
        nrm = [sem(n) for n in ("h1_agg", "h1_var_eps", "h1_rstd", "scale1_ready", "mean_scaled1", "shift1_ready")]
        ldh = [sem(f"h1_loaded{i}") for i in range(2)]
        sto = [sem(f"h2_stored{i}") for i in range(2)]
        stl = sem("h2_last_stored")
        awr, hir, lor = sem("a_ready"), sem("a_hi_ready"), sem("a_lo_ready")
        mmr, evr, str_ = sem("h2_psum"), sem("h2_evicted"), sem("h2_stats")

        def span(c):
            return bass.ds(c * CW, CW)

        def static(c, least):
            return isinstance(c, int) and c < least

        def chunks(eng, body):
            body(0, 0)
            body(1, 1)
            with eng.Fori(1, NCH // 2) as it:
                body(it * 2, 0)
                body(it * 2 + 1, 1)

        def half(c, b, of):
            return (c - b) * (of // 2) + of

        with nc.Block() as block:
            @block.sync
            def _(sp):
                def load(c, b):
                    if not static(c, 2):
                        sp.wait_ge(hir, (c - 1) * KF)
                    sp.dma_start(h1[b][:, :, :], h1T[:, :, span(c)].rearrange("m p n -> p m n")).then_inc(ldh[b], 16)

                def store(c, b):
                    sp.wait_ge(evr, (c + 1) * KH)
                    sp.dma_start(h2T[:, :, span(c)].rearrange("m p n -> p m n"), h2o[b][:, :, :]).then_inc(sto[b], 16)

                for i in range(PIECES):
                    ks = slice(i * KF // PIECES, (i + 1) * KF // PIECES)
                    sp.dma_start(h1[0][:, ks, :], h1T[ks, :, span(0)].rearrange("m p n -> p m n")).then_inc(ldp[i], 16)
                load(1, 1)
                with sp.Fori(0, NCH // 2 - 1) as it:
                    load(it * 2 + 2, 0)
                    store(it * 2, 0)
                    load(it * 2 + 3, 1)
                    store(it * 2 + 1, 1)
                store(NCH - 2, 0)
                for m in range(KH):
                    sp.wait_ge(evr, (NCH - 1) * KH + m + 1)
                    sp.dma_start(h2T[m, :, span(NCH - 1)], h2o[1][:, m, :]).then_inc(stl, 16)
                sp.wait_ge(sto[0], 16 * (NCH // 2))
                sp.wait_ge(sto[1], 16 * (NCH // 2 - 1))
                sp.wait_ge(stl, 16 * KH)

            @block.gpsimd
            def _(pool):
                pool.wait_ge(nrm[1], 1)
                nc.gpsimd.tensor_tensor(rs[:, :], ve[:, :], mhalf[:, 0:KF], ALU.pow).then_inc(nrm[2], 1)

            @block.vector
            def _(dve):
                norm_constants(nc, dve, None, gc, bc, stats1, mv, ve, rs, sc, sh, nrm, KF, None)

                def low(c, b):
                    if not static(c, 2):
                        dve.wait_ge(mmr, (c - 1) * KH)
                    for k in range(KF):
                        dve.wait_ge(hir, c * KF + k + 1)
                        nc.vector.tensor_tensor(alo[b][:, k, :], aw[:, k, :], ahi[b][:, k, :].bitcast(F32),
                                                ALU.subtract).then_inc(lor, 1)

                def stats(c, b):
                    for m in range(KH):
                        dve.wait_ge(evr, c * KH + m + 1)
                        nc.vector.bn_stats(stats2[:, m, bass.ds(c * 6, 6)], h2o[b][:, m, :]).then_inc(str_, 1)

                low(0, 0)
                low(1, 1)
                stats(0, 0)
                with dve.Fori(1, NCH // 2) as it:
                    low(it * 2, 0)
                    stats(it * 2 - 1, 1)
                    low(it * 2 + 1, 1)
                    stats(it * 2, 0)
                stats(NCH - 1, 1)
                dve.wait_ge(str_, NCH * KH)

            @block.scalar
            def _(act):
                act.wait_ge(nrm[5], 1)

                def nonlinear(c, b):
                    if not static(c, 1):
                        act.wait_ge(ldh[b], half(c, b, 16) - (16 if b == 0 else 0))
                    if not static(c, 2):
                        act.wait_ge(mmr, (c - 1) * KH)
                    for k in range(KF):
                        if not static(c, 1):
                            act.wait_ge(lor, (c - 1) * KF + k + 1)
                        elif k % (KF // PIECES) == 0:
                            act.wait_ge(ldp[k * PIECES // KF], 16)
                        nc.scalar.activation(aw[:, k, :], h1[b][:, k, :], ACT.Silu, bias=sh[:, k:k + 1],
                                             scale=sc[:, k:k + 1]).then_inc(awr, 1)
                        act.wait_ge(awr, c * KF + k + 1)
                        nc.scalar.activation(ahi[b][:, k, :], aw[:, k, :], ACT.Copy).then_inc(hir, 1)

                def evict(c, b):
                    if not static(c, 2):
                        act.wait_ge(sto[b], half(c, b, 16) - 16)
                        act.wait_ge(str_, (c - 1) * KH)
                    for m in range(KH):
                        act.wait_ge(mmr, c * KH + m + 1)
                        nc.scalar.activation(h2o[b][:, m, :], psum[(4 * b + m)][:, 0:CW], ACT.Identity,
                                             bias=b2c[:, m:m + 1]).then_inc(evr, 1)

                nonlinear(0, 0)
                nonlinear(1, 1)
                evict(0, 0)
                with act.Fori(1, NCH // 2) as it:
                    nonlinear(it * 2, 0)
                    evict(it * 2 - 1, 1)
                    nonlinear(it * 2 + 1, 1)
                    evict(it * 2, 0)
                evict(NCH - 1, 1)

            @block.tensor
            def _(pe):
                def multiply(c, b):
                    if not static(c, 1):
                        pe.wait_ge(lor, (c + 1) * KF)
                    for m in range(KH):
                        if not static(c, 2):
                            pe.wait_ge(evr, (c - 2) * KH + m + 1)
                        part = (lambda k: pe.wait_ge(lor, k + 1)) if static(c, 1) and m == 0 else None
                        product(nc, psum[4 * b + m][:, 0:CW], whi, wlo, ahi[b], alo[b], KF, m, part).then_inc(mmr, 1)

                chunks(pe, multiply)


def mixture(nc, sem, psum, ident, mhalf, x, h2T, x1d, vec, controller, f1, f2, out, stats2):
    with ExitStack() as ctx:
        def sb(name, shape, dt=F32):
            return ctx.enter_context(nc.sbuf_tensor(name, shape, dt))

        f1s = sb("f1s", [P, KH, ES * FF])
        f2s = sb("f2s", [P, NE, H])
        cts = sb("controller_s", [P, KH, ES])
        yT = sb("yT", [P, KH, ES, TB * GB])
        ibd = sb("inner_bd", [P, NE, TB, NS, GB])
        pT = sb("perm_T", [ES, TB, P], F32R)
        pn = [sb(f"perm_new{i}", [ES, P], F32R) for i in range(2)]
        gc, bc = vec["g2"], vec["beta2"]
        mv2, ve2, rs2 = sb("mv2", [P, KH, 2]), sb("ve2", [P, KH]), sb("rs2", [P, KH])
        sc, sh = sb("scale2", [P, KH]), sb("shift2", [P, KH])
        h2 = [sb(f"h2in{i}", [P, KH, 2 * P]) for i in range(2)]
        gT = sb("gT", [P, KH, 2 * P])
        x1 = [sb(f"x1_{i}", [P, H]) for i in range(2)]
        st, mv = sb("st2", [P, 6]), sb("mvx", [P, 2])
        ve, rs = sb("vex", [P, 1]), sb("rsx", [P, 1])
        xn = sb("xn2", [P, H])
        xhi = [sb(f"xn2_hi{i}", [P, H], F32R) for i in range(2)]
        xlo = [sb(f"xn2_lo{i}", [P, H], F32R) for i in range(2)]
        xT = sb("xn2_T", [P, KH, P])
        lg, mx = sb("logits", [ES, P]), sb("logits_max", [ES, GB])
        tie = sb("tie", [ES, GT])
        pbd = sb("perm_bd", [P, ES, GB], F32R)
        rbd = [sb(f"back_bd{i}", [P, QB, P], F32R) for i in range(2)]
        ihi = [sb(f"inter_hi{i}", [P, H], F32R) for i in range(UB)]
        ilo = [sb(f"inter_lo{i}", [P, H], F32R) for i in range(UB)]
        x1b = [sb(f"x1_back{i}", [P, H]) for i in range(2)]
        rep = sb("rep", [ES, QB * P], F32R)
        repf = x1b[0][0:ES, :]
        pidx, pq = sb("pidx", [P, 1], I32), sb("pq", [P, 2], I32)
        pqf = sb("pqf", [P, 2])
        gid, tgid = sb("gid", [P, GB]), x1b[1][:, 0:P]
        mtg, mrt = sb("mask_token_group", [P, GB]), sb("mask_row_token", [P, P])

        bA, bB, bD, bF = psum[0], psum[1], psum[3:5], psum[7]
        bI = [psum[2], psum[5], psum[6]]
        bL, bP = bB[0:ES, 0:P], bB[:, 0:ES]

        wctl, wf1, wf2 = sem("controller_loaded"), sem("f1_loaded"), sem("f2_loaded")
        nrm = [sem(n) for n in ("h2_agg", "h2_var_eps", "h2_rstd", "scale2_ready", "mean_scaled2", "shift2_ready")]
        cst, cstv = sem("ffn_const"), sem("ffn_const_v")
        ldh = [sem(f"h2_loaded{i}") for i in range(2)]
        ldx = [sem(f"x_loaded{i}") for i in range(2)]
        x1s = [sem(f"x1_stored{i}") for i in range(2)]
        ldb = [sem(f"x1_back_loaded{i}") for i in range(2)]
        ots = [sem(f"out_stored{i}") for i in range(2)]
        gr, t1, x1r = sem("g_ready"), sem("g_transposed"), sem("x1_ready")
        bst, bag, vpe, rst = sem("x1_stats"), sem("x1_meanvar"), sem("x1_var_eps"), sem("x1_rstd")
        xnr, xhr, xlr, t2, xTr = sem("xn2_ready"), sem("xn2_hi_r"), sem("xn2_lo_r"), sem("xn2_transposed"), sem("xn2T_ready")
        pnr = sem("perm_new_ready")
        lgp, lgr, mxr, pTr = sem("logits_psum"), sem("logits_ready"), sem("max_ready"), sem("permT_ready")
        ptp, pbr, yp, yr = sem("perm_transposed"), sem("perm_bd_ready"), sem("y_psum"), sem("y_ready")
        inp, inv, ina = sem("inner_psum"), sem("inner_ready_v"), sem("inner_ready_a")
        rp, rr, ip, ihr, ilr = sem("r_psum"), sem("r_ready"), sem("inter_psum"), sem("inter_hi_r"), sem("inter_lo_r")
        fp, otr = sem("final_psum"), sem("out_ready")

        def static(c, least):
            return isinstance(c, int) and c < least

        def row(k, j):
            if isinstance(k, int) and k * TB + j >= (NB - 1) * TB:
                return N - BW + (k - (NB - 1)) * BW + j * P
            return k * BW + j * P

        def by2(t, par, of):
            return (t - par) * (of // 2) + of

        def blocks(eng, body):
            body(0, None)
            body(1, 0)
            with eng.Fori(2, NB - 2) as k:
                body(k, k - 1)
            body(NB - 2, NB - 3)
            body(NB - 1, NB - 2)
            body(None, NB - 1)

        STEPS = TB + 1
        UNITS = TB * QB

        def exists(k, j):
            return k is not None and not (isinstance(k, int) and k == NB - 1 and j >= TB)

        def schedule(front, back):
            if front is not None and static(front, 1):
                yield "turn_g", 0
                yield "turn_x", 0
            given = 0
            for m in range(STEPS):
                goal = min(QB * (m + 1) - 2, UNITS)
                units = list(range(given, goal)) if back is not None else []
                given = goal
                if m == 0:
                    units = [None, None, *units]
                slots = [[u] if u is not None else [] for u in units] + [[]] * (QB - len(units))
                new = m < TB and exists(front, m + 1)
                if back is not None and m >= 2:
                    yield "result", m - 2
                if m > 0 and m < TB and new or m == 0 and front is not None and static(front, 1):
                    yield "turn_g", m + 1
                if m == TB and exists(front, TB + 1):
                    yield "turn_g", TB + 1
                if front is not None and m < TB:
                    yield "select", m
                if front is not None and m >= 1:
                    yield "sum_a", m - 1
                if back is not None and m == 0:
                    yield "inner", 1
                for u in slots[0] + slots[1]:
                    yield "unit", u
                if new:
                    yield "turn_x", m + 1
                if back is not None and m < TB:
                    yield "rows", m
                if front is not None and m >= 1:
                    yield "sum_b", m - 1
                for u in slots[2]:
                    yield "unit", u
                if front is not None and m < TB:
                    yield "spread", m
                for u in slots[3]:
                    yield "unit", u
            if back is not None:
                yield "ends", UNITS
            if front is not None:
                yield "inner", 0

        def relu(op, h, s, *more):
            return op(ibd[32 * s:32 * s + 32, 8 * h:8 * h + 8, :, s, :],
                      bD[h][32 * s:32 * s + 32, :].rearrange("p (e j g) -> p e j g", e=8, g=GB), *more)

        def unit_of(kb, u):
            return kb * UNITS + u

        def freed(kb, u):
            if u >= UB:
                return unit_of(kb, u - UB) + 1
            if static(kb, 1):
                return 0
            return (kb - 1) * UNITS + max(v for v in range(UNITS) if v % UB == u % UB) + 1

        with nc.Block() as block:
            @block.sync
            def _(sp):
                def load_weights(i):
                    if i < KH:
                        sp.dma_start(f1s[:, i, :], f1[i * P:(i + 1) * P].rearrange("p e s f -> p (e s f)")).then_inc(wf1, 16)
                    elif i < KH + F2P:
                        es = slice((i - KH) * (NE // F2P), (i - KH + 1) * (NE // F2P))
                        sp.dma_start(f2s[:, es, :], f2[es].rearrange("e s f d -> (s f) e d")).then_inc(wf2, 16)

                def load_h(k, p):
                    pair = k * (TB // 2) + p
                    if not static(pair, 2):
                        sp.wait_ge(gr, (pair - 1) * KH)
                    sp.dma_start(h2[p % 2][:, :, :], h2T[:, :, bass.ds(row(k, 2 * p), 2 * P)].rearrange("m p n -> p m n"))\
                        .then_inc(ldh[p % 2], 16)

                def load_x(k, j):
                    t = k * TB + j
                    if not static(t, 2):
                        wait_apart(sp, (wctl, 16), (xnr, t - 1), (x1s[j % 2], by2(t, j % 2, 16) - 16))
                    sp.dma_start(x1[j % 2][:, :], x[bass.ds(row(k, j), P), :]).then_inc(ldx[j % 2], 16)

                def store_x1(k, j):
                    t = k * TB + j
                    sp.wait_ge(x1r, t + 1)
                    sp.dma_start(x1d[bass.ds(t * P, P), :], x1[j % 2][:, :]).then_inc(x1s[j % 2], 16)

                def load_back(kb, j):
                    t = kb * TB + j
                    sp.wait_ge(x1s[j % 2], by2(t, j % 2, 16))
                    if not static(t, 2):
                        sp.wait_ge(ots[j % 2], by2(t, j % 2, 16) - 16)
                    sp.dma_start(x1b[j % 2][:, :], x1d[bass.ds(t * P, P), :]).then_inc(ldb[j % 2], 16)

                def store_out(kb, j):
                    t = kb * TB + j
                    sp.wait_ge(otr, t + 1)
                    sp.dma_start(out[bass.ds(row(kb, j), P), :], x1b[j % 2][:, :]).then_inc(ots[j % 2], 16)

                def body(k, kb):
                    if static(k, 1):
                        load_h(k, 0)
                        load_x(k, 0)
                        load_x(k, 1)
                        load_h(k, 1)
                        sp.dma_start(cts[:, :, :], controller.rearrange("(k p) e s -> p k (e s)", p=P)).then_inc(wctl, 16)
                    if kb is not None and not static(kb, 1):
                        store_out(kb - 1, TB - 1)
                    if k is None:
                        for b in range(2):
                            sp.wait_ge(ots[b], 16 * (TB // 2) * (NB - 1))
                    for what, n in schedule(k, kb):
                        if what == "turn_g":
                            store_x1(k, n)
                            if static(k, 1) and n >= 1:
                                load_weights(n - 1)
                            if n >= 1 and exists(k, n + 1):
                                load_x(k, n + 1)
                            if n % 2 and exists(k, n + 3):
                                load_h(k, n // 2 + 2)
                        if what == "result":
                            store_out(kb, n)
                        if what == "rows":
                            load_back(kb, n)
                    if k is None:
                        store_out(kb, TB - 1)

                blocks(sp, body)
                for b in range(2):
                    sp.wait_ge(ots[b], 16 * (TB // 2) * NB)

            @block.gpsimd
            def _(pool):
                pool.wait_ge(nrm[1], 1)
                nc.gpsimd.tensor_tensor(rs2[:, :], ve2[:, :], mhalf[:, 0:KH], ALU.pow).then_inc(nrm[2], 1)
                nc.gpsimd.memset(ibd[:, :, :, :, :], 0.0).then_inc(cst, 1)
                nc.gpsimd.iota(pidx[:, :], pattern=[[0, 1]], base=0, channel_multiplier=1).then_inc(cst, 1)
                nc.gpsimd.iota(gid[:, :], pattern=[[1, GB]], base=0, channel_multiplier=0,
                               allow_small_or_imprecise_dtypes=True).then_inc(cst, 1)
                nc.gpsimd.iota(tgid[:, :], pattern=[[1, GB], [0, GT]], base=0, channel_multiplier=0,
                               allow_small_or_imprecise_dtypes=True).then_inc(cst, 1)
                pool.wait_ge(cst, 4)
                pool.wait_ge(cstv, 1)
                nc.gpsimd.affine_select(out=repf[:, :], in_=repf[:, :], compare_op=ALU.is_ge, fill=0.0, base=0,
                                        pattern=[[1, QB * P]], channel_multiplier=-GB).then_inc(cst, 1)
                pool.wait_ge(cst, 5)
                nc.gpsimd.affine_select(out=repf[:, :], in_=repf[:, :], compare_op=ALU.is_ge, fill=0.0, base=GB - 1,
                                        pattern=[[-1, QB * P]], channel_multiplier=GB).then_inc(cst, 1)
                def keep(k, j):
                    t = k * TB + j
                    free = [] if static(k, 1) else [(rp, t - TB + 1)]
                    wait_apart(pool, (cst, 6), (pnr, t + 1), *free)
                    nc.gpsimd.tensor_copy(pT[:, j, :], pn[j % 2][:, :].bitcast(F32)).then_inc(pTr, 1)

                def body(k, kb):
                    for what, n in schedule(k, kb):
                        if what == "turn_g":
                            t = k * TB + n
                            pool.wait_ge(vpe, t + 1)
                            nc.gpsimd.tensor_tensor(rs[:, :], ve[:, :], mhalf[:, 0:1], ALU.pow).then_inc(rst, 1)
                            free = [] if static(t, 2) else [(yp, (t - 1) * KH)]
                            wait_apart(pool, (cst, 6), (xnr, t + 1), *free)
                            nc.gpsimd.tensor_copy(xhi[n % 2][:, :], xn[:, :]).then_inc(xhr, 1)
                            pool.wait_ge(xhr, t + 1)
                            nc.gpsimd.tensor_tensor(xlo[n % 2][:, :], xn[:, :], xhi[n % 2][:, :].bitcast(F32),
                                                    ALU.subtract).then_inc(xlr, 1)

                        if what == "spread":
                            keep(k, n)

                blocks(pool, body)

            @block.vector
            def _(dve):
                norm_constants(nc, dve, None, gc, bc, stats2, mv2, ve2, rs2, sc, sh, nrm, KH, None)
                nc.vector.memset(repf[:, :], 1.0).then_inc(cstv, 1)
                for t in range(GT):
                    nc.vector.memset(tie[:, t:t + 1], float(np.linspace(0.0, 1e-6, GT, dtype=np.float32)[t])).then_inc(cstv, 1)
                dve.wait_ge(cst, 6)
                nc.vector.tensor_copy(rep[:, :], repf[:, :]).then_inc(cstv, 1)
                nc.vector.tensor_scalar(pq[:, 0:1], pidx[:, :], 4, None, ALU.logical_shift_right).then_inc(cstv, 1)
                nc.vector.tensor_scalar(pq[:, 1:2], pidx[:, :], GB - 1, None, ALU.bitwise_and).then_inc(cstv, 1)
                dve.wait_ge(cstv, GT + 4)
                nc.vector.tensor_copy(pqf[:, :], pq[:, :]).then_inc(cstv, 1)
                dve.wait_ge(cstv, GT + 5)
                nc.vector.tensor_scalar(mtg[:, :], gid[:, :], pqf[:, 0:1], None, ALU.is_equal).then_inc(cstv, 1)
                nc.vector.tensor_scalar(mrt[:, :], tgid[:, :], pqf[:, 1:2], None, ALU.is_equal).then_inc(cstv, 1)
                dve.wait_ge(cstv, GT + 7)

                def new_tile(k, j):
                    t = k * TB + j
                    dve.wait_ge(t1, t + 1)
                    dve.wait_ge(ldx[j % 2], by2(t, j % 2, 16))
                    nc.vector.tensor_tensor(x1[j % 2][:, :], x1[j % 2][:, :], bA[:, :], ALU.add).then_inc(x1r, 1)
                    dve.wait_ge(x1r, t + 1)
                    nc.vector.bn_stats(st[:, :], x1[j % 2][:, :]).then_inc(bst, 1)
                    wait_apart(dve, (cstv, GT + 7), (bst, t + 1))
                    nc.vector.bn_aggr(mv[:, :], st[:, :]).then_inc(bag, 1)
                    dve.wait_ge(bag, t + 1)
                    nc.vector.tensor_scalar_add(ve[:, :], mv[:, 1:2], EPS).then_inc(vpe, 1)

                def normalize(k, j):
                    t = k * TB + j
                    dve.wait_ge(rst, t + 1)
                    if not static(t, 1):
                        dve.wait_ge(t2, t)
                        dve.wait_ge(xlr, t)
                    nc.vector.tensor_scalar(xn[:, :], x1[j % 2][:, :], mv[:, 0:1], rs[:, 0:1],
                                            ALU.subtract, ALU.mult).then_inc(xnr, 1)

                def select(k, j):
                    t = k * TB + j
                    dve.wait_ge(lgp, t + 1)
                    lg3 = lg[:, :].rearrange("p (g t) -> p g t", t=GT)
                    nc.vector.tensor_tensor(lg3, bL.rearrange("p (g t) -> p g t", t=GT),
                                            tie[:, :].unsqueeze(1).to_broadcast([ES, GB, GT]), ALU.add).then_inc(lgr, 1)
                    dve.wait_ge(lgr, t + 1)
                    nc.vector.tensor_reduce(mx[:, :], lg3, AX.X, ALU.max).then_inc(mxr, 1)
                    dve.wait_ge(mxr, t + 1)
                    if not static(t, 2):
                        dve.wait_ge(pTr, t - 1)
                        dve.wait_ge(ptp, t - 1)
                    nc.vector.tensor_tensor(pn[j % 2][:, :].rearrange("p (g t) -> p g t", t=GT), lg3,
                                            mx[:, :].unsqueeze(2).to_broadcast([ES, GB, GT]), ALU.is_equal).then_inc(pnr, 1)

                def spread(k, j):
                    t = k * TB + j
                    dve.wait_ge(ptp, t + 1)
                    if not static(t, 1):
                        dve.wait_ge(yp, t * KH)
                    nc.vector.tensor_tensor(pbd[:, :, :], bP.unsqueeze(2).to_broadcast([P, ES, GB]),
                                            mtg[:, :].unsqueeze(1).to_broadcast([P, ES, GB]), ALU.mult).then_inc(pbr, 1)

                def back_rows(kb, j):
                    t = kb * TB + j
                    dve.wait_ge(rp, t + 1)
                    if not static(t, 2):
                        dve.wait_ge(fp, (t - 1) * QB)
                    nc.vector.tensor_tensor(rbd[j % 2][:, :, :], bA[:, :].rearrange("p (b t) -> p b t", t=P),
                                            mrt[:, :].unsqueeze(1).to_broadcast([P, QB, P]), ALU.mult).then_inc(rr, 1)

                def inter_low(kb, u):
                    q = unit_of(kb, u)
                    dve.wait_ge(ihr, q + 1)
                    if not static(freed(kb, u), 1):
                        dve.wait_ge(fp, freed(kb, u))
                    nc.vector.tensor_tensor(ilo[u % UB][:, :], bI[u % UB][:, :], ihi[u % UB][:, :].bitcast(F32),
                                            ALU.subtract).then_inc(ilr, 1)

                def result(kb, j):
                    t = kb * TB + j
                    dve.wait_ge(fp, (t + 1) * QB)
                    dve.wait_ge(ldb[j % 2], by2(t, j % 2, 16))
                    nc.vector.tensor_tensor(x1b[j % 2][:, :], bF[:, :], x1b[j % 2][:, :], ALU.add).then_inc(otr, 1)

                def body(k, kb):
                    for what, n in schedule(k, kb):
                        if what == "turn_g":
                            new_tile(k, n)
                            if n in (0, TB + 1):
                                normalize(k, n)
                        if what == "select":
                            select(k, n)
                            if exists(k, n + 1) and (n > 0 or static(k, 1)):
                                normalize(k, n + 1)
                        if what == "spread":
                            spread(k, n)
                        if what == "unit":
                            inter_low(kb, n)
                        if what == "result":
                            result(kb, n)
                        if what == "rows":
                            back_rows(kb, n)
                        if what == "inner":
                            dve.wait_ge(inp, (k if n == 0 else kb) * 2 + n + 1)
                            for s in range(0, NS, 2):
                                relu(nc.vector.tensor_scalar_max, n, s, 0.0).then_inc(inv, 1)
                        if what == "ends":
                            result(kb, TB - 1)

                blocks(dve, body)

            @block.scalar
            def _(act):
                act.wait_ge(nrm[5], 1)

                def nonlinear(k, p, chunks):
                    pair = k * (TB // 2) + p
                    if chunks[0] == 0:
                        act.wait_ge(ldh[p % 2], by2(pair, p % 2, 16))
                        if not static(pair, 1):
                            act.wait_ge(t1, pair * 2)
                    for c in chunks:
                        nc.scalar.activation(gT[:, c, :], h2[p % 2][:, c, :], ACT.Silu, bias=sh[:, c:c + 1],
                                             scale=sc[:, c:c + 1]).then_inc(gr, 1)

                def to_yT(k, j, c):
                    t = k * TB + j
                    act.wait_ge(yp, t * KH + c + 1)
                    nc.scalar.activation(yT[:, c, :, j * GB:(j + 1) * GB],
                                         bD[c % 2][:, :].rearrange("p (e g) -> p e g", g=GB), ACT.Copy).then_inc(yr, 1)

                def body(k, kb):
                    if static(k, 1):
                        nonlinear(k, 0, range(KH))
                    chunk = KH
                    for what, n in schedule(k, kb):
                        if what == "turn_g" and n % 2 and exists(k, n + 1):
                            pair, chunk = n // 2 + 1, 0
                        elif chunk < KH and what in ("select", "sum_b", "unit") and kb is not None:
                            nonlinear(k, pair, [chunk])
                            chunk += 1
                        elif chunk < KH and what in ("select", "spread", "inner"):
                            nonlinear(k, pair, range(chunk, KH))
                            chunk = KH
                        if what == "sum_a":
                            if n == 0 and not static(k, 1):
                                act.wait_ge(inp, k * 2)
                            to_yT(k, n, 0)
                            to_yT(k, n, 1)
                        if what == "sum_b":
                            to_yT(k, n, 2)
                            to_yT(k, n, 3)
                        if what == "unit":
                            q = unit_of(kb, n)
                            act.wait_ge(ip, q + 1)
                            if not static(freed(kb, n), 1):
                                act.wait_ge(fp, freed(kb, n))
                            nc.scalar.activation(ihi[n % UB][:, :], bI[n % UB][:, :], ACT.Copy).then_inc(ihr, 1)
                        if what == "turn_x":
                            t = k * TB + n
                            act.wait_ge(t2, t + 1)
                            if not static(t, 1):
                                act.wait_ge(lgp, t)
                            nc.scalar.activation(xT[:, :, :], bB[:, :].rearrange("p (k n) -> p k n", n=P),
                                                 ACT.Copy).then_inc(xTr, 1)
                        if what == "inner":
                            act.wait_ge(inp, (k if n == 0 else kb) * 2 + n + 1)
                            for s in range(1, NS, 2):
                                relu(nc.scalar.activation, n, s, ACT.Relu).then_inc(ina, 1)

                blocks(act, body)

            @block.tensor
            def _(pe):
                def turn_g(k, kb, j, rowed):
                    t = k * TB + j
                    pe.wait_ge(gr, (k * (TB // 2) + j // 2 + 1) * KH)
                    if not static(t, 1):
                        pe.wait_ge(x1r, t)
                    if kb is not None and not (static(kb, 1) and rowed == 0):
                        pe.wait_ge(rr, kb * TB + rowed)
                    for c in range(KH):
                        last = nc.tensor.transpose(bA[:, c * P:(c + 1) * P],
                                                   gT[:, c, (j % 2) * P:(j % 2 + 1) * P], ident[:, :])
                    last.then_inc(t1, 1)

                def turn_x(k, j):
                    t = k * TB + j
                    pe.wait_ge(xnr, t + 1)
                    if not static(t, 1):
                        pe.wait_ge(lgr, t)
                    for c in range(KH):
                        last = nc.tensor.transpose(bB[:, c * P:(c + 1) * P], xn[:, c * P:(c + 1) * P], ident[:, :])
                    last.then_inc(t2, 1)

                def logits(k, j):
                    t = k * TB + j
                    pe.wait_ge(xTr, t + 1)
                    if static(t, 1):
                        pe.wait_ge(wctl, 16)
                        pe.wait_ge(cstv, GT + 7)
                    else:
                        pe.wait_ge(pbr, t)
                    for c in range(KH):
                        last = nc.tensor.matmul(bL, cts[:, c, :], xT[:, c, :], start=(c == 0), stop=(c == KH - 1))
                    last.then_inc(lgp, 1)

                def turn_p(k, j):
                    t = k * TB + j
                    turned = t + 2 if exists(k, j + 1) else t + 1
                    wait_apart(pe, (cstv, GT + 7), (pnr, t + 1), (xTr, turned))
                    nc.tensor.transpose(bP, pn[j % 2][:, :].bitcast(F32), ident[0:ES, 0:ES]).then_inc(ptp, 1)

                def sums(k, j, chunks):
                    t = k * TB + j
                    if chunks[0] == 0:
                        pe.wait_ge(pbr, t + 1)
                        pe.wait_ge(xlr, t + 1)
                        if j == 0 and not static(k, 1):
                            pe.wait_ge(inv, k * NS)
                            pe.wait_ge(ina, k * NS)
                    for c in chunks:
                        q = t * KH + c
                        if not static(q, 2):
                            pe.wait_ge(yr, q - 1)
                        o = bD[c % 2][:, :]
                        r = pbd[:, :, :].rearrange("p e g -> p (e g)")
                        nc.tensor.matmul(o, xhi[j % 2][:, c * P:(c + 1) * P], r, start=True, stop=False)
                        nc.tensor.matmul(o, xlo[j % 2][:, c * P:(c + 1) * P], r, start=False, stop=True).then_inc(yp, 1)

                def rows(k, kb, j, turned):
                    if k is not None:
                        pe.wait_ge(x1r, k * TB + turned)
                    if not static(kb * TB + j, 1):
                        pe.wait_ge(rr, kb * TB + j)
                    pe.wait_ge(pTr, kb * TB + j + 1)
                    for b in range(QB):
                        last = nc.tensor.matmul(bA[:, b * P:(b + 1) * P], rep[:, b * P:(b + 1) * P], pT[:, j, :],
                                                start=True, stop=True)
                    last.then_inc(rp, 1)

                def inter(kb, u):
                    j, b, q = u // QB, u % QB, unit_of(kb, u)
                    if static(kb, 1) and u == 0:
                        pe.wait_ge(wf2, 16 * F2P)
                    if j == 0 and b % 2 == 0:
                        pe.wait_ge(inv, kb * NS + b + 2)
                        pe.wait_ge(ina, kb * NS + b + 2)
                    if not static(freed(kb, u), 1):
                        pe.wait_ge(ilr, freed(kb, u))
                    for i in range(NS):
                        e = 4 * b + i
                        last = nc.tensor.matmul(bI[u % UB][32 * i:32 * i + 32, :],
                                                ibd[:, e, j, :, :].rearrange("p s g -> p (s g)"), f2s[:, e, :],
                                                start=True, stop=True)
                    last.then_inc(ip, 1)

                def final(kb, u):
                    j, b, q = u // QB, u % QB, unit_of(kb, u)
                    if b == 0:
                        pe.wait_ge(rr, kb * TB + j + 1)
                        if not static(kb * TB + j, 1):
                            pe.wait_ge(otr, kb * TB + j)
                    pe.wait_ge(ilr, q + 1)
                    nc.tensor.matmul(bF[:, :], rbd[j % 2][:, b, :], ihi[u % UB][:, :], start=(b == 0), stop=False)
                    nc.tensor.matmul(bF[:, :], rbd[j % 2][:, b, :], ilo[u % UB][:, :], start=False, stop=(b == QB - 1))\
                        .then_inc(fp, 1)

                def inner(k, h):
                    if static(k, 1):
                        pe.wait_ge(wf1, 16 * KH)
                    if h == 0:
                        pe.wait_ge(yr, (k + 1) * TB * KH)
                    for e in range(8 * h, 8 * h + 8):
                        for c in range(KH):
                            for s in range(NS):
                                es = e * NS + s
                                last = nc.tensor.matmul(
                                    bD[h][32 * s:32 * s + 32, (e % 8) * 64:(e % 8) * 64 + 64],
                                    f1s[:, c, es * FF:(es + 1) * FF], yT[:, c, es, :],
                                    start=(c == 0), stop=(c == KH - 1))
                    last.then_inc(inp, 1)

                def body(k, kb):
                    turned, rowed = (0 if static(k, 1) else 2), 0
                    for what, n in schedule(k, kb):
                        if what == "turn_g":
                            turn_g(k, kb, n, rowed)
                            turned += 1
                        if what == "select":
                            logits(k, n)
                        if what == "sum_a":
                            sums(k, n, (0, 1))
                        if what == "sum_b":
                            sums(k, n, (2, 3))
                        if what == "turn_x":
                            turn_x(k, n)
                        if what == "spread":
                            turn_p(k, n)
                        if what == "rows":
                            rows(k, kb, n, turned)
                            rowed += 1
                        if what == "unit":
                            inter(kb, n)
                            if n >= 2:
                                final(kb, n - 2)
                        if what == "ends":
                            final(kb, n - 2)
                            final(kb, n - 1)
                        if what == "inner":
                            inner(k if n == 0 else kb, n)

                blocks(pe, body)


def gnn_mixture(nc, x, src, dst, edge_attr, W_e, b_e, W1, b1, g1, beta1, W2, b2, g2, beta2, eps,
                controller, f1, f2, out):
    agg = nc.dram_tensor("aggregate", [N + TRASH, H], F32, kind="Internal").ap()
    h1T = nc.dram_tensor("h1T", [KF, P, N], F32, kind="Internal").ap()
    h2T = nc.dram_tensor("h2T", [KH, P, N], F32, kind="Internal").ap()
    x1d = nc.dram_tensor("x1", [NB * BW, H], F32, kind="Internal").ap()
    with ExitStack() as ctx:
        psum = [ctx.enter_context(nc.psum_tensor(f"bank{i}", [P, 512], F32)) for i in range(8)]
        ident = ctx.enter_context(nc.sbuf_tensor("ident", [P, P], F32))
        mhalf = ctx.enter_context(nc.sbuf_tensor("mhalf", [P, KF], F32))
        stats2 = ctx.enter_context(nc.sbuf_tensor("stats2", [P, KH, NCH * 6], F32))

        def sem(name):
            return ctx.enter_context(nc.semaphore(name))

        vectors = {"b1": b1, "g1": g1, "beta1": beta1, "b2": b2, "g2": g2, "beta2": beta2, "eps": eps}
        vec = {name: ctx.enter_context(nc.sbuf_tensor(f"{name}_by_channel", [P, max(v.shape[0] // P, 1)], F32))
               for name, v in vectors.items()}
        identity = sem("identity_ready")
        with nc.Block() as block:
            @block.gpsimd
            def _(pool):
                nc.gpsimd.memset(ident[:, :], 0.0).then_inc(identity, 1)
                pool.wait_ge(identity, 1)
                nc.gpsimd.affine_select(out=ident[:, :], in_=ident[:, :], compare_op=ALU.not_equal, fill=1.0,
                                        base=0, pattern=[[-1, P]], channel_multiplier=1).then_inc(identity, 1)
                pool.wait_ge(identity, 2)
                nc.gpsimd.memset(mhalf[:, :], -0.5).then_inc(identity, 1)
                pool.wait_ge(identity, 3)

            @block.tensor
            def _(pe):
                pe.wait_ge(identity, 3)

        with nc.sbuf_tensor("stats1", [P, KF, NCH * 6], F32) as stats1, ExitStack() as second:
            def split_buffers(ctx, name, chunks, width):
                return {part: ctx.enter_context(nc.sbuf_tensor(f"{name}_{part}", [P, chunks, width], F32R))
                        for part in ("hi", "lo")}

            w2 = split_buffers(second, "w2", KF, H)
            with ExitStack() as first:
                w1 = split_buffers(first, "w1", KH, F)
                whole = first.enter_context(nc.sbuf_tensor("weight_whole", [P, KH * F], F32))
                w1["whole"] = whole[:, :].rearrange("p (k n) -> p k n", k=KH)
                w2["whole"] = whole[:, :].rearrange("p (k n) -> p k n", k=KF)
                edge_aggregate(nc, sem, psum, ident, x, src, dst, edge_attr, W_e, b_e, agg, W1, w1, vectors, vec)
                gnn_up(nc, sem, psum, ident, mhalf, x, agg, w1, vec, h1T, stats1, W2, w2)
            gnn_down(nc, sem, psum, mhalf, h1T, vec, w2, h2T, stats1, stats2)
        mixture(nc, sem, psum, ident, mhalf, x, h2T, x1d, vec, controller, f1, f2, out, stats2)


_INS = ["x", "src", "dst", "edge_attr_64", "L0_gnn_W_e", "L0_gnn_b_e", "L0_gnn_W1", "L0_gnn_b1", "L0_gnn_g1",
        "L0_gnn_beta1", "L0_gnn_W2", "L0_gnn_b2", "L0_gnn_g2", "L0_gnn_beta2", "L0_gnn_eps", "L0_ffn_controller",
        "L0_ffn_f1", "L0_ffn_f2"]


def kernel(**inputs):
    import concourse.bacc as _bacc
    from concourse.bass_utils import run_bass_kernel_spmd as _run

    nc = _bacc.Bacc("TRN2", target_bir_lowering=False, num_devices=1)
    arrays, args = {}, []
    for name in _INS:
        a = np.ascontiguousarray(inputs[name])
        if a.ndim == 0:
            a = a.reshape(1)
        arrays[f"in_{name}"] = a
        args.append(nc.dram_tensor(f"in_{name}", a.shape, mybir.dt.from_np(a.dtype), kind="ExternalInput").ap())
    args.append(nc.dram_tensor("out_0", (N, H), F32, kind="ExternalOutput").ap())
    gnn_mixture(nc, *args)
    r = _run(nc, [arrays], core_ids=[0])
    return r.results[0]["out_0"]
```
